# Optimizing a Trainium2 kernel written in Bass

```python
import numpy as np
import jax
import jax.numpy as jnp

def _softmax(x, axis=-1):
    return jax.nn.softmax(x, axis=axis)

def _gelu(x):
    return jax.nn.gelu(x, approximate=True)

def _silu(x):
    return jax.nn.silu(x)

def _sigmoid(x):
    return jax.nn.sigmoid(x)

def _layernorm(x, axis=-1, eps=1e-05):
    m = jnp.mean(x, axis=axis, keepdims=True)
    v = jnp.var(x, axis=axis, keepdims=True)
    return (x - m) / jnp.sqrt(v + eps)

def _scatter_add(tgt, idx, src, axis=0):
    return tgt.at[idx].add(src)

def _segment_sum(src, seg, n):
    return jax.ops.segment_sum(src, seg, n)
kernel_name = 'mk_gps_d2_gnn_r8_739824'

def setup_inputs(seed: int=0):
    np.random.seed(seed)
    _w = jnp.asarray

    def _rec_inputs():
        import jax
        import jax.numpy as jnp
        _gk = jax.random.key(seed)
        x = -0.0001394 + 0.9999 * jax.random.normal(jax.random.fold_in(_gk, 1), (1250, 768), jnp.float32)
        _s = jax.random.randint(jax.random.fold_in(_gk, 2), (20000,), 0, 1250, jnp.int32)
        _d = jax.random.randint(jax.random.fold_in(_gk, 3), (20000,), 0, 1250, jnp.int32)
        _loop = jnp.arange(1250, dtype=jnp.int32)
        src = jnp.concatenate([_s, _d, _loop])
        dst = jnp.concatenate([_d, _s, _loop])
        _o = jnp.argsort(dst, stable=True)
        src = src[_o]
        dst = dst[_o]
        return (x, src, dst)
    x, src, dst = _rec_inputs()

    def _L0_gnn_setup():
        import jax, jax.numpy as jnp
        import numpy as np
        N = 6250
        E = 31250
        H = 12
        D = 64
        NEG_SLOPE = 0.2
        key = jax.random.key(seed)
        k1, k2, k3, k4, k5, k6, k7 = jax.random.split(key, 7)
        h = jax.random.normal(k1, (N, H * D), dtype=jnp.float32)
        src = jnp.concatenate([jnp.arange(N, dtype=jnp.int32), jax.random.randint(k2, (E - N,), 0, N, dtype=jnp.int32)])
        dst = jnp.concatenate([jnp.arange(N, dtype=jnp.int32), jax.random.randint(k3, (E - N,), 0, N, dtype=jnp.int32)])
        xav = 1.414 / np.sqrt(D)
        W_fc = jax.random.normal(k4, (D, D), dtype=jnp.float32) * xav
        attn_l = jax.random.normal(k5, (H, D), dtype=jnp.float32) * 0.15
        attn_r = jax.random.normal(k6, (H, D), dtype=jnp.float32) * 0.15
        W_res = jax.random.normal(k7, (D, D), dtype=jnp.float32) * xav
        return {'h': h, 'W_fc': W_fc, 'attn_l': attn_l, 'attn_r': attn_r, 'W_res': W_res, 'src': src, 'dst': dst}
    _L0_gnn_all = _L0_gnn_setup()
    _L0_gnn_in = {k: v for k, v in _L0_gnn_all.items() if k in ('W_fc', 'attn_l', 'attn_r', 'W_res')}
    del _L0_gnn_all

    def _L0_mix_setup():
        import jax, jax.numpy as jnp
        import numpy as np
        NUM_HEADS = 12

        def _reference_tuple_inner(x, w_qkv, w_proj, b_proj):
            B, N, C = x.shape
            H = NUM_HEADS
            D = C // H
            qkv = (x @ w_qkv).reshape(B, N, 3, H, D)
            q = jnp.transpose(qkv[:, :, 0], (0, 2, 1, 3))
            k = jnp.transpose(qkv[:, :, 1], (0, 2, 1, 3))
            v = jnp.transpose(qkv[:, :, 2], (0, 2, 1, 3))
            q = jax.nn.elu(q) + 1.0
            k = jax.nn.elu(k) + 1.0
            attn = jnp.einsum('bhnd,bhmd->bhnm', q, k)
            attn = attn / jnp.sum(attn, axis=-1, keepdims=True)
            out = jnp.einsum('bhnm,bhmd->bhnd', attn, v)
            out = jnp.transpose(out, (0, 2, 1, 3)).reshape(B, N, C)
            out = out @ w_proj + b_proj
            return (out, attn)
        key = jax.random.key(seed)
        k1, k2, k3 = jax.random.split(key, 3)
        B, N, C = (2, 256, 768)
        x = jax.random.normal(k1, (B, N, C), dtype=jnp.float32)
        w_qkv = jax.random.normal(k2, (C, 3 * C), dtype=jnp.float32) * 0.02
        w_proj = jax.random.normal(k3, (C, C), dtype=jnp.float32) * 0.02
        b_proj = jnp.zeros((C,), dtype=jnp.float32)
        return {'x': x, 'w_qkv': w_qkv, 'w_proj': w_proj, 'b_proj': b_proj}
    _L0_mix_all = _L0_mix_setup()
    _L0_mix_in = {k: v for k, v in _L0_mix_all.items() if k in ('w_qkv', 'w_proj', 'b_proj')}
    del _L0_mix_all

    def _L0_ffn_setup():
        import jax, jax.numpy as jnp
        import numpy as np
        B, T, H, F, E = (512, 32, 768, 384, 3)
        key = jax.random.key(seed)
        ks = jax.random.split(key, 4)
        s = 0.02
        return {'x': jax.random.normal(ks[0], (B, T, H), jnp.float32), 'Wg': jax.random.normal(ks[1], (E, H), jnp.float32) * s, 'W1': jax.random.normal(ks[2], (E, H, F), jnp.float32) * s, 'b1': jnp.zeros((E, F), jnp.float32), 'W2': jax.random.normal(ks[3], (E, F, H), jnp.float32) * s, 'b2': jnp.zeros((E, H), jnp.float32)}
    _L0_ffn_all = _L0_ffn_setup()
    _L0_ffn_in = {k: v for k, v in _L0_ffn_all.items() if k in ('Wg', 'W1', 'b1', 'W2', 'b2')}
    del _L0_ffn_all

    def _L1_gnn_setup():
        import jax, jax.numpy as jnp
        import numpy as np
        N_NODES = 1250
        N_EDGES = 12500
        DIM = 768
        key = jax.random.key(seed)
        k1, k2, k3, k4 = jax.random.split(key, 4)
        x = jax.random.normal(k1, (N_NODES, DIM), dtype=jnp.float32)
        edge_index = jax.random.randint(k2, (2, N_EDGES), 0, N_NODES, dtype=jnp.int32)
        W = jax.random.normal(k3, (DIM, DIM), dtype=jnp.float32) / np.sqrt(DIM)
        b = jnp.zeros((DIM,), dtype=jnp.float32)
        return {'x': x, 'edge_index': edge_index, 'W': W, 'b': b}
    _L1_gnn_all = _L1_gnn_setup()
    _L1_gnn_in = {k: v for k, v in _L1_gnn_all.items() if k in ('W', 'b')}
    del _L1_gnn_all

    def _L1_mix_setup():
        import jax, jax.numpy as jnp
        import numpy as np
        NUM_HEADS = 12
        EPS = 1e-06
        key = jax.random.key(seed)
        k1, k2, k3, k4, k5 = jax.random.split(key, 5)
        B, N, C = (8, 512, 768)
        scale = 1.0 / np.sqrt(C)
        return {'x': jax.random.normal(k1, (B, N, C), dtype=jnp.float32), 'W_qkv': jax.random.normal(k2, (C, 3 * C), dtype=jnp.float32) * scale, 'b_qkv': jax.random.normal(k3, (3 * C,), dtype=jnp.float32) * 0.02, 'W_proj': jax.random.normal(k4, (C, C), dtype=jnp.float32) * scale, 'b_proj': jax.random.normal(k5, (C,), dtype=jnp.float32) * 0.02}
    _L1_mix_all = _L1_mix_setup()
    _L1_mix_in = {k: v for k, v in _L1_mix_all.items() if k in ('W_qkv', 'b_qkv', 'W_proj', 'b_proj')}
    del _L1_mix_all

    def _L1_ffn_setup():
        import jax, jax.numpy as jnp
        import numpy as np
        DIM = 768
        HEADS = 12
        EXPERTS = 8
        HID = 384
        TOP_K = 2
        LN_EPS = 1e-05

        def _layer_norm(x, g, b):
            mu = x.mean(-1, keepdims=True)
            var = ((x - mu) ** 2).mean(-1, keepdims=True)
            return (x - mu) * jax.lax.rsqrt(var + LN_EPS) * g + b

        def _attention(x, qkv_w, qkv_b, proj_w, proj_b):
            B, N, C = x.shape
            hd = C // HEADS
            qkv = (x @ qkv_w + qkv_b).reshape(B, N, 3, HEADS, hd).transpose(2, 0, 3, 1, 4)
            q, k, v = (qkv[0], qkv[1], qkv[2])
            attn = jax.nn.softmax(jnp.einsum('bhnd,bhmd->bhnm', q, k) * hd ** (-0.5), axis=-1)
            o = jnp.einsum('bhnm,bhmd->bhnd', attn, v).transpose(0, 2, 1, 3).reshape(B, N, C)
            return o @ proj_w + proj_b

        def _moe_mlp(xn, gate_w, w1, b1, w2, b2):
            T = xn.shape[0]
            logits = xn @ gate_w
            top_logits, top_idx = jax.lax.top_k(logits, TOP_K)
            top_gates = jax.nn.softmax(top_logits, axis=-1)
            gates = jnp.zeros((T, EXPERTS), xn.dtype).at[jnp.arange(T)[:, None], top_idx].set(top_gates)
            h = jax.nn.gelu(jnp.einsum('td,edh->teh', xn, w1) + b1, approximate=False)
            y = jnp.einsum('teh,ehd->ted', h, w2) + b2
            return jnp.einsum('ted,te->td', y, gates)
        key = jax.random.key(seed)
        ks = jax.random.split(key, 16)
        s = 0.02
        return {'x': jax.random.normal(ks[0], (8, 196, DIM), jnp.float32), 'ln1_g': jnp.ones((DIM,), jnp.float32), 'ln1_b': jnp.zeros((DIM,), jnp.float32), 'qkv_w': jax.random.normal(ks[1], (DIM, 3 * DIM), jnp.float32) * s, 'qkv_b': jnp.zeros((3 * DIM,), jnp.float32), 'proj_w': jax.random.normal(ks[2], (DIM, DIM), jnp.float32) * s, 'proj_b': jnp.zeros((DIM,), jnp.float32), 'ln2_g': jnp.ones((DIM,), jnp.float32), 'ln2_b': jnp.zeros((DIM,), jnp.float32), 'gate_w': jax.random.normal(ks[3], (DIM, EXPERTS), jnp.float32) * s, 'w1': jax.random.normal(ks[4], (EXPERTS, DIM, HID), jnp.float32) * s, 'b1': jnp.zeros((EXPERTS, HID), jnp.float32), 'w2': jax.random.normal(ks[5], (EXPERTS, HID, DIM), jnp.float32) * s, 'b2': jnp.zeros((EXPERTS, DIM), jnp.float32)}
    _L1_ffn_all = _L1_ffn_setup()
    _L1_ffn_in = {k: v for k, v in _L1_ffn_all.items() if k in ('ln1_g', 'ln1_b', 'qkv_w', 'qkv_b', 'proj_w', 'proj_b', 'ln2_g', 'ln2_b', 'gate_w', 'w1', 'b1', 'w2', 'b2')}
    del _L1_ffn_all
    return {'x': x, 'src': src, 'dst': dst, 'L0_gnn_W_fc': _L0_gnn_in['W_fc'], 'L0_gnn_attn_l': _L0_gnn_in['attn_l'], 'L0_gnn_attn_r': _L0_gnn_in['attn_r'], 'L0_gnn_W_res': _L0_gnn_in['W_res'], 'L0_mix_w_qkv': _L0_mix_in['w_qkv'], 'L0_mix_w_proj': _L0_mix_in['w_proj'], 'L0_mix_b_proj': _L0_mix_in['b_proj'], 'L0_ffn_Wg': _L0_ffn_in['Wg'], 'L0_ffn_W1': _L0_ffn_in['W1'], 'L0_ffn_b1': _L0_ffn_in['b1'], 'L0_ffn_W2': _L0_ffn_in['W2'], 'L0_ffn_b2': _L0_ffn_in['b2'], 'L1_gnn_W': _L1_gnn_in['W'], 'L1_gnn_b': _L1_gnn_in['b'], 'L1_mix_W_qkv': _L1_mix_in['W_qkv'], 'L1_mix_b_qkv': _L1_mix_in['b_qkv'], 'L1_mix_W_proj': _L1_mix_in['W_proj'], 'L1_mix_b_proj': _L1_mix_in['b_proj'], 'L1_ffn_ln1_g': _L1_ffn_in['ln1_g'], 'L1_ffn_ln1_b': _L1_ffn_in['ln1_b'], 'L1_ffn_qkv_w': _L1_ffn_in['qkv_w'], 'L1_ffn_qkv_b': _L1_ffn_in['qkv_b'], 'L1_ffn_proj_w': _L1_ffn_in['proj_w'], 'L1_ffn_proj_b': _L1_ffn_in['proj_b'], 'L1_ffn_ln2_g': _L1_ffn_in['ln2_g'], 'L1_ffn_ln2_b': _L1_ffn_in['ln2_b'], 'L1_ffn_gate_w': _L1_ffn_in['gate_w'], 'L1_ffn_w1': _L1_ffn_in['w1'], 'L1_ffn_b1': _L1_ffn_in['b1'], 'L1_ffn_w2': _L1_ffn_in['w2'], 'L1_ffn_b2': _L1_ffn_in['b2']}

def reference(x, src, dst, L0_gnn_W_fc, L0_gnn_attn_l, L0_gnn_attn_r, L0_gnn_W_res, L0_mix_w_qkv, L0_mix_w_proj, L0_mix_b_proj, L0_ffn_Wg, L0_ffn_W1, L0_ffn_b1, L0_ffn_W2, L0_ffn_b2, L1_gnn_W, L1_gnn_b, L1_mix_W_qkv, L1_mix_b_qkv, L1_mix_W_proj, L1_mix_b_proj, L1_ffn_ln1_g, L1_ffn_ln1_b, L1_ffn_qkv_w, L1_ffn_qkv_b, L1_ffn_proj_w, L1_ffn_proj_b, L1_ffn_ln2_g, L1_ffn_ln2_b, L1_ffn_gate_w, L1_ffn_w1, L1_ffn_b1, L1_ffn_w2, L1_ffn_b2):
    import jax
    import jax.numpy as jnp

    def _L0_gnn_ref(h, W_fc, attn_l, attn_r, W_res, src, dst):
        import jax, jax.numpy as jnp
        import numpy as np
        N = 6250
        E = 31250
        H = 12
        D = 64
        NEG_SLOPE = 0.2
        n = h.shape[0]
        hh = h.reshape(n, H, D)
        ft = jnp.einsum('nhd,ed->nhe', hh, W_fc)
        a1 = jnp.einsum('nhd,hd->nh', ft, attn_l)
        a2 = jnp.einsum('nhd,hd->nh', ft, attn_r)
        e = jax.nn.leaky_relu(a1[src] + a2[dst], negative_slope=NEG_SLOPE)
        m = jax.ops.segment_max(e, dst, num_segments=n)
        ee = jnp.exp(e - m[dst])
        denom = jax.ops.segment_sum(ee, dst, num_segments=n)
        alpha = ee / denom[dst]
        agg = jax.ops.segment_sum(alpha[:, :, None] * ft[src], dst, num_segments=n)
        res = jnp.einsum('nhd,ed->nhe', hh, W_res)
        return jax.nn.relu((res + agg).reshape(n, H * D))

    def _L0_mix_ref(x, w_qkv, w_proj, b_proj):
        import jax, jax.numpy as jnp
        import numpy as np
        NUM_HEADS = 12

        def _reference_tuple_inner(x, w_qkv, w_proj, b_proj):
            B, N, C = x.shape
            H = NUM_HEADS
            D = C // H
            qkv = (x @ w_qkv).reshape(B, N, 3, H, D)
            q = jnp.transpose(qkv[:, :, 0], (0, 2, 1, 3))
            k = jnp.transpose(qkv[:, :, 1], (0, 2, 1, 3))
            v = jnp.transpose(qkv[:, :, 2], (0, 2, 1, 3))
            q = jax.nn.elu(q) + 1.0
            k = jax.nn.elu(k) + 1.0
            attn = jnp.einsum('bhnd,bhmd->bhnm', q, k)
            attn = attn / jnp.sum(attn, axis=-1, keepdims=True)
            out = jnp.einsum('bhnm,bhmd->bhnd', attn, v)
            out = jnp.transpose(out, (0, 2, 1, 3)).reshape(B, N, C)
            out = out @ w_proj + b_proj
            return (out, attn)
        return _reference_tuple_inner(x, w_qkv, w_proj, b_proj)[0]

    def _L0_ffn_ref(x, Wg, W1, b1, W2, b2):
        import jax, jax.numpy as jnp
        import numpy as np
        B, T, H, F, E = (512, 32, 768, 384, 3)
        scores = jax.nn.softmax(jnp.mean(x, axis=1) @ Wg.T, axis=-1)
        _, idx = jax.lax.top_k(scores, 1)
        sel = idx[:, 0]
        h = jax.nn.gelu(jnp.einsum('bth,ehf->betf', x, W1) + b1[None, :, None, :], approximate=False)
        y = jnp.einsum('betf,efh->beth', h, W2) + b2[None, :, None, :]
        w = scores * jax.nn.one_hot(sel, E, dtype=scores.dtype)
        out = jnp.einsum('beth,be->bth', y, w)
        return out

    def _L1_gnn_ref(x, edge_index, W, b):
        import jax, jax.numpy as jnp
        import numpy as np
        N_NODES = 1250
        N_EDGES = 12500
        DIM = 768
        n = x.shape[0]
        loop = jnp.arange(n, dtype=edge_index.dtype)
        src = jnp.concatenate([edge_index[0], loop])
        dst = jnp.concatenate([edge_index[1], loop])
        deg = jax.ops.segment_sum(jnp.ones_like(dst, dtype=x.dtype), dst, num_segments=n)
        deg_inv_sqrt = jnp.where(deg > 0, jax.lax.rsqrt(deg), 0.0)
        norm = deg_inv_sqrt[src] * deg_inv_sqrt[dst]
        h = x @ W
        msg = h[src] * norm[:, None]
        out = jax.ops.segment_sum(msg, dst, num_segments=n)
        return out + b

    def _L1_mix_ref(x, W_qkv, b_qkv, W_proj, b_proj):
        import jax, jax.numpy as jnp
        import numpy as np
        NUM_HEADS = 12
        EPS = 1e-06
        B, N, C = x.shape
        H = NUM_HEADS
        D = C // H
        qkv = (x @ W_qkv + b_qkv).reshape(B, N, 3, H, D).transpose(2, 0, 3, 1, 4)
        q, k, v = (qkv[0], qkv[1], qkv[2])
        q = jax.nn.sigmoid(q)
        k = jax.nn.sigmoid(k)
        ksum = k.sum(axis=2)
        qsum = q.sum(axis=2)
        sink_incoming = 1.0 / (jnp.einsum('bhnd,bhd->bhn', q + EPS, ksum + EPS) + EPS)
        source_outgoing = 1.0 / (jnp.einsum('bhnd,bhd->bhn', k + EPS, qsum + EPS) + EPS)
        conserved_sink = jnp.einsum('bhnd,bhd->bhn', q + EPS, (k * source_outgoing[..., None]).sum(axis=2) + EPS) + EPS
        conserved_source = jnp.einsum('bhnd,bhd->bhn', k + EPS, (q * sink_incoming[..., None]).sum(axis=2) + EPS) + EPS
        conserved_source = jnp.clip(conserved_source, -1.0, 1.0)
        sink_allocation = jax.nn.sigmoid(conserved_sink * (float(N) / float(N)))
        source_competition = jax.nn.softmax(conserved_source, axis=-1) * float(N)
        kv = jnp.einsum('bhnd,bhne->bhde', k, v * source_competition[..., None])
        x_update = jnp.einsum('bhnd,bhde->bhne', q, kv)
        x_update = x_update * sink_incoming[..., None] * sink_allocation[..., None]
        out = x_update.transpose(0, 2, 1, 3).reshape(B, N, C)
        out = out @ W_proj + b_proj
        return jax.nn.sigmoid(2.0 * out)

    def _L1_ffn_ref(x, ln1_g, ln1_b, qkv_w, qkv_b, proj_w, proj_b, ln2_g, ln2_b, gate_w, w1, b1, w2, b2):
        import jax, jax.numpy as jnp
        import numpy as np
        DIM = 768
        HEADS = 12
        EXPERTS = 8
        HID = 384
        TOP_K = 2
        LN_EPS = 1e-05

        def _layer_norm(x, g, b):
            mu = x.mean(-1, keepdims=True)
            var = ((x - mu) ** 2).mean(-1, keepdims=True)
            return (x - mu) * jax.lax.rsqrt(var + LN_EPS) * g + b

        def _attention(x, qkv_w, qkv_b, proj_w, proj_b):
            B, N, C = x.shape
            hd = C // HEADS
            qkv = (x @ qkv_w + qkv_b).reshape(B, N, 3, HEADS, hd).transpose(2, 0, 3, 1, 4)
            q, k, v = (qkv[0], qkv[1], qkv[2])
            attn = jax.nn.softmax(jnp.einsum('bhnd,bhmd->bhnm', q, k) * hd ** (-0.5), axis=-1)
            o = jnp.einsum('bhnm,bhmd->bhnd', attn, v).transpose(0, 2, 1, 3).reshape(B, N, C)
            return o @ proj_w + proj_b

        def _moe_mlp(xn, gate_w, w1, b1, w2, b2):
            T = xn.shape[0]
            logits = xn @ gate_w
            top_logits, top_idx = jax.lax.top_k(logits, TOP_K)
            top_gates = jax.nn.softmax(top_logits, axis=-1)
            gates = jnp.zeros((T, EXPERTS), xn.dtype).at[jnp.arange(T)[:, None], top_idx].set(top_gates)
            h = jax.nn.gelu(jnp.einsum('td,edh->teh', xn, w1) + b1, approximate=False)
            y = jnp.einsum('teh,ehd->ted', h, w2) + b2
            return jnp.einsum('ted,te->td', y, gates)
        B, N, C = x.shape
        x = x + _attention(_layer_norm(x, ln1_g, ln1_b), qkv_w, qkv_b, proj_w, proj_b)
        xn = _layer_norm(x, ln2_g, ln2_b).reshape(B * N, C)
        moe_out = _moe_mlp(xn, gate_w, w1, b1, w2, b2).reshape(B, N, C)
        return x + moe_out
    edge_index = jnp.stack([src, dst])
    xn = _layernorm(x, axis=-1)
    x = x + _L0_gnn_ref(xn, L0_gnn_W_fc, L0_gnn_attn_l, L0_gnn_attn_r, L0_gnn_W_res, src, dst) + _L0_mix_ref(xn[None], L0_mix_w_qkv, L0_mix_w_proj, L0_mix_b_proj)[0]
    x = x + _L0_ffn_ref(_layernorm(x, axis=-1)[None], L0_ffn_Wg, L0_ffn_W1, L0_ffn_b1, L0_ffn_W2, L0_ffn_b2)[0]
    xn = _layernorm(x, axis=-1)
    x = x + _L1_gnn_ref(xn, edge_index, L1_gnn_W, L1_gnn_b) + _L1_mix_ref(xn[None], L1_mix_W_qkv, L1_mix_b_qkv, L1_mix_W_proj, L1_mix_b_proj)[0]
    x = x + _L1_ffn_ref(_layernorm(x, axis=-1)[None], L1_ffn_ln1_g, L1_ffn_ln1_b, L1_ffn_qkv_w, L1_ffn_qkv_b, L1_ffn_proj_w, L1_ffn_proj_b, L1_ffn_ln2_g, L1_ffn_ln2_b, L1_ffn_gate_w, L1_ffn_w1, L1_ffn_b1, L1_ffn_w2, L1_ffn_b2)[0]
    return x

_drawn_inputs = setup_inputs


def setup_inputs(seed=0):
    import zlib

    import numpy as np

    out = dict(_drawn_inputs(seed))
    spreads = {'L0_mix_b_proj': (0.0, 0.1),
     'L0_ffn_b1': (0.0, 0.8),
     'L0_ffn_b2': (0.0, 0.1),
     'L1_gnn_b': (0.0, 0.1),
     'L1_ffn_ln1_g': (1.0, 0.6),
     'L1_ffn_ln1_b': (0.0, 0.583),
     'L1_ffn_qkv_b': (0.0, 0.34),
     'L1_ffn_proj_b': (0.0, 0.1),
     'L1_ffn_ln2_g': (1.0, 0.6),
     'L1_ffn_ln2_b': (0.0, 0.57),
     'L1_ffn_b1': (0.0, 0.8),
     'L1_ffn_b2': (0.0, 0.29)}
    factors = {'L0_mix_w_qkv': 7.025, 'L0_mix_w_proj': 7.487, 'L1_mix_b_qkv': 8.0, 'L1_mix_b_proj': 7.719}
    for name, (base, spread) in spreads.items():
        noise = np.random.default_rng([zlib.crc32(name.encode()), seed]).standard_normal(out[name].shape)
        drawn = base * np.exp(spread * noise) if base else spread * noise
        out[name] = jnp.asarray(drawn.astype(out[name].dtype))
    for name, factor in factors.items():
        out[name] = (out[name] * factor).astype(out[name].dtype)
    return out
```

```python
from contextlib import ExitStack

import concourse.bass as bass
from concourse import mybir

F32 = mybir.dt.float32
F16 = mybir.dt.float16
BF16 = mybir.dt.bfloat16
I32 = mybir.dt.int32
ALU = mybir.AluOpType
ACT = mybir.ActivationFunctionType
AX_X = mybir.AxisListType.X

P = 128
N = 1250
D = 768
KT = D // P
TT = 125
NT = N // TT
H = 12
E = 41250
ET = E // TT
EG = 3
ER = ET // EG
CHUNKS = ((0, 417), (417, 417), (834, 416))
CW = 417
BIG = 3.0e38
LN_EPS = 1e-5


def bank(banks, i):
    return banks[i]


def wide(ap, n):
    return ap.unsqueeze(1).broadcast_to([ap.shape[0], n, ap.shape[1]])


def stage_constants(nc, g):
    g.new_stage()
    with nc.Block() as block:
        filled = g.sem("const_filled")
        done = g.sem("const_done")

        @block.gpsimd
        def _(pool):
            pool.memset(g.ident[:, :], 0.0).then_inc(filled, 1)
            pool.memset(g.ones[:, :], 1.0).then_inc(filled, 1)
            pool.memset(g.pair_mask[:, :], 0.0).then_inc(filled, 1)
            pool.memset(g.eps5[:, :], LN_EPS).then_inc(filled, 1)
            pool.wait_ge(filled, 4)
            pool.affine_select(out=g.ident[:, :], in_=g.ident[:, :], compare_op=ALU.not_equal, fill=1.0,
                               base=0, pattern=[[-1, P]], channel_multiplier=1).then_inc(done, 1)

        @block.vector
        def _(dve):
            dve.wait_ge(filled, 4)
            dve.memset(g.pair_mask[0:64, 0:64], 1.0).then_inc(done, 1)
            dve.memset(g.pair_mask[64:128, 64:128], 1.0).then_inc(done, 1)


def stage_adjacency(nc, g, src, dst):
    g.new_stage()
    with ExitStack() as c:
        edge_rows = g.sb(c, "edge_rows", [ER, 2, EG, TT], I32)
        edge_f = g.sb(c, "edge_f", [ER, 2, EG, TT], F32)
        edge_cols = g.sb(c, "edge_cols", [TT, 2, ET], F32)
        node_ids = g.sb(c, "node_ids", [TT, N], I32)
        node_ids16 = g.sb(c, "node_ids16", [TT, N], F16)
        tile_range = g.sb(c, "tile_range", [ER, 2, EG], F32)
        range_rows = g.sb(c, "range_rows", [NT, 2, ET], F32)
        tile_ids = g.sb(c, "tile_ids", [NT, 2, ET], I32)
        tile_idf = g.sb(c, "tile_idf", [NT, 2, ET], F32)
        block_lo_i = g.sb(c, "block_lo_i", [NT, 2], I32)
        block_lo = g.sb(c, "block_lo", [NT, 2], F32)
        touches = g.sb(c, "touches", [NT, ET], F32)
        first_last = g.sb(c, "first_last", [NT, 6], F32)
        before = g.sb(c, "before", [NT, NT], F32)
        loop_f = g.sb(c, "loop_f", [NT, 3], F32)
        loop_i = g.sb(c, "loop_i", [NT, 3], I32)
        loop_row = g.sb(c, "loop_row", [1, NT * 3], I32)
        zeros = g.sb(c, "zeros", [TT, TT], BF16)
        SLOTS = 4
        hot_dst = g.sb(c, "hot_dst", [TT, SLOTS, TT], BF16)
        hot_src = g.sb(c, "hot_src", [TT, SLOTS, N], BF16)
        staged = g.sb(c, "staged", [TT, N], F32)

        loaded = g.sem("adj_loaded")
        made = g.sem("adj_ids_made")
        floats = g.sem("adj_floats")
        turned = g.sem("adj_turned")
        vec = g.sem("adj_vec")
        cnt = g.sem("adj_cumulative")
        ranged = g.sem("adj_ranges_stored")
        hots = g.sem("adj_onehots")
        used = g.sem("adj_onehots_used")
        counted = g.sem("adj_counted")
        staged_s = g.sem("adj_staged")
        turned_t = g.sem("adj_counts_turned")
        kept = g.sem("adj_kept")
        ps = g.psum

        with nc.Block() as block:
            @block.sync
            def _(sp):
                for n, e in ((0, src), (1, dst)):
                    sp.dma_start(edge_rows[:, n], e.rearrange("(g r e) -> r g e", g=EG, e=TT)).then_inc(loaded, 16)
                sp.wait_ge(vec, 12)
                sp.dma_start(loop_row[0:1, :], loop_i[:, :]).then_inc(ranged, 16)

            @block.gpsimd
            def _(pool):
                pool.iota(node_ids[:, :], pattern=[[1, N]], base=0, channel_multiplier=0).then_inc(made, 1)
                pool.iota(tile_ids[:, 0], pattern=[[1, ET]], base=1, channel_multiplier=0).then_inc(made, 1)
                pool.iota(tile_ids[:, 1], pattern=[[-1, ET]], base=ET, channel_multiplier=0).then_inc(made, 1)
                pool.iota(block_lo_i[:, 0:1], pattern=[[0, 1]], base=0, channel_multiplier=TT).then_inc(made, 1)
                pool.iota(block_lo_i[:, 1:2], pattern=[[0, 1]], base=TT, channel_multiplier=TT).then_inc(made, 1)
                pool.memset(before[:, :], 1.0).then_inc(made, 1)
                pool.memset(zeros[:, :], 0.0).then_inc(made, 1)
                pool.wait_ge(made, 7)
                pool.affine_select(out=before[:, :], in_=before[:, :], compare_op=ALU.is_gt, fill=0.0,
                                   base=0, pattern=[[1, NT]], channel_multiplier=-1).then_inc(made, 1)

            @block.vector
            def _(dve):
                dve.wait_ge(loaded, 32)
                dve.tensor_copy(edge_f[:, :, :, :], edge_rows[:, :, :, :]).then_inc(floats, 1)
                dve.wait_ge(floats, 1)
                dve.tensor_reduce(tile_range[:, 0], edge_f[:, 1], AX_X, ALU.min).then_inc(floats, 1)
                dve.tensor_reduce(tile_range[:, 1], edge_f[:, 1], AX_X, ALU.max).then_inc(floats, 1)
                dve.wait_ge(made, 8)
                dve.tensor_copy(node_ids16[:, :], node_ids[:, :]).then_inc(vec, 1)
                dve.tensor_copy(tile_idf[:, :, :], tile_ids[:, :, :]).then_inc(vec, 1)
                dve.tensor_copy(block_lo[:, :], block_lo_i[:, :]).then_inc(vec, 1)
                dve.wait_ge(turned, 1)
                dve.tensor_copy(edge_cols[:, 0], ps[0][0:TT, 0:ET]).then_inc(vec, 1)
                dve.tensor_copy(edge_cols[:, 1], ps[1][0:TT, 0:ET]).then_inc(vec, 1)
                dve.wait_ge(turned, 2)
                dve.tensor_copy(range_rows[:, 0], ps[2][0:NT, 0:ET]).then_inc(vec, 1)
                dve.tensor_copy(range_rows[:, 1], ps[3][0:NT, 0:ET]).then_inc(vec, 1)
                dve.wait_ge(vec, 7)
                dve.tensor_scalar(touches[:, :], range_rows[:, 0], block_lo[:, 1:2], None, ALU.is_lt).then_inc(vec, 1)
                dve.wait_ge(vec, 8)
                dve.scalar_tensor_tensor(out=touches[:, :], in0=range_rows[:, 1], scalar=block_lo[:, 0:1],
                                         in1=touches[:, :], op0=ALU.is_ge, op1=ALU.mult).then_inc(vec, 1)
                dve.wait_ge(vec, 9)
                dve.tensor_tensor(range_rows[:, :, :], tile_idf[:, :, :], wide(touches[:, :], 2), ALU.mult).then_inc(vec, 1)
                dve.wait_ge(vec, 10)
                dve.tensor_reduce(first_last[:, 0:2], range_rows[:, :, :], AX_X, ALU.max).then_inc(vec, 1)
                dve.wait_ge(vec, 11)
                dve.tensor_scalar(first_last[:, 2:3], first_last[:, 1:2], -1.0, float(ET), ALU.mult, ALU.add).then_inc(cnt, 1)
                dve.wait_ge(cnt, 1)
                dve.tensor_scalar(first_last[:, 3:4], first_last[:, 2:3], float(ET - 1), None, ALU.min).then_inc(cnt, 1)
                dve.wait_ge(cnt, 2)
                dve.tensor_tensor(first_last[:, 4:5], first_last[:, 0:1], first_last[:, 3:4], ALU.subtract).then_inc(cnt, 1)
                dve.wait_ge(cnt, 3)
                dve.tensor_scalar(first_last[:, 5:6], first_last[:, 4:5], 1.0, None, ALU.max).then_inc(cnt, 1)
                dve.wait_ge(turned, 3)
                dve.tensor_copy(loop_f[:, 0:1], ps[4][0:NT, 0:1]).then_inc(cnt, 1)
                dve.wait_ge(cnt, 5)
                dve.tensor_tensor(loop_f[:, 1:2], loop_f[:, 0:1], first_last[:, 5:6], ALU.add).then_inc(cnt, 1)
                dve.tensor_tensor(loop_f[:, 2:3], first_last[:, 3:4], loop_f[:, 0:1], ALU.subtract).then_inc(cnt, 1)
                dve.wait_ge(cnt, 7)
                dve.tensor_copy(loop_i[:, :], loop_f[:, :]).then_inc(vec, 1)
                dve.sem_inc(kept, 1)
                dve.wait_ge(ranged, 16)
                dve.sem_inc(used, SLOTS)
                with dve.Fori(0, NT) as b:
                    lo = dve.value_load(loop_row[0:1, bass.ds(b * 3, 1)], min_val=0, max_val=ET * NT - 1)
                    hi = dve.value_load(loop_row[0:1, bass.ds(b * 3 + 1, 1)], min_val=1, max_val=ET * NT)
                    shift = dve.value_load(loop_row[0:1, bass.ds(b * 3 + 2, 1)], min_val=-ET * NT, max_val=ET)
                    with dve.Fori(lo, hi) as i:
                        t = nc.s_assert_within(dve.snap(i + shift), 0, ET - 1)
                        slot = dve.snap(i % SLOTS)
                        dve.wait_ge(used, i + 1)
                        dve.tensor_scalar(hot_dst[:, bass.ds(slot, 1)].squeeze(1), node_ids16[:, bass.ds(b * TT, TT)],
                                          edge_cols[:, 1, bass.ds(t, 1)], None, ALU.is_equal)
                        dve.tensor_scalar(hot_src[:, bass.ds(slot, 1)].squeeze(1), node_ids16[:, :],
                                          edge_cols[:, 0, bass.ds(t, 1)], None, ALU.is_equal).then_inc(hots, 1)
                    dve.wait_ge(turned_t, b + 1)
                    for j0, j1 in ((0, 4), (4, 8), (8, 10)):
                        op = dve.tensor_copy(g.counts_T[:, j0:j1, bass.ds(b * TT, TT)],
                                             ps[4 + j0 // 4][0:TT, 0:(j1 - j0) * TT].rearrange("p (j d) -> p j d", j=j1 - j0))
                    dve.tensor_scalar(g.no_edge[:, bass.ds(b, 1)].squeeze(1), staged[:, :], 0.5, -BIG, ALU.is_lt, ALU.mult).then_inc(kept, 1)

            @block.scalar
            def _(act):
                with act.Fori(0, NT) as b:
                    act.wait_ge(counted, b + 1)
                    act.wait_ge(kept, b + 1)
                    for n, (c0, w) in enumerate(CHUNKS):
                        op = act.activation(staged[:, c0:c0 + w], ps[n][0:TT, 0:w], ACT.Copy)
                    op.then_inc(staged_s, 1)

            @block.tensor
            def _(pe):
                pe.wait_ge(floats, 1)
                for n in range(2):
                    for k in range(EG):
                        op = pe.transpose(ps[n][0:TT, k * ER:(k + 1) * ER], edge_f[:, n, k], g.ident[0:ER, 0:ER])
                op.then_inc(turned, 1)
                pe.wait_ge(floats, 3)
                for n in range(2):
                    for k in range(EG):
                        op = pe.matmul(ps[2 + n][0:NT, k * ER:(k + 1) * ER],
                                       tile_range[:, n, k:k + 1].broadcast_to([ER, NT]), g.ident[0:ER, 0:ER],
                                       start=True, stop=True)
                op.then_inc(turned, 1)
                pe.wait_ge(cnt, 4)
                pe.matmul(ps[4][0:NT, 0:1], before[:, :], first_last[:, 5:6], start=True, stop=True).then_inc(turned, 1)
                pe.wait_ge(vec, 12)
                pe.wait_ge(ranged, 16)
                with pe.Fori(0, NT) as b:
                    lo = pe.value_load(loop_row[0:1, bass.ds(b * 3, 1)], min_val=0, max_val=ET * NT - 1)
                    hi = pe.value_load(loop_row[0:1, bass.ds(b * 3 + 1, 1)], min_val=1, max_val=ET * NT)
                    pe.wait_ge(made, 8)
                    for n, (c0, w) in enumerate(CHUNKS):
                        pe.matmul(ps[n][0:TT, 0:w], zeros[:, :], node_ids16[:, 0:w], start=True, stop=False,
                                  skip_group_check=True)
                    with pe.Fori(lo, hi) as i:
                        slot = pe.snap(i % SLOTS)
                        pe.wait_ge(hots, i + 1)
                        for n, (c0, w) in enumerate(CHUNKS):
                            op = pe.matmul(ps[n][0:TT, 0:w], hot_dst[:, bass.ds(slot, 1)].squeeze(1),
                                           hot_src[:, bass.ds(slot, 1), c0:c0 + w].squeeze(1),
                                           start=False, stop=False, skip_group_check=True)
                        op.then_inc(used, 1)
                    for n, (c0, w) in enumerate(CHUNKS):
                        op = pe.matmul(ps[n][0:TT, 0:w], zeros[:, :], node_ids16[:, 0:w], start=False, stop=True,
                                       skip_group_check=True)
                    op.then_inc(counted, 1)
                    pe.wait_ge(staged_s, b + 1)
                    for j in range(NT):
                        op = pe.transpose(ps[4 + j // 4][0:TT, (j % 4) * TT:(j % 4 + 1) * TT],
                                          staged[:, j * TT:(j + 1) * TT], g.ident[0:TT, 0:TT])
                    op.then_inc(turned_t, 1)


def stage_load(nc, g, x):
    g.new_stage()
    with ExitStack() as c:
        x_rows = g.sb(c, "x_rows", [TT, NT, D], F32)
        loaded = [g.sem(f"x_loaded{i}") for i in range(NT)]
        turned = g.sem("x_turned")
        kept = g.sem("x_kept")
        ps = g.psum
        with nc.Block() as block:
            @block.sync
            def _(sp):
                for t in range(NT):
                    sp.dma_start(x_rows[:, t], x[t * TT:(t + 1) * TT, :]).then_inc(loaded[t], 16)

            @block.tensor
            def _(pe):
                for t in range(NT):
                    pe.wait_ge(loaded[t], 16)
                    if t >= 4:
                        pe.wait_ge(kept, t - 3)
                    for k in range(KT):
                        op = pe.transpose(ps[2 * (t % 4) + k // 3][:, (k % 3) * TT:(k % 3 + 1) * TT],
                                          x_rows[:, t, k * P:(k + 1) * P], g.ident[0:TT, 0:TT])
                    op.then_inc(turned, 1)

            @block.vector
            def _(dve):
                for t in range(NT):
                    dve.wait_ge(turned, t + 1)
                    for h in range(2):
                        op = dve.tensor_copy(g.x_T[:, 3 * h:3 * h + 3, t * TT:(t + 1) * TT],
                                             ps[2 * (t % 4) + h][:, 0:3 * TT].rearrange("p (k n) -> p k n", k=3))
                    op.then_inc(kept, 1)


def stage_store(nc, g, out, add=None):
    g.new_stage()
    with ExitStack() as c:
        rows = g.sb(c, "out_rows", [TT, 2, D], F32)
        turned = g.sem("out_turned")
        kept = g.sem("out_kept")
        whole = g.sem("out_whole")
        stored = [g.sem(f"out_stored{i}") for i in range(2)]
        ps = g.psum
        with nc.Block() as block:
            @block.tensor
            def _(pe):
                if add is not None:
                    pe.wait_ge(whole, KT)
                for t in range(NT):
                    if t >= 4:
                        pe.wait_ge(kept, t - 3)
                    for k in range(KT):
                        op = pe.transpose(ps[2 * (t % 4) + k // 3][0:TT, (k % 3) * P:(k % 3 + 1) * P],
                                          g.x_T[:, k, t * TT:(t + 1) * TT], g.ident[:, :])
                    op.then_inc(turned, 1)

            @block.vector
            def _(dve):
                if add is not None:
                    for k in range(KT):
                        dve.tensor_tensor(g.x_T[:, k], g.x_T[:, k], add[:, k], ALU.add).then_inc(whole, 1)
                for t in range(NT):
                    dve.wait_ge(turned, t + 1)
                    if t >= 2:
                        dve.wait_ge(stored[t % 2], 16 * (t // 2))
                    for h in range(2):
                        op = dve.tensor_copy(rows[:, t % 2, h * 384:(h + 1) * 384], ps[2 * (t % 4) + h][0:TT, 0:3 * P])
                    op.then_inc(kept, 1)

            @block.sync
            def _(sp):
                for t in range(NT):
                    sp.wait_ge(kept, t + 1)
                    sp.dma_start(out[t * TT:(t + 1) * TT, :], rows[:, t % 2]).then_inc(stored[t % 2], 16)
                for s in range(2):
                    sp.wait_ge(stored[s], 16 * (NT // 2))


def stage_norm(nc, g, name, src, dst, gamma=None, beta=None):
    g.new_stage()
    with ExitStack() as c:
        mean = g.sb(c, f"{name}_mean", [P, 2, CW], F32)
        square = g.sb(c, f"{name}_square", [P, 2, KT, CW], F32)
        std = g.sb(c, f"{name}_std", [P, 2, CW], F32)
        rstd = g.sb(c, f"{name}_rstd", [P, 2, CW], F32)
        gb = g.sb(c, f"{name}_gb", [P, 2, KT], F32)
        summed = g.sem(f"{name}_summed")
        meaned = g.sem(f"{name}_meaned")
        centred = g.sem(f"{name}_centred")
        squared = g.sem(f"{name}_squared")
        varied = g.sem(f"{name}_varied")
        rooted = g.sem(f"{name}_rooted")
        inverted = g.sem(f"{name}_inverted")
        scaled = g.sem(f"{name}_scaled")
        gb_loaded = g.sem(f"{name}_gb_loaded")
        ps = g.psum
        n_ch = len(CHUNKS)
        with nc.Block() as block:
            if gamma is not None:
                @block.sync
                def _(sp):
                    sp.dma_start(gb[:, 0], gamma.rearrange("(k p) -> p k", p=P), allow_slow_non_contiguous=True).then_inc(gb_loaded, 16)
                    sp.dma_start(gb[:, 1], beta.rearrange("(k p) -> p k", p=P), allow_slow_non_contiguous=True).then_inc(gb_loaded, 16)

            @block.tensor
            def _(pe):
                def total(n, tensor, b, sem):
                    c0, w = CHUNKS[n]
                    for k in range(KT):
                        op = pe.matmul(ps[b][:, 0:w], g.ones[:, :], tensor(k), start=(k == 0), stop=(k == KT - 1))
                    op.then_inc(sem, 1)

                for n, (c0, w) in enumerate(CHUNKS):
                    total(n, lambda k: src[:, k, c0:c0 + w], n, summed)
                for n, (c0, w) in enumerate(CHUNKS):
                    pe.wait_ge(squared, n + 1)
                    total(n, lambda k: square[:, n % 2, k, 0:w], 3 + n, varied)

            @block.scalar
            def _(act):
                def to_mean(n):
                    c0, w = CHUNKS[n]
                    act.wait_ge(summed, n + 1)
                    if n >= 2:
                        act.wait_ge(centred, n - 1)
                    act.activation(mean[:, n % 2, 0:w], ps[n][:, 0:w], ACT.Copy, scale=1.0 / D).then_inc(meaned, 1)

                def to_square(n):
                    c0, w = CHUNKS[n]
                    act.wait_ge(centred, n + 1)
                    if n >= 2:
                        act.wait_ge(varied, n - 1)
                    act.activation(square[:, n % 2, :, 0:w], dst[:, :, c0:c0 + w], ACT.Square).then_inc(squared, 1)

                def to_std(n):
                    c0, w = CHUNKS[n]
                    act.wait_ge(varied, n + 1)
                    if n >= 2:
                        act.wait_ge(inverted, n - 1)
                    act.activation(std[:, n % 2, 0:w], ps[3 + n][:, 0:w], ACT.Sqrt, bias=g.eps5[:, 0:1],
                                   scale=1.0 / D).then_inc(rooted, 1)

                to_mean(0)
                to_mean(1)
                to_square(0)
                to_mean(2)
                to_square(1)
                to_square(2)
                for n in range(n_ch):
                    to_std(n)
                if gamma is not None:
                    act.wait_ge(gb_loaded, 32)
                    act.wait_ge(scaled, n_ch)
                    for k in range(KT):
                        act.activation(dst[:, k, :], dst[:, k, :], ACT.Identity, bias=gb[:, 1, k:k + 1], scale=gb[:, 0, k:k + 1])

            @block.vector
            def _(dve):
                for n, (c0, w) in enumerate(CHUNKS):
                    dve.wait_ge(meaned, n + 1)
                    dve.tensor_tensor(dst[:, :, c0:c0 + w], src[:, :, c0:c0 + w], wide(mean[:, n % 2, 0:w], KT),
                                      ALU.subtract).then_inc(centred, 1)
                for n, (c0, w) in enumerate(CHUNKS):
                    dve.wait_ge(rooted, n + 1)
                    if n >= 2:
                        dve.wait_ge(scaled, n - 1)
                    dve.reciprocal(rstd[:, n % 2, 0:w], std[:, n % 2, 0:w]).then_inc(inverted, 1)
                    dve.wait_ge(inverted, n + 1)
                    dve.wait_ge(squared, n + 1)
                    dve.tensor_tensor(dst[:, :, c0:c0 + w], dst[:, :, c0:c0 + w], wide(rstd[:, n % 2, 0:w], KT),
                                      ALU.mult).then_inc(scaled, 1)


def stage_gat_project(nc, g, W):
    g.new_stage()
    with ExitStack() as c:
        w_rows = g.sb(c, "gat_w_rows", [P, 2, P], F32)
        attn_rows = g.sb(c, "gat_attn_rows", [KT, 2, P], F32)
        attn_T = g.sb(c, "gat_attn_T", [P, 2, KT], F32)
        attn_pair = g.sb(c, "gat_attn_pair", [P, KT, 4], F32)
        rhs = g.sb(c, "gat_rhs", [P, KT, P + 4], F32)
        a1_rows = g.sb(c, "gat_a1_rows", [H, N], F32)
        cleared = g.sem("gatp_cleared")
        loaded = g.sem("gatp_loaded")
        turned = g.sem("gatp_turned")
        kept = g.sem("gatp_kept")
        folded = g.sem("gatp_folded")
        rhs_ready = g.sem("gatp_rhs_ready")
        projected = g.sem("gatp_projected")
        ft_kept = g.sem("gatp_ft_kept")
        a_kept = g.sem("gatp_a_kept")
        a_turned = g.sem("gatp_a_turned")
        row_kept = g.sem("gatp_row_kept")
        stored = g.sem("gatp_stored")
        ps = g.psum
        with nc.Block() as block:
            @block.gpsimd
            def _(pool):
                pool.memset(w_rows[:, :, :], 0.0).then_inc(cleared, 1)
                pool.memset(attn_pair[:, :, :], 0.0).then_inc(cleared, 1)

            @block.sync
            def _(sp):
                sp.wait_ge(cleared, 2)
                for n, w in enumerate((W["L0_gnn_W_fc"], W["L0_gnn_W_res"])):
                    for h in range(2):
                        sp.dma_start(w_rows[64 * h:64 * h + 64, n, 64 * h:64 * h + 64], w).then_inc(loaded, 16)
                for n, a in enumerate((W["L0_gnn_attn_l"], W["L0_gnn_attn_r"])):
                    sp.dma_start(attn_rows[:, n], a.rearrange("(p h) e -> p (h e)", h=2)).then_inc(loaded, 16)
                sp.wait_ge(row_kept, NT)
                sp.dma_start(g.a1_dram, a1_rows[:, :]).then_inc(stored, 16)
                sp.wait_ge(stored, 16)

            @block.tensor
            def _(pe):
                pe.wait_ge(loaded, 96)
                for n in range(2):
                    pe.transpose(ps[0][:, n * P:(n + 1) * P], w_rows[:, n], g.ident[:, :])
                    op = pe.transpose(ps[1][:, n * KT:(n + 1) * KT], attn_rows[:, n], g.ident[0:KT, 0:KT])
                op.then_inc(turned, 1)
                pe.wait_ge(kept, 6)
                for k in range(KT):
                    op = pe.matmul(ps[2][:, 4 * k:4 * k + 4], w_rows[:, 0], attn_pair[:, k], start=True, stop=True)
                op.then_inc(folded, 1)
                pe.wait_ge(rhs_ready, 2)
                for t in range(NT):
                    if t >= 3:
                        pe.wait_ge(ft_kept, t - 2)
                    for k in range(KT):
                        op = pe.matmul(ps[2 * (t % 3) + k // 3][0:TT, (k % 3) * (P + 4):(k % 3 + 1) * (P + 4)],
                                       g.y_T[:, k, t * TT:(t + 1) * TT], rhs[:, k], start=True, stop=True)
                    op.then_inc(projected, 1)
                for t in range(NT):
                    pe.wait_ge(a_kept, t + 1)
                    if t >= 2:
                        pe.wait_ge(row_kept, t - 1)
                    pe.transpose(ps[6 + t % 2][0:H, 0:TT], g.a_cols[:, t, 0], g.ident[0:TT, 0:TT]).then_inc(a_turned, 1)

            @block.vector
            def _(dve):
                dve.wait_ge(turned, 1)
                dve.wait_ge(cleared, 2)
                dve.tensor_copy(g.w_res[:, :], ps[0][:, P:2 * P]).then_inc(kept, 1)
                dve.tensor_copy(attn_T[:, :, :], ps[1][:, 0:2 * KT].rearrange("p (n k) -> p n k", n=2)).then_inc(kept, 1)
                dve.wait_ge(kept, 2)
                for n in range(2):
                    for h in range(2):
                        dve.tensor_copy(attn_pair[64 * h:64 * h + 64, :, 2 * n + h], attn_T[64 * h:64 * h + 64, n]).then_inc(kept, 1)
                dve.tensor_copy(rhs[:, :, 0:P], wide(ps[0][:, 0:P], KT)).then_inc(rhs_ready, 1)
                dve.wait_ge(folded, 1)
                dve.tensor_copy(rhs[:, :, P:P + 4], ps[2][:, 0:4 * KT].rearrange("p (k j) -> p k j", k=KT)).then_inc(rhs_ready, 1)
                for t in range(NT):
                    dve.wait_ge(projected, t + 1)
                    for h in range(2):
                        part = ps[2 * (t % 3) + h][0:TT, 0:3 * (P + 4)].rearrange("p (k j) -> p k j", k=3)
                        for n in range(2):
                            op = dve.tensor_copy(g.a_cols[:, t, n, 6 * h:6 * h + 6].rearrange("p (k j) -> p k j", k=3),
                                                 part[:, :, P + 2 * n:P + 2 * n + 2])
                    op.then_inc(a_kept, 1)
                for t in range(NT):
                    dve.wait_ge(a_turned, t + 1)
                    dve.tensor_copy(a1_rows[:, t * TT:(t + 1) * TT], ps[6 + t % 2][0:H, 0:TT]).then_inc(row_kept, 1)

            @block.scalar
            def _(act):
                for t in range(NT):
                    act.wait_ge(a_kept, t + 1)
                    for h in range(2):
                        part = ps[2 * (t % 3) + h][0:TT, 0:3 * (P + 4)].rearrange("p (k j) -> p k j", k=3)
                        op = act.activation(g.ft[:, t, 3 * h:3 * h + 3, :], part[:, :, 0:P], ACT.Copy)
                    op.then_inc(ft_kept, 1)


def stage_gat_max(nc, g):
    g.new_stage()
    with ExitStack() as c:
        a1_wide = g.sb(c, "a1_wide", [TT, 2, N], F32)
        masked = g.sb(c, "masked", [TT, 2, N], F32)
        a1_max = g.sb(c, "a1_max", [TT, NT, H], F32)
        e_max = g.sb(c, "e_max", [TT, NT, H], F32)
        e_sum = g.sb(c, "e_sum", [TT, NT, H], F32)
        uv = g.sb(c, "uv", [TT, NT, 2, H], F32)
        uv_rows = g.sb(c, "uv_rows", [2 * H, N], F32)
        wide_s = [g.sem(f"gatm_wide{i}") for i in range(2)]
        maxed = g.sem("gatm_maxed")
        chain = g.sem("gatm_chain")
        turned = g.sem("gatm_turned")
        row_kept = g.sem("gatm_row_kept")
        stored = g.sem("gatm_stored")
        ps = g.psum
        with nc.Block() as block:
            @block.sync
            def _(sp):
                for h in range(2):
                    sp.dma_start(a1_wide[:, h], g.a1_dram[h:h + 1, :].partition_broadcast(TT)).then_inc(wide_s[h], 16)
                with sp.Fori(1, KT) as p:
                    for h in range(2):
                        sp.wait_ge(maxed, NT * (2 * p + h - 1))
                        sp.dma_start(a1_wide[:, h], g.a1_dram[bass.ds(2 * p + h, 1), :].partition_broadcast(TT)).then_inc(wide_s[h], 16)
                sp.wait_ge(row_kept, NT)
                sp.dma_start(g.uv_dram, uv_rows[:, :]).then_inc(stored, 16)
                sp.wait_ge(stored, 16)

            @block.vector
            def _(dve):
                for h in range(H):
                    dve.wait_ge(wide_s[h % 2], 16 * (h // 2) + 16)
                    for b in range(NT):
                        if h * NT + b >= 2:
                            dve.wait_ge(maxed, h * NT + b - 1)
                        dve.tensor_tensor_reduce(masked[:, b % 2], a1_wide[:, h % 2], g.no_edge[:, b], 1.0, -BIG,
                                                 ALU.add, ALU.max, a1_max[:, b, h:h + 1]).then_inc(maxed, 1)
                a1, a2 = g.a_cols[:, :, 0], g.a_cols[:, :, 1]
                dve.wait_ge(maxed, H * NT)
                dve.tensor_tensor(e_sum[:, :, :], a2, a1_max[:, :, :], ALU.add).then_inc(chain, 1)
                dve.wait_ge(chain, 1)
                dve.scalar_tensor_tensor(out=e_max[:, :, :], in0=e_sum[:, :, :], scalar=0.2, in1=e_sum[:, :, :],
                                         op0=ALU.mult, op1=ALU.max).then_inc(chain, 1)
                dve.wait_ge(chain, 2)
                dve.tensor_tensor(uv[:, :, 0], a2, e_max[:, :, :], ALU.subtract).then_inc(chain, 1)
                dve.scalar_tensor_tensor(out=uv[:, :, 1], in0=a2, scalar=0.2, in1=e_max[:, :, :],
                                         op0=ALU.mult, op1=ALU.subtract).then_inc(chain, 1)
                dve.tensor_scalar(g.a1_fifth[:, :, :], a1, 0.2, None, ALU.mult).then_inc(chain, 1)
                for t in range(NT):
                    dve.wait_ge(turned, t + 1)
                    dve.tensor_copy(uv_rows[:, t * TT:(t + 1) * TT], ps[t % 2][0:2 * H, 0:TT]).then_inc(row_kept, 1)

            @block.tensor
            def _(pe):
                pe.wait_ge(chain, 4)
                for t in range(NT):
                    if t >= 2:
                        pe.wait_ge(row_kept, t - 1)
                    pe.transpose(ps[t % 2][0:2 * H, 0:TT], uv[:, t].rearrange("p n h -> p (n h)"),
                                 g.ident[0:TT, 0:TT]).then_inc(turned, 1)


def stage_gat_attend(nc, g):
    g.new_stage()
    with ExitStack() as c:
        u_wide = g.sb(c, "u_wide", [TT, 2, N], F32)
        v_wide = g.sb(c, "v_wide", [TT, 2, N], F32)
        ft_pair = g.sb(c, "ft_pair", [TT, NT, 192], F32)
        low = g.sb(c, "gat_low", [TT, 2, N], F32)
        high = g.sb(c, "gat_high", [TT, 2, N], F32)
        prob = g.sb(c, "gat_prob", [TT, 2, N], F32)
        den = g.sb(c, "gat_den", [P, N], F32)
        inv = g.sb(c, "gat_inv", [P, N], F32)
        agg = den
        ones_s = g.sem("gata_ones")
        uv_loaded = [g.sem(f"gata_uv{i}") for i in range(2)]
        ft_s = g.sem("gata_ft")
        low_s = g.sem("gata_low")
        high_s = g.sem("gata_high")
        exp_s = g.sem("gata_exp")
        prob_s = g.sem("gata_prob")
        used = g.sem("gata_used")
        den_s = g.sem("gata_den")
        fin = g.sem("gata_finish")
        freed = g.sem("gata_freed")
        res_s = g.sem("gata_res")
        ps = g.psum
        n2 = 2 * NT
        with nc.Block() as block:
            @block.sync
            def _(sp):
                for h in range(2):
                    for wide_t, o in ((u_wide, 0), (v_wide, H)):
                        sp.dma_start(wide_t[:, h], g.uv_dram[h + o:h + o + 1, :].partition_broadcast(TT)).then_inc(uv_loaded[h], 16)
                with sp.Fori(1, KT) as p:
                    for h in range(2):
                        sp.wait_ge(high_s, n2 * p - n2 + NT * (h + 1) + 2)
                        for wide_t, o in ((u_wide, 0), (v_wide, H)):
                            sp.dma_start(wide_t[:, h], g.uv_dram[bass.ds(p * 2 + h + o, 1), :].partition_broadcast(TT)).then_inc(uv_loaded[h], 16)

            @block.gpsimd
            def _(pool):
                pool.memset(ft_pair[:, :, 64:128], 1.0).then_inc(ones_s, 1)
                with pool.Fori(0, KT) as p:
                    pool.wait_ge(used, n2 * p + 2)
                    ftp = g.ft[:, :, bass.ds(p, 1), :].squeeze(2)
                    pool.tensor_copy(ft_pair[:, :, 0:64], ftp[:, :, 0:64]).then_inc(ft_s, 1)
                    pool.tensor_copy(ft_pair[:, :, 128:192], ftp[:, :, 64:128]).then_inc(ft_s, 1)

            @block.scalar
            def _(act):
                with act.Fori(0, KT) as p:
                    def lower(i):
                        h, j = i // NT, i % NT
                        act.wait_ge(uv_loaded[h], 32 * p + 32)
                        act.wait_ge(high_s, n2 * p + i + 1)
                        act.activation(low[:, i % 2], v_wide[:, h], ACT.Identity,
                                       bias=g.a1_fifth[:, j, bass.ds(2 * p + h, 1)]).then_inc(low_s, 1)

                    def expo(i):
                        act.wait_ge(high_s, n2 * p + i + 3)
                        act.activation(high[:, i % 2], high[:, i % 2], ACT.Exp).then_inc(exp_s, 1)

                    lower(0)
                    for i in range(n2):
                        if i + 1 < n2:
                            lower(i + 1)
                        expo(i)
                    for h in range(2):
                        act.wait_ge(used, n2 * p + NT * (h + 1) + 2)
                        act.wait_ge(fin, 3 * p + 1)
                        for n, (c0, w) in enumerate(CHUNKS):
                            op = act.activation(den[64 * h:64 * h + 64, c0:c0 + w], ps[3 * h + n][64 - 64 * h:128 - 64 * h, 0:w], ACT.Copy)
                        op.then_inc(den_s, 1)

            @block.vector
            def _(dve):
                dve.sem_inc(high_s, 2)
                dve.sem_inc(fin, 1)
                dve.sem_inc(used, 2)
                dve.sem_inc(freed, 1)
                with dve.Fori(0, KT) as p:
                    def raise_(i):
                        h, j = i // NT, i % NT
                        dve.wait_ge(uv_loaded[h], 32 * p + 32)
                        dve.wait_ge(low_s, n2 * p + i + 1)
                        if i >= 2:
                            dve.wait_ge(prob_s, n2 * p + i - 1)
                        dve.scalar_tensor_tensor(out=high[:, i % 2], in0=u_wide[:, h],
                                                 scalar=g.a_cols[:, j, 0, bass.ds(2 * p + h, 1)],
                                                 in1=low[:, i % 2], op0=ALU.add, op1=ALU.max).then_inc(high_s, 1)

                    def weigh(i):
                        j = i % NT
                        dve.wait_ge(exp_s, n2 * p + i + 1)
                        dve.wait_ge(used, n2 * p + i + 1)
                        dve.scalar_tensor_tensor(out=prob[:, i % 2], in0=high[:, i % 2], scalar=1.0, in1=g.counts_T[:, j],
                                                 op0=ALU.min, op1=ALU.mult).then_inc(prob_s, 1)

                    raise_(0)
                    for i in range(n2):
                        if i + 1 < n2:
                            raise_(i + 1)
                        weigh(i)
                    dve.wait_ge(den_s, 2 * p + 2)
                    dve.tensor_scalar(den[:, :], den[:, :], 0.5, None, ALU.max).then_inc(fin, 1)
                    dve.wait_ge(fin, 3 * p + 2)
                    dve.reciprocal(inv[:, :], den[:, :]).then_inc(fin, 1)
                    dve.wait_ge(fin, 3 * p + 3)
                    for h in range(2):
                        r = slice(64 * h, 64 * h + 64)
                        for n, (c0, w) in enumerate(CHUNKS):
                            op = dve.tensor_tensor(agg[r, c0:c0 + w], ps[3 * h + n][r, 0:w], inv[r, c0:c0 + w], ALU.mult)
                    op.then_inc(freed, 1)
                    dve.wait_ge(freed, 4 * p + 2)
                    for n, (c0, w) in enumerate(CHUNKS):
                        dve.wait_ge(res_s, 3 * p + n + 1)
                        dve.tensor_tensor(agg[:, c0:c0 + w], agg[:, c0:c0 + w], ps[6 + n % 2][:, 0:w], ALU.add).then_inc(freed, 1)
                    dve.wait_ge(freed, 4 * p + 5)
                    xp = g.x_T[:, bass.ds(p, 1), :].squeeze(1)
                    dve.scalar_tensor_tensor(out=xp, in0=agg[:, :], scalar=0.0, in1=xp, op0=ALU.max, op1=ALU.add).then_inc(fin, 1)

            @block.tensor
            def _(pe):
                with pe.Fori(0, KT) as p:
                    pe.wait_ge(freed, 4 * p + 1)
                    pe.wait_ge(ones_s, 1)
                    pe.wait_ge(ft_s, 2 * p + 2)
                    for i in range(n2):
                        h, j = i // NT, i % NT
                        pe.wait_ge(prob_s, n2 * p + i + 1)
                        for n, (c0, w) in enumerate(CHUNKS):
                            op = pe.matmul(ps[3 * h + n][:, 0:w], ft_pair[:, j, 64 * h:64 * h + 128],
                                           prob[:, i % 2, c0:c0 + w], start=(j == 0), stop=(j == NT - 1))
                        op.then_inc(used, 1)
                    for n, (c0, w) in enumerate(CHUNKS):
                        if n == 2:
                            pe.wait_ge(freed, 4 * p + 3)
                        pe.matmul(ps[6 + n % 2][:, 0:w], g.w_res[:, :], g.y_T[:, bass.ds(p, 1), c0:c0 + w].squeeze(1),
                                  start=True, stop=True).then_inc(res_s, 1)


def project_T(pe, banks, w, src):
    for k in range(KT):
        for n, (c0, wd) in enumerate(CHUNKS):
            op = pe.matmul(banks[n][:, 0:wd], w[:, k], src[:, k, c0:c0 + wd], start=(k == 0), stop=(k == KT - 1))
    return op


def stage_mix0(nc, g, w_qkv, src, o_T):
    g.new_stage()
    with ExitStack() as c:
        w = g.sb(c, "mix0_w", [P, KT, 3, P], F32)
        q = g.sb(c, "mix0_q", [P, N], F32)
        q_low = g.sb(c, "mix0_q_low", [P, N], F32)
        k = g.sb(c, "mix0_k", [TT, NT, P], F32)
        k_low = g.sb(c, "mix0_k_low", [TT, NT, P], F32)
        v1 = g.sb(c, "mix0_v1", [TT, NT, 2 * P], F32)
        kv = g.sb(c, "mix0_kv", [P, 2, P], F32)
        inv = g.sb(c, "mix0_inv", [P, N], F32)
        ones_s = g.sem("mix0_ones")
        loaded = g.sem("mix0_w_loaded")
        w_used = g.sem("mix0_w_used")
        projected = g.sem("mix0_projected")
        lows = g.sem("mix0_lows")
        exps = g.sem("mix0_exps")
        elus = g.sem("mix0_elus")
        kv_sum = g.sem("mix0_kv_sum")
        kv_s = g.sem("mix0_kv")
        outs = g.sem("mix0_outs")
        inv_s = g.sem("mix0_inv")
        done = g.sem("mix0_done")
        ps = g.psum
        with nc.Block() as block:
            @block.sync
            def _(sp):
                with sp.Fori(0, KT) as p:
                    sp.wait_ge(w_used, p + 1)
                    for n in range(3):
                        sp.dma_start(w[:, :, n], w_qkv.rearrange("(k f) (n m) -> f k n m", f=P, n=3)[:, :, n, bass.ds(p * P, P)]).then_inc(loaded, 16)

            @block.gpsimd
            def _(pool):
                pool.memset(v1[:, :, P:2 * P], 1.0).then_inc(ones_s, 1)
                pool.sem_inc(w_used, 1)
                pool.sem_inc(done, 1)

            @block.tensor
            def _(pe):
                pe.wait_ge(ones_s, 1)
                with pe.Fori(0, KT) as p:
                    pe.wait_ge(loaded, 48 * p + 48)
                    pe.wait_ge(done, p + 1)
                    project_T(pe, ps[0:3], w[:, :, 0], src).then_inc(projected, 1)
                    for t in range(NT):
                        for kk in range(KT):
                            op = pe.matmul(ps[3 + t // 2][0:TT, (t % 2) * 256:(t % 2) * 256 + 256],
                                           src[:, kk, t * TT:(t + 1) * TT], w[:, kk, 1:3, :],
                                           start=(kk == 0), stop=(kk == KT - 1))
                        if t % 2:
                            op.then_inc(projected, 1)
                    pe.wait_ge(projected, 6 * p + 6)
                    pe.sem_inc(w_used, 1)
                    pe.wait_ge(elus, 8 * p + 8)
                    for t in range(NT):
                        op = pe.matmul(ps[3][:, 0:256], k[:, t], v1[:, t], start=(t == 0), stop=(t == NT - 1))
                    op.then_inc(kv_sum, 1)
                    pe.wait_ge(kv_s, 2 * p + 2)
                    for n, (c0, wd) in enumerate(CHUNKS):
                        pe.matmul(ps[4 + n][:, 0:wd], kv[:, 1], q[:, c0:c0 + wd], start=True, stop=True)
                        pe.matmul(ps[n][:, 0:wd], kv[:, 0], q[:, c0:c0 + wd], start=True, stop=True).then_inc(outs, 1)

            @block.scalar
            def _(act):
                with act.Fori(0, KT) as p:
                    for n, (c0, wd) in enumerate(CHUNKS):
                        act.wait_ge(lows, 8 * p + n + 1)
                        act.activation(q_low[:, c0:c0 + wd], q_low[:, c0:c0 + wd], ACT.Exp).then_inc(exps, 1)
                    for b in range(5):
                        act.wait_ge(lows, 8 * p + b + 4)
                        act.activation(k_low[:, 2 * b:2 * b + 2], k_low[:, 2 * b:2 * b + 2], ACT.Exp).then_inc(exps, 1)

            @block.vector
            def _(dve):
                with dve.Fori(0, KT) as p:
                    dve.wait_ge(projected, 6 * p + 1)
                    for n, (c0, wd) in enumerate(CHUNKS):
                        dve.tensor_scalar(q_low[:, c0:c0 + wd], ps[n][:, 0:wd], 0.0, None, ALU.min).then_inc(lows, 1)
                    for n, (c0, wd) in enumerate(CHUNKS):
                        dve.wait_ge(exps, 8 * p + n + 1)
                        dve.scalar_tensor_tensor(out=q[:, c0:c0 + wd], in0=ps[n][:, 0:wd], scalar=0.0, in1=q_low[:, c0:c0 + wd],
                                                 op0=ALU.max, op1=ALU.add).then_inc(elus, 1)
                    for b in range(5):
                        dve.wait_ge(projected, 6 * p + b + 2)
                        kvb = ps[3 + b][0:TT, 0:512].rearrange("p (t n m) -> p t n m", t=2, n=2)
                        dve.tensor_scalar(k_low[:, 2 * b:2 * b + 2], kvb[:, :, 0], 0.0, None, ALU.min).then_inc(lows, 1)
                        dve.tensor_copy(v1[:, 2 * b:2 * b + 2, 0:P], kvb[:, :, 1])
                    for b in range(5):
                        kvb = ps[3 + b][0:TT, 0:512].rearrange("p (t n m) -> p t n m", t=2, n=2)
                        dve.wait_ge(exps, 8 * p + b + 4)
                        dve.scalar_tensor_tensor(out=k[:, 2 * b:2 * b + 2], in0=kvb[:, :, 0], scalar=0.0, in1=k_low[:, 2 * b:2 * b + 2],
                                                 op0=ALU.max, op1=ALU.add).then_inc(elus, 1)
                    dve.wait_ge(kv_sum, p + 1)
                    for n in range(2):
                        dve.tensor_tensor(kv[:, n], ps[3][:, n * P:(n + 1) * P], g.pair_mask[:, :], ALU.mult).then_inc(kv_s, 1)
                    for n, (c0, wd) in enumerate(CHUNKS):
                        dve.wait_ge(outs, 3 * p + n + 1)
                        dve.reciprocal(inv[:, c0:c0 + wd], ps[4 + n][:, 0:wd]).then_inc(inv_s, 1)
                        dve.wait_ge(inv_s, 3 * p + n + 1)
                        op = dve.tensor_tensor(o_T[:, bass.ds(p, 1), c0:c0 + wd].squeeze(1), ps[n][:, 0:wd], inv[:, c0:c0 + wd], ALU.mult)
                    op.then_inc(done, 1)


def stage_linear(nc, g, name, w, bias, src, kt, mt, func, dst=None, add_to=None, scale=1.0, times=None, expert=None):
    g.new_stage()
    with ExitStack() as c:
        w_sb = g.sb(c, f"{name}_w", [P, 2, kt, P], F32)
        bias_sb = g.sb(c, f"{name}_bias", [P, mt], F32)
        bias_x = g.sb(c, f"{name}_bias_x", [P, mt], F32)
        t_sb = g.sb(c, f"{name}_t", [P, 2, N], F32) if add_to is not None else None
        loaded = [g.sem(f"{name}_w_loaded{i}") for i in range(2)]
        bias_loaded = g.sem(f"{name}_bias_loaded")
        bias_s = g.sem(f"{name}_bias_scaled")
        summed = g.sem(f"{name}_summed")
        taken = g.sem(f"{name}_taken")
        added = g.sem(f"{name}_added")
        ps = g.psum
        with nc.Block() as block:
            @block.sync
            def _(sp):
                if expert is None:
                    w_of, b_of = w, bias
                else:
                    e = sp.value_load(expert, min_val=0, max_val=w.shape[0] - 1)
                    w_of = w[bass.ds(e, 1)].squeeze(0)
                    b_of = bias[bass.ds(e, 1)].squeeze(0)
                w_v = w_of.rearrange("(k f) m -> f k m", f=P)
                sp.dma_start(w_sb[:, 0], w_v[:, :, 0:P]).then_inc(loaded[0], 16)
                sp.dma_start(bias_sb[:, :], b_of.rearrange("(m f) -> f m", f=P), allow_slow_non_contiguous=True).then_inc(bias_loaded, 16)
                for m in range(1, mt):
                    if m >= 2:
                        sp.wait_ge(summed, m - 1)
                    sp.dma_start(w_sb[:, m % 2], w_v[:, :, m * P:(m + 1) * P]).then_inc(loaded[m % 2], 16)

            @block.tensor
            def _(pe):
                for m in range(mt):
                    pe.wait_ge(loaded[m % 2], 16 * (m // 2) + 16)
                    if m >= 2:
                        pe.wait_ge(taken, m - 1)
                    for k in range(kt):
                        for n, (c0, wd) in enumerate(CHUNKS):
                            op = pe.matmul(ps[3 * (m % 2) + n][:, 0:wd], w_sb[:, m % 2, k], src[:, k, c0:c0 + wd],
                                           start=(k == 0), stop=(k == kt - 1))
                    op.then_inc(summed, 1)

            @block.scalar
            def _(act):
                act.wait_ge(bias_loaded, 16)
                act.activation(bias_x[:, :], bias_sb[:, :], ACT.Copy, scale=scale).then_inc(bias_s, 1)
                act.wait_ge(bias_s, 1)
                for m in range(mt):
                    act.wait_ge(summed, m + 1)
                    if add_to is not None and m >= 2:
                        act.wait_ge(added, m - 1)
                    for n, (c0, wd) in enumerate(CHUNKS):
                        out = dst[:, m, c0:c0 + wd] if add_to is None else t_sb[:, m % 2, c0:c0 + wd]
                        op = act.activation(out, ps[3 * (m % 2) + n][:, 0:wd], func, bias=bias_x[:, m:m + 1], scale=scale)
                    op.then_inc(taken, 1)

            if add_to is not None:
                @block.vector
                def _(dve):
                    for m in range(mt):
                        dve.wait_ge(taken, m + 1)
                        if times is None:
                            op = dve.tensor_tensor(add_to[:, m], add_to[:, m], t_sb[:, m % 2], ALU.add)
                        else:
                            op = dve.scalar_tensor_tensor(out=add_to[:, m], in0=t_sb[:, m % 2], scalar=times,
                                                          in1=add_to[:, m], op0=ALU.mult, op1=ALU.add)
                        op.then_inc(added, 1)


def stage_choose(nc, g, w_gate, src, weight, expert):
    g.new_stage()
    NE = 3
    with ExitStack() as c:
        wg = g.sb(c, "choose_wg", [P, KT, NE], F32)
        mean = g.sb(c, "choose_mean", [P, KT], F32)
        mean_wide = g.sb(c, "choose_mean_wide", [P, KT, P], F32)
        s = g.sb(c, "choose_s", [P, 16], F32)
        loaded = g.sem("choose_loaded")
        mean_s = g.sem("choose_mean_s")
        logits = g.sem("choose_logits")
        top_s = g.sem("choose_top")
        exp_s = g.sem("choose_exp")
        chain = g.sem("choose_chain")
        ps = g.psum
        top, exps, total, inv, prob, is1, is2, nof = (slice(0, 1), slice(1, 4), slice(4, 5), slice(5, 6),
                                                      slice(6, 9), slice(9, 10), slice(10, 11), slice(11, 12))
        with nc.Block() as block:
            @block.sync
            def _(sp):
                for e in range(NE):
                    sp.dma_start(wg[:, :, e], w_gate[e].rearrange("(k f) -> f k", f=P), allow_slow_non_contiguous=True).then_inc(loaded, 16)

            @block.vector
            def _(dve):
                n = [0]

                def step(op):
                    n[0] += 1
                    op.then_inc(chain, 1)
                    dve.wait_ge(chain, n[0])

                step(dve.tensor_reduce(mean[:, :], src[:, :, :], AX_X, ALU.add))
                dve.tensor_scalar(mean_wide[:, :, :], mean[:, :].unsqueeze(2).broadcast_to([P, KT, P]), 1.0 / N, None,
                                  ALU.mult).then_inc(mean_s, 1)
                dve.wait_ge(logits, 1)
                dve.tensor_reduce(s[:, top], ps[0][:, 0:NE], AX_X, ALU.max, negate=True).then_inc(top_s, 1)
                dve.wait_ge(exp_s, 1)
                step(dve.reciprocal(s[:, inv], s[:, total]))
                step(dve.tensor_scalar(s[:, prob], s[:, exps], s[:, inv], None, ALU.mult))
                step(dve.tensor_reduce(weight, s[:, prob], AX_X, ALU.max))
                step(dve.tensor_tensor(s[:, nof], s[:, 6:7], s[:, 7:8], ALU.max))
                step(dve.tensor_tensor(s[:, is2], s[:, 8:9], s[:, nof], ALU.is_gt))
                step(dve.tensor_tensor(s[:, is1], s[:, 7:8], s[:, 6:7], ALU.is_gt))
                step(dve.scalar_tensor_tensor(out=s[:, nof], in0=s[:, is2], scalar=2.0, in1=s[:, is1], op0=ALU.mult, op1=ALU.max))
                dve.tensor_copy(expert, s[:, nof])

            @block.scalar
            def _(act):
                act.wait_ge(top_s, 1)
                act.activation(s[:, exps], ps[0][:, 0:NE], ACT.Exp, bias=s[:, top], accum_out=s[:, total]).then_inc(exp_s, 1)

            @block.tensor
            def _(pe):
                pe.wait_ge(loaded, 16 * NE)
                pe.wait_ge(mean_s, 1)
                for k in range(KT):
                    op = pe.matmul(ps[0][:, 0:NE], mean_wide[:, k], wg[:, k], start=(k == 0), stop=(k == KT - 1))
                op.then_inc(logits, 1)


def stage_gcn(nc, g, w_gcn, bias, src, x_T):
    g.new_stage()
    HALF = D // 2
    with ExitStack() as c:
        w = g.sb(c, "gcn_w", [P, 2, KT, HALF], F32)
        bias_sb = g.sb(c, "gcn_bias", [P, KT], F32)
        root = g.sb(c, "gcn_root", [P, N], F32)
        norm = g.sb(c, "gcn_norm", [P, N], F32)
        norm_cols = g.sb(c, "gcn_norm_cols", [TT, NT], F32)
        h = g.sb(c, "gcn_h", [TT, NT, D], F32)
        t_sb = g.sb(c, "gcn_t", [P, 2, N], F32)
        loaded = g.sem("gcn_loaded")
        looped = g.sem("gcn_looped")
        degrees = g.sem("gcn_degrees")
        rooted = g.sem("gcn_rooted")
        normed = g.sem("gcn_normed")
        cols = g.sem("gcn_cols")
        cols_s = g.sem("gcn_cols_kept")
        projected = g.sem("gcn_projected")
        h_s = g.sem("gcn_h_s")
        summed = g.sem("gcn_summed")
        scaled = g.sem("gcn_scaled")
        added = g.sem("gcn_added")
        ps = g.psum
        with nc.Block() as block:
            @block.sync
            def _(sp):
                for i in range(2):
                    sp.dma_start(w[:, i], w_gcn.rearrange("(k f) m -> f k m", f=P)[:, :, i * HALF:(i + 1) * HALF]).then_inc(loaded, 16)
                sp.dma_start(bias_sb[:, :], bias.rearrange("(m f) -> f m", f=P), allow_slow_non_contiguous=True).then_inc(loaded, 16)

            @block.tensor
            def _(pe):
                pe.wait_ge(looped, NT)
                for n, (c0, wd) in enumerate(CHUNKS):
                    for j in range(NT):
                        op = pe.matmul(ps[n][:, 0:wd], g.ones[0:TT, :], g.counts_T[:, j, c0:c0 + wd], start=(j == 0), stop=(j == NT - 1))
                    op.then_inc(degrees, 1)
                pe.wait_ge(normed, 3)
                for t in range(NT):
                    op = pe.matmul(ps[3][0:TT, t:t + 1], norm[0:1, t * TT:(t + 1) * TT], g.ones[0:1, 0:1], start=True, stop=True)
                op.then_inc(cols, 1)
                pe.wait_ge(loaded, 48)
                for i in range(2 * NT):
                    t = i % NT
                    if i >= 4:
                        pe.wait_ge(h_s, i - 3)
                    for k in range(KT):
                        op = pe.matmul(ps[4 + i % 4][0:TT, 0:HALF], src[:, k, t * TT:(t + 1) * TT], w[:, i // NT, k],
                                       start=(k == 0), stop=(k == KT - 1))
                    op.then_inc(projected, 1)
                pe.wait_ge(h_s, 2 * NT)
                for m in range(KT):
                    if m >= 2:
                        pe.wait_ge(scaled, m - 1)
                    for j in range(NT):
                        for n, (c0, wd) in enumerate(CHUNKS):
                            op = pe.matmul(ps[3 * (m % 2) + n][:, 0:wd], h[:, j, m * P:(m + 1) * P], g.counts_T[:, j, c0:c0 + wd],
                                           start=(j == 0), stop=(j == NT - 1))
                    op.then_inc(summed, 1)

            @block.scalar
            def _(act):
                for n, (c0, wd) in enumerate(CHUNKS):
                    act.wait_ge(degrees, n + 1)
                    act.activation(root[:, c0:c0 + wd], ps[n][:, 0:wd], ACT.Sqrt).then_inc(rooted, 1)
                act.wait_ge(cols_s, 1)
                for i in range(2 * NT):
                    t, half = i % NT, i // NT
                    act.wait_ge(projected, i + 1)
                    act.activation(h[:, t, half * HALF:(half + 1) * HALF], ps[4 + i % 4][0:TT, 0:HALF], ACT.Copy,
                                   scale=norm_cols[:, t:t + 1]).then_inc(h_s, 1)

            @block.vector
            def _(dve):
                for j in range(NT):
                    own = g.counts_T[:, j, j * TT:(j + 1) * TT]
                    dve.tensor_tensor(own, own, g.ident[0:TT, 0:TT], ALU.add).then_inc(looped, 1)
                for n, (c0, wd) in enumerate(CHUNKS):
                    dve.wait_ge(rooted, n + 1)
                    dve.reciprocal(norm[:, c0:c0 + wd], root[:, c0:c0 + wd]).then_inc(normed, 1)
                dve.wait_ge(cols, 1)
                dve.tensor_copy(norm_cols[:, :], ps[3][0:TT, 0:NT]).then_inc(cols_s, 1)
                dve.wait_ge(normed, 3)
                dve.wait_ge(loaded, 48)
                for m in range(KT):
                    dve.wait_ge(summed, m + 1)
                    if m >= 2:
                        dve.wait_ge(added, m - 1)
                    for n, (c0, wd) in enumerate(CHUNKS):
                        op = dve.tensor_tensor(t_sb[:, m % 2, c0:c0 + wd], ps[3 * (m % 2) + n][:, 0:wd], norm[:, c0:c0 + wd], ALU.mult)
                    op.then_inc(scaled, 1)
                    dve.wait_ge(scaled, m + 1)
                    dve.scalar_tensor_tensor(out=x_T[:, m], in0=t_sb[:, m % 2], scalar=bias_sb[:, m:m + 1], in1=x_T[:, m],
                                             op0=ALU.add, op1=ALU.add).then_inc(added, 1)


def stage_mix1(nc, g, w_qkv, b_qkv, src, o_T):
    g.new_stage()
    EPS = 1e-6
    with ExitStack() as c:
        w = g.sb(c, "mix1_w", [P, KT, 3, P], F32)
        bias_q = g.sb(c, "mix1_bias_q", [P, KT], F32)
        bias_kv = g.sb(c, "mix1_bias_kv", [TT, 2, P], F32)
        eps = g.sb(c, "mix1_eps", [P, 1], F32)
        q = g.sb(c, "mix1_q", [P, N], F32)
        q_eps = g.sb(c, "mix1_q_eps", [P, N], F32)
        q_sums = g.sb(c, "mix1_q_sums", [P, 3], F32)
        q_sum = g.sb(c, "mix1_q_sum", [P, 2], F32)
        col_wide = g.sb(c, "mix1_col_wide", [P, 2, TT], F32)
        row = g.sb(c, "mix1_row", [TT, 2, P], F32)
        k = g.sb(c, "mix1_k", [TT, NT, P], F32)
        k_eps = g.sb(c, "mix1_k_eps", [TT, NT, P], F32)
        prod = g.sb(c, "mix1_prod", [TT, NT, P], F32)
        v = g.sb(c, "mix1_v", [TT, NT, P], F32)
        outgoing = g.sb(c, "mix1_outgoing", [TT, 4, NT, 2], F32)
        outgoing_wide = g.sb(c, "mix1_outgoing_wide", [TT, NT, P], F32)
        comp = g.sb(c, "mix1_comp", [TT, 3, NT, 2], F32)
        ends = g.sb(c, "mix1_ends", [P, 3, P], F32)
        factor = g.sb(c, "mix1_factor", [P, 3], F32)
        sink_den = g.sb(c, "mix1_sink_den", [P, N], F32)
        sink = g.sb(c, "mix1_sink", [P, N], F32)
        alloc = g.sb(c, "mix1_alloc", [P, N], F32)
        junk = g.sb(c, "mix1_junk", [P, N], F32)
        eps_s = g.sem("mix1_eps_s")
        bias_loaded = g.sem("mix1_bias_loaded")
        loaded = g.sem("mix1_w_loaded")
        kv_bias_loaded = g.sem("mix1_kv_bias_loaded")
        kv_bias_free = g.sem("mix1_kv_bias_free")
        w_used = g.sem("mix1_w_used")
        projected = g.sem("mix1_projected")
        pe_s = g.sem("mix1_products")
        act_s = g.sem("mix1_acts")
        dve_s = g.sem("mix1_dve")
        ps = g.psum
        STEPS = 44
        at = {}
        with nc.Block() as block:
            @block.vector
            def _(dve):
                dve.sem_inc(dve_s, 1)
                with dve.Fori(0, KT) as p:
                    n = [0]

                    def step(op, name):
                        op.then_inc(dve_s, 1)
                        n[0] += 1
                        at[name] = n[0] + 1

                    def after(name):
                        dve.wait_ge(dve_s, STEPS * p + at[name])

                    dve.wait_ge(kv_bias_loaded, 32 * p + 32)
                    for b in range(5):
                        dve.wait_ge(projected, 6 * p + b + 2)
                        kvb = ps[3 + b][0:TT, 0:512].rearrange("p (t n m) -> p t n m", t=2, n=2)
                        for i, to in ((0, k), (1, v)):
                            step(dve.tensor_tensor(to[:, 2 * b:2 * b + 2], kvb[:, :, i], wide(bias_kv[:, i], 2), ALU.add), f"kv{b}")
                    dve.wait_ge(act_s, 10 * p + 3)
                    step(dve.tensor_scalar(q_eps[:, :], q[:, :], EPS, None, ALU.add), "q_eps")
                    step(dve.tensor_reduce(q_sum[:, 0:1], q_sums[:, :], AX_X, ALU.add), "q_sum")
                    after("q_sum")
                    step(dve.tensor_scalar(col_wide[:, 0], g.ones[:, 0:TT], q_sum[:, 0:1], None, ALU.mult), "q_sum_wide")
                    dve.wait_ge(act_s, 10 * p + 8)
                    step(dve.tensor_scalar(k_eps[:, :, :], k[:, :, :], EPS, None, ALU.add), "k_eps")
                    dve.wait_ge(pe_s, 12 * p + 1)
                    step(dve.scalar_tensor_tensor(out=ends[:, 0], in0=ps[3][:, 0:P], scalar=EPS, in1=g.pair_mask[:, :],
                                                  op0=ALU.add, op1=ALU.mult), "k_sum")
                    dve.wait_ge(pe_s, 12 * p + 2)
                    step(dve.tensor_scalar(row[:, 0], ps[4][0:TT, 0:P], EPS, None, ALU.add), "q_row")
                    after("q_row")
                    step(dve.tensor_tensor(prod[:, :, :], k_eps[:, :, :], wide(row[:, 0], NT), ALU.mult), "prod0")
                    after("prod0")
                    step(dve.tensor_reduce(outgoing[:, 0], prod[:, :, :].rearrange("p t (h d) -> p t h d", h=2), AX_X, ALU.add), "out0")
                    after("out0")
                    step(dve.tensor_scalar(outgoing[:, 1], outgoing[:, 0], EPS, None, ALU.add), "out1")
                    after("out1")
                    step(dve.reciprocal(outgoing[:, 2], outgoing[:, 1]), "out2")
                    after("out2")
                    for hh in range(2):
                        step(dve.tensor_copy(outgoing_wide[:, :, 64 * hh:64 * hh + 64],
                                             outgoing[:, 2, :, hh:hh + 1].broadcast_to([TT, NT, 64])), "outgoing")
                    for i, (c0, wd) in enumerate(CHUNKS):
                        dve.wait_ge(pe_s, 12 * p + 3 + i)
                        step(dve.tensor_scalar(sink_den[:, c0:c0 + wd], ps[5 + i][:, 0:wd], EPS, None, ALU.add), "sink_den")
                    after("sink_den")
                    step(dve.reciprocal(sink[:, :], sink_den[:, :]), "sink")
                    after("sink")
                    step(dve.tensor_tensor_reduce(junk[:, :], q[:, :], sink[:, :], 1.0, 0.0, ALU.mult, ALU.add, q_sum[:, 1:2]), "q_sink")
                    after("q_sink")
                    step(dve.tensor_scalar(col_wide[:, 1], g.ones[:, 0:TT], q_sum[:, 1:2], None, ALU.mult), "q_sink_wide")
                    dve.wait_ge(pe_s, 12 * p + 6)
                    step(dve.scalar_tensor_tensor(out=ends[:, 1], in0=ps[3][:, 0:P], scalar=EPS, in1=g.pair_mask[:, :],
                                                  op0=ALU.add, op1=ALU.mult), "k_out_sum")
                    dve.wait_ge(pe_s, 12 * p + 7)
                    step(dve.tensor_scalar(row[:, 1], ps[4][0:TT, 0:P], EPS, None, ALU.add), "q_sink_row")
                    after("q_sink_row")
                    step(dve.tensor_tensor(prod[:, :, :], k_eps[:, :, :], wide(row[:, 1], NT), ALU.mult), "prod1")
                    after("prod1")
                    step(dve.tensor_reduce(comp[:, 0], prod[:, :, :].rearrange("p t (h d) -> p t h d", h=2), AX_X, ALU.add), "comp0")
                    after("comp0")
                    step(dve.tensor_scalar(comp[:, 1], comp[:, 0], EPS, 1.0, ALU.add, ALU.min), "comp1")
                    after("comp1")
                    step(dve.tensor_scalar(comp[:, 2], comp[:, 1], -1.0, None, ALU.max), "comp2")
                    dve.wait_ge(act_s, 10 * p + 9)
                    for hh in range(2):
                        vh = v[:, :, 64 * hh:64 * hh + 64]
                        step(dve.tensor_tensor(vh, vh, outgoing[:, 3, :, hh:hh + 1].broadcast_to([TT, NT, 64]), ALU.mult), "v")
                    dve.wait_ge(pe_s, 12 * p + 8)
                    step(dve.reciprocal(factor[:, 0:2], ps[3][:, 0:2]), "inv")
                    after("inv")
                    for hh in range(2):
                        r = slice(64 * hh, 64 * hh + 64)
                        step(dve.tensor_scalar(factor[r, 2:3], factor[r, hh:hh + 1], float(N), None, ALU.mult), "factor")
                    after("factor")
                    dve.wait_ge(pe_s, 12 * p + 9)
                    step(dve.scalar_tensor_tensor(out=ends[:, 2], in0=ps[4][:, 0:P], scalar=factor[:, 2:3], in1=g.pair_mask[:, :],
                                                  op0=ALU.mult, op1=ALU.mult), "kv")
                    dve.wait_ge(act_s, 10 * p + 10)
                    step(dve.tensor_tensor(junk[:, :], sink[:, :], alloc[:, :], ALU.mult), "gain")
                    after("gain")
                    for i, (c0, wd) in enumerate(CHUNKS):
                        dve.wait_ge(pe_s, 12 * p + 10 + i)
                        step(dve.tensor_tensor(o_T[:, bass.ds(p, 1), c0:c0 + wd].squeeze(1), ps[i][:, 0:wd], junk[:, c0:c0 + wd], ALU.mult), "o")
                    assert n[0] == STEPS, n[0]

            @block.sync
            def _(sp):
                sp.dma_start(bias_q[:, :], b_qkv[0:D].rearrange("(m f) -> f m", f=P), allow_slow_non_contiguous=True).then_inc(bias_loaded, 16)
                with sp.Fori(0, KT) as p:
                    sp.wait_ge(w_used, p + 1)
                    for n in range(3):
                        sp.dma_start(w[:, :, n], w_qkv.rearrange("(k f) (n m) -> f k n m", f=P, n=3)[:, :, n, bass.ds(p * P, P)]).then_inc(loaded, 16)
                    sp.wait_ge(kv_bias_free, p + 1)
                    for n in range(2):
                        sp.dma_start(bias_kv[:, n], b_qkv.rearrange("(n m) -> n m", n=3)[n + 1:n + 2, bass.ds(p * P, P)].partition_broadcast(TT)).then_inc(kv_bias_loaded, 16)

            @block.gpsimd
            def _(pool):
                pool.memset(eps[:, :], EPS).then_inc(eps_s, 1)
                pool.sem_inc(w_used, 1)
                pool.sem_inc(kv_bias_free, 1)
                with pool.Fori(0, KT) as p:
                    pool.wait_ge(dve_s, STEPS * p + at["kv4"])
                    pool.sem_inc(kv_bias_free, 1)

            @block.tensor
            def _(pe):
                pe.wait_ge(eps_s, 1)
                with pe.Fori(0, KT) as p:
                    pe.wait_ge(loaded, 48 * p + 48)
                    pe.wait_ge(dve_s, STEPS * p + 1)
                    project_T(pe, ps[0:3], w[:, :, 0], src).then_inc(projected, 1)
                    for t in range(NT):
                        for kk in range(KT):
                            op = pe.matmul(ps[3 + t // 2][0:TT, (t % 2) * 256:(t % 2) * 256 + 256],
                                           src[:, kk, t * TT:(t + 1) * TT], w[:, kk, 1:3, :],
                                           start=(kk == 0), stop=(kk == KT - 1))
                        if t % 2:
                            op.then_inc(projected, 1)
                    pe.wait_ge(projected, 6 * p + 6)
                    pe.sem_inc(w_used, 1)

                    def made(name):
                        pe.wait_ge(dve_s, STEPS * p + at[name])

                    def by_tokens(bank_, rhs, width):
                        for t in range(NT):
                            op = pe.matmul(ps[bank_][:, 0:width], k[:, t], rhs(t), start=(t == 0), stop=(t == NT - 1))
                        op.then_inc(pe_s, 1)

                    pe.wait_ge(act_s, 10 * p + 8)
                    by_tokens(3, lambda t: g.ones[0:TT, :], P)
                    made("q_sum_wide")
                    pe.matmul(ps[4][0:TT, 0:P], col_wide[:, 0], g.ident[:, :], start=True, stop=True).then_inc(pe_s, 1)
                    made("k_sum")
                    for i, (c0, wd) in enumerate(CHUNKS):
                        pe.matmul(ps[5 + i][:, 0:wd], ends[:, 0], q_eps[:, c0:c0 + wd], start=True, stop=True).then_inc(pe_s, 1)
                    made("outgoing")
                    by_tokens(3, lambda t: outgoing_wide[:, t], P)
                    made("q_sink_wide")
                    pe.matmul(ps[4][0:TT, 0:P], col_wide[:, 1], g.ident[:, :], start=True, stop=True).then_inc(pe_s, 1)
                    made("k_out_sum")
                    for i, (c0, wd) in enumerate(CHUNKS):
                        op = pe.matmul(ps[5 + i][:, 0:wd], ends[:, 1], q_eps[:, c0:c0 + wd], start=True, stop=True)
                    pe.wait_ge(act_s, 10 * p + 9)
                    for t in range(NT):
                        op = pe.matmul(ps[3][:, 0:2], g.ones[0:TT, :], outgoing[:, 3, t], start=(t == 0), stop=(t == NT - 1))
                    op.then_inc(pe_s, 1)
                    made("v")
                    by_tokens(4, lambda t: v[:, t], P)
                    made("kv")
                    for i, (c0, wd) in enumerate(CHUNKS):
                        pe.matmul(ps[i][:, 0:wd], ends[:, 2], q[:, c0:c0 + wd], start=True, stop=True).then_inc(pe_s, 1)

            @block.scalar
            def _(act):
                act.wait_ge(bias_loaded, 16)
                act.wait_ge(eps_s, 1)
                with act.Fori(0, KT) as p:
                    act.wait_ge(projected, 6 * p + 1)
                    for i, (c0, wd) in enumerate(CHUNKS):
                        act.activation(q[:, c0:c0 + wd], ps[i][:, 0:wd], ACT.Sigmoid, bias=bias_q[:, bass.ds(p, 1)],
                                       accum_out=q_sums[:, i:i + 1]).then_inc(act_s, 1)
                    for b in range(5):
                        act.wait_ge(dve_s, STEPS * p + at[f"kv{b}"])
                        act.activation(k[:, 2 * b:2 * b + 2], k[:, 2 * b:2 * b + 2], ACT.Sigmoid).then_inc(act_s, 1)
                    act.wait_ge(dve_s, STEPS * p + at["comp2"])
                    act.activation(outgoing[:, 3], comp[:, 2], ACT.Exp).then_inc(act_s, 1)
                    act.wait_ge(pe_s, 12 * p + 8)
                    for i, (c0, wd) in enumerate(CHUNKS):
                        op = act.activation(alloc[:, c0:c0 + wd], ps[5 + i][:, 0:wd], ACT.Sigmoid, bias=eps[:, 0:1])
                    op.then_inc(act_s, 1)


def stage_attention(nc, g, w_qkv, b_qkv, src, o_T):
    g.new_stage()
    G = 2
    GW = G * TT
    STEPS = 2 * NT
    GROUPS = STEPS // G
    with ExitStack() as c:
        w = g.sb(c, "att_w", [P, KT, 3, P], F32)
        bias_qk = g.sb(c, "att_bias_qk", [P, 2, KT], F32)
        bias_q8 = g.sb(c, "att_bias_q8", [P, KT], F32)
        bias_v = g.sb(c, "att_bias_v", [TT, 2, 64], F32)
        q = g.sb(c, "att_q", [P, N], F32)
        k = g.sb(c, "att_k", [P, N], F32)
        v = g.sb(c, "att_v", [TT, NT, 3, 64], F32)
        top = g.sb(c, "att_top", [TT, 2, 3], F32)
        neg_top = g.sb(c, "att_neg_top", [TT, 2], F32)
        prob = g.sb(c, "att_prob", [TT, 2, N], F32)
        prob_T = g.sb(c, "att_prob_T", [TT, 2, NT, GW], F32)
        inv = g.sb(c, "att_inv", [P, 2, GW], F32)
        ones_s = g.sem("att_ones")
        bias_loaded = g.sem("att_bias_loaded")
        bias_s = g.sem("att_bias_scaled")
        loaded = g.sem("att_w_loaded")
        v_bias_loaded = g.sem("att_v_bias_loaded")
        w_used = g.sem("att_w_used")
        projected = g.sem("att_projected")
        v_s = g.sem("att_v_s")
        qk_s = g.sem("att_qk_s")
        scored = g.sem("att_scored")
        tops = g.sem("att_tops")
        maxed = g.sem("att_maxed")
        exped = g.sem("att_exped")
        turned = g.sem("att_turned")
        kept = g.sem("att_kept")
        summed = g.sem("att_summed")
        inverted = g.sem("att_inverted")
        done = g.sem("att_done")
        ps = g.psum
        THIRDS = ((0, 4), (4, 8), (8, 10))
        with nc.Block() as block:
            @block.sync
            def _(sp):
                sp.dma_start(bias_qk[:, :, :], b_qkv[0:2 * D].rearrange("(n m f) -> f n m", f=P, n=2), allow_slow_non_contiguous=True).then_inc(bias_loaded, 16)
                with sp.Fori(0, KT) as p:
                    sp.wait_ge(w_used, p + 1)
                    for n in range(3):
                        sp.dma_start(w[:, :, n], w_qkv.rearrange("(k f) (n m) -> f k n m", f=P, n=3)[:, :, n, bass.ds(p * P, P)]).then_inc(loaded, 16)
                    sp.wait_ge(done, GROUPS * p + 1)
                    sp.dma_start(bias_v[:, :, :].rearrange("p h e -> p (h e)"),
                                 b_qkv.rearrange("(n m) -> n m", n=3)[2:3, bass.ds(p * P, P)].partition_broadcast(TT)).then_inc(v_bias_loaded, 16)

            @block.gpsimd
            def _(pool):
                pool.memset(v[:, :, 1], 1.0).then_inc(ones_s, 1)
                pool.sem_inc(w_used, 1)
                pool.sem_inc(done, 1)

            @block.tensor
            def _(pe):
                pe.wait_ge(ones_s, 1)
                with pe.Fori(0, KT) as p:
                    pe.wait_ge(loaded, 48 * p + 48)
                    pe.wait_ge(done, GROUPS * p + 1)
                    for b, (t0, t1) in enumerate(THIRDS):
                        for t in range(t0, t1):
                            for kk in range(KT):
                                op = pe.matmul(ps[b][0:TT, (t - t0) * P:(t - t0 + 1) * P], src[:, kk, t * TT:(t + 1) * TT],
                                               w[:, kk, 2], start=(kk == 0), stop=(kk == KT - 1))
                        op.then_inc(projected, 1)
                    project_T(pe, ps[3:6], w[:, :, 0], src).then_inc(projected, 1)
                    pe.wait_ge(v_s, 3 * p + 1)
                    project_T(pe, (ps[6], ps[7], ps[0]), w[:, :, 1], src).then_inc(projected, 1)
                    pe.wait_ge(projected, 5 * p + 5)
                    pe.sem_inc(w_used, 1)

                    def scores(i):
                        h, t = i // NT, i % NT
                        if i:
                            pe.wait_ge(exped, STEPS * p + i)
                        else:
                            pe.wait_ge(qk_s, 2 * p + 2)
                            pe.wait_ge(v_s, 3 * p + 3)
                        for n, (c0, wd) in enumerate(CHUNKS):
                            op = pe.matmul(ps[n][0:TT, 0:wd], q[64 * h:64 * h + 64, t * TT:(t + 1) * TT],
                                           k[64 * h:64 * h + 64, c0:c0 + wd], start=True, stop=True)
                        op.then_inc(scored, 1)

                    def turn(i):
                        pe.wait_ge(exped, STEPS * p + i + 1)
                        if i:
                            pe.wait_ge(kept, STEPS * p + i)
                        for b, (j0, j1) in enumerate(THIRDS):
                            for j in range(j0, j1):
                                op = pe.transpose(ps[3 + b][0:TT, (j - j0) * TT:(j - j0 + 1) * TT], prob[:, i % 2, j * TT:(j + 1) * TT],
                                                  g.ident[0:TT, 0:TT])
                        op.then_inc(turned, 1)

                    def weigh(gr, half):
                        h = gr * G // NT
                        if half == 0:
                            pe.wait_ge(kept, STEPS * p + G * gr + G)
                            if gr >= 2:
                                pe.wait_ge(done, GROUPS * p + gr)
                        for j in range(5 * half, 5 * half + 5):
                            op = pe.matmul(ps[6 + gr % 2][:, 0:GW], v[:, j, h:h + 2], prob_T[:, gr % 2, j],
                                           start=(j == 0), stop=(j == NT - 1))
                        if half:
                            op.then_inc(summed, 1)

                    for i in range(STEPS):
                        scores(i)
                        if i >= 1:
                            turn(i - 1)
                        if i >= 3:
                            weigh((i - 3) // 2, (i - 3) % 2)
                    turn(STEPS - 1)
                    for i in range(STEPS, STEPS + 3):
                        weigh((i - 3) // 2, (i - 3) % 2)

            @block.scalar
            def _(act):
                act.wait_ge(bias_loaded, 16)
                act.activation(bias_q8[:, :], bias_qk[:, 0], ACT.Copy, scale=0.125).then_inc(bias_s, 1)
                act.wait_ge(bias_s, 1)
                with act.Fori(0, KT) as p:
                    act.wait_ge(projected, 5 * p + 4)
                    for n, (c0, wd) in enumerate(CHUNKS):
                        op = act.activation(q[:, c0:c0 + wd], ps[3 + n][:, 0:wd], ACT.Identity, bias=bias_q8[:, bass.ds(p, 1)], scale=0.125)
                    op.then_inc(qk_s, 1)
                    act.wait_ge(projected, 5 * p + 5)
                    for bk, (c0, wd) in zip((6, 7, 0), CHUNKS):
                        op = act.activation(k[:, c0:c0 + wd], ps[bk][:, 0:wd], ACT.Identity, bias=bias_qk[:, 1, bass.ds(p, 1)])
                    op.then_inc(qk_s, 1)

                    def expo(i):
                        act.wait_ge(maxed, STEPS * p + i + 1)
                        if i >= 2:
                            act.wait_ge(turned, STEPS * p + i - 1)
                        for n, (c0, wd) in enumerate(CHUNKS):
                            op = act.activation(prob[:, i % 2, c0:c0 + wd], ps[n][0:TT, 0:wd], ACT.Exp, bias=neg_top[:, i % 2:i % 2 + 1])
                        op.then_inc(exped, 1)

                    def keep(i):
                        gr = i // G
                        act.wait_ge(turned, STEPS * p + i + 1)
                        if gr >= 2 and i % G == 0:
                            act.wait_ge(summed, GROUPS * p + gr - 1)
                        for b, (j0, j1) in enumerate(THIRDS):
                            op = act.activation(prob_T[:, gr % 2, j0:j1, (i % G) * TT:(i % G + 1) * TT],
                                                ps[3 + b][0:TT, 0:(j1 - j0) * TT].rearrange("p (j n) -> p j n", j=j1 - j0), ACT.Copy)
                        op.then_inc(kept, 1)

                    for i in range(STEPS):
                        if i >= 1:
                            keep(i - 1) if i >= 2 else None
                        expo(i)
                        if i == 1:
                            keep(0)
                    keep(STEPS - 1)

            @block.vector
            def _(dve):
                with dve.Fori(0, KT) as p:
                    dve.wait_ge(v_bias_loaded, 16 * p + 16)
                    for b, (t0, t1) in enumerate(THIRDS):
                        dve.wait_ge(projected, 5 * p + b + 1)
                        dve.tensor_tensor(v[:, t0:t1, 0:3:2], ps[b][0:TT, 0:(t1 - t0) * P].rearrange("p (t h e) -> p t h e", h=2, e=64),
                                          bias_v[:, :, :].unsqueeze(1).broadcast_to([TT, t1 - t0, 2, 64]), ALU.add).then_inc(v_s, 1)

                    def most(i):
                        dve.wait_ge(scored, STEPS * p + i + 1)
                        for n, (c0, wd) in enumerate(CHUNKS):
                            dve.tensor_reduce(top[:, i % 2, n:n + 1], ps[n][0:TT, 0:wd], AX_X, ALU.max).then_inc(tops, 1)
                        dve.wait_ge(tops, 3 * (STEPS * p + i + 1))
                        dve.tensor_reduce(neg_top[:, i % 2:i % 2 + 1], top[:, i % 2], AX_X, ALU.max, negate=True).then_inc(maxed, 1)

                    def finish(gr):
                        h, t0 = gr * G // NT, (gr * G % NT) * TT
                        mine, other = slice(64 * h, 64 * h + 64), slice(64 - 64 * h, 128 - 64 * h)
                        dve.wait_ge(summed, GROUPS * p + gr + 1)
                        dve.reciprocal(inv[mine, gr % 2], ps[6 + gr % 2][other, 0:GW]).then_inc(inverted, 1)
                        dve.wait_ge(inverted, GROUPS * p + gr + 1)
                        dve.tensor_tensor(o_T[mine, bass.ds(p, 1), t0:t0 + GW].squeeze(1), ps[6 + gr % 2][mine, 0:GW], inv[mine, gr % 2],
                                          ALU.mult).then_inc(done, 1)

                    for i in range(STEPS):
                        most(i)
                        if i >= 5 and i % 2:
                            finish((i - 5) // 2)
                    finish(GROUPS - 2)
                    finish(GROUPS - 1)


def stage_gates(nc, g, gate_w, b2, src, z_T):
    g.new_stage()
    NE = 8
    with ExitStack() as c:
        wg = g.sb(c, "gates_w", [P, KT, NE], F32)
        b2_sb = g.sb(c, "gates_b2", [NE, D], F32)
        logit = g.sb(c, "gates_logit", [TT, NT, NE], F32)
        above = g.sb(c, "gates_above", [TT, NT, NE, NE], F32)
        equal = g.sb(c, "gates_equal", [TT, NT, NE, NE], F32)
        lower = g.sb(c, "gates_lower", [TT, NE, NE], F32)
        rank = g.sb(c, "gates_rank", [TT, NT, NE], F32)
        top = g.sb(c, "gates_top", [TT, NT, 3], F32)
        diff = g.sb(c, "gates_diff", [TT, NT, NE], F32)
        gate = g.sb(c, "gates_gate", [TT, NT, NE], F32)
        rows = g.sb(c, "gates_rows", [NE, N], F32)
        loaded = g.sem("gates_loaded")
        lower_s = g.sem("gates_lower_s")
        logits = g.sem("gates_logits")
        chain = g.sem("gates_chain")
        diffed = g.sem("gates_diffed")
        exped = g.sem("gates_exped")
        gated = g.sem("gates_gated")
        turned = g.sem("gates_turned")
        row_kept = g.sem("gates_row_kept")
        stored = g.sem("gates_stored")
        biased = g.sem("gates_biased")
        added = g.sem("gates_added")
        ps = g.psum
        with nc.Block() as block:
            @block.sync
            def _(sp):
                sp.dma_start(wg[:, :, :], gate_w.rearrange("(k f) e -> f k e", f=P)).then_inc(loaded, 16)
                sp.dma_start(b2_sb[:, :], b2).then_inc(loaded, 16)
                sp.wait_ge(row_kept, NT)
                sp.dma_start(g.gates_dram, rows[:, :]).then_inc(stored, 16)
                sp.wait_ge(stored, 16)

            @block.gpsimd
            def _(pool):
                pool.memset(lower[:, :, :], 1.0).then_inc(lower_s, 1)
                pool.wait_ge(lower_s, 1)
                pool.affine_select(out=lower[:, :, :], in_=lower[:, :, :], compare_op=ALU.is_gt, fill=0.0,
                                   base=0, pattern=[[1, NE], [-1, NE]], channel_multiplier=0).then_inc(lower_s, 1)

            @block.tensor
            def _(pe):
                pe.wait_ge(loaded, 32)
                for t in range(NT):
                    for k in range(KT):
                        op = pe.matmul(ps[0][0:TT, t * NE:(t + 1) * NE], src[:, k, t * TT:(t + 1) * TT], wg[:, k],
                                       start=(k == 0), stop=(k == KT - 1))
                op.then_inc(logits, 1)
                pe.wait_ge(gated, 1)
                for t in range(NT):
                    if t >= 2:
                        pe.wait_ge(row_kept, t - 1)
                    pe.transpose(ps[t % 2][0:NE, 0:TT], gate[:, t], g.ident[0:TT, 0:TT]).then_inc(turned, 1)
                pe.wait_ge(row_kept, NT)
                for m in range(KT):
                    if m >= 2:
                        pe.wait_ge(added, m - 1)
                    for n, (c0, wd) in enumerate(CHUNKS):
                        op = pe.matmul(ps[2 + 3 * (m % 2) + n][:, 0:wd], b2_sb[:, m * P:(m + 1) * P], rows[:, c0:c0 + wd], start=True, stop=True)
                    op.then_inc(biased, 1)

            @block.scalar
            def _(act):
                act.wait_ge(diffed, 1)
                act.activation(diff[:, :, :], diff[:, :, :], ACT.Exp).then_inc(exped, 1)

            @block.vector
            def _(dve):
                n = [0]

                def step(op):
                    n[0] += 1
                    op.then_inc(chain, 1)
                    dve.wait_ge(chain, n[0])

                dve.wait_ge(logits, 1)
                step(dve.tensor_copy(logit[:, :, :], ps[0][0:TT, 0:NT * NE].rearrange("p (t e) -> p t e", e=NE)))
                step(dve.tensor_reduce(top[:, :, 0:1], logit[:, :, :], AX_X, ALU.max))
                dve.tensor_tensor(diff[:, :, :], logit[:, :, :], top[:, :, 0:1].broadcast_to([TT, NT, NE]), ALU.subtract).then_inc(diffed, 1)
                of_f = logit[:, :, :].unsqueeze(2).broadcast_to([TT, NT, NE, NE])
                of_e = logit[:, :, :].unsqueeze(3).broadcast_to([TT, NT, NE, NE])
                step(dve.tensor_tensor(above[:, :, :, :], of_f, of_e, ALU.is_gt))
                step(dve.tensor_tensor(equal[:, :, :, :], of_f, of_e, ALU.is_equal))
                dve.wait_ge(lower_s, 2)
                step(dve.tensor_tensor(equal[:, :, :, :], equal[:, :, :, :], lower[:, :, :].unsqueeze(1).broadcast_to([TT, NT, NE, NE]), ALU.mult))
                step(dve.tensor_tensor(above[:, :, :, :], above[:, :, :, :], equal[:, :, :, :], ALU.add))
                step(dve.tensor_reduce(rank[:, :, :], above[:, :, :, :], AX_X, ALU.add))
                dve.wait_ge(exped, 1)
                step(dve.scalar_tensor_tensor(out=diff[:, :, :], in0=rank[:, :, :], scalar=2.0, in1=diff[:, :, :], op0=ALU.is_lt, op1=ALU.mult))
                step(dve.tensor_reduce(top[:, :, 1:2], diff[:, :, :], AX_X, ALU.add))
                step(dve.reciprocal(top[:, :, 2:3], top[:, :, 1:2]))
                dve.tensor_tensor(gate[:, :, :], diff[:, :, :], top[:, :, 2:3].broadcast_to([TT, NT, NE]), ALU.mult).then_inc(gated, 1)
                for t in range(NT):
                    dve.wait_ge(turned, t + 1)
                    dve.tensor_copy(rows[:, t * TT:(t + 1) * TT], ps[t % 2][0:NE, 0:TT]).then_inc(row_kept, 1)
                for m in range(KT):
                    dve.wait_ge(biased, m + 1)
                    for i, (c0, wd) in enumerate(CHUNKS):
                        op = dve.tensor_tensor(z_T[:, m, c0:c0 + wd], z_T[:, m, c0:c0 + wd], ps[2 + 3 * (m % 2) + i][:, 0:wd], ALU.add)
                    op.then_inc(added, 1)


def stage_experts(nc, g, w1, b1, w2, src, z_T):
    g.new_stage()
    NE, HT = 8, 3
    with ExitStack() as c:
        w1_sb = g.sb(c, "exp_w1", [P, KT, HT * P], F32)
        w2_sb = g.sb(c, "exp_w2", [P, HT, D], F32)
        b1_sb = g.sb(c, "exp_b1", [P, NE, HT], F32)
        gate = g.sb(c, "exp_gate", [P, N], F32)
        hid = g.sb(c, "exp_hid", [P, HT, N], F32)
        gated_sb = g.sb(c, "exp_gated", [P, HT, N], F32)
        b1_loaded = g.sem("exp_b1_loaded")
        w1_loaded = g.sem("exp_w1_loaded")
        w2_loaded = g.sem("exp_w2_loaded")
        gate_loaded = g.sem("exp_gate_loaded")
        up = g.sem("exp_up")
        made = g.sem("exp_made")
        gated = g.sem("exp_gated_s")
        down = g.sem("exp_down")
        drained = g.sem("exp_drained")
        ps = g.psum
        w1_v = w1.rearrange("e (k f) m -> f e k m", f=P)
        w2_v = w2.rearrange("e (k f) m -> f e k m", f=P)
        with nc.Block() as block:
            @block.sync
            def _(sp):
                sp.dma_start(w1_sb[:, :, :], w1_v[:, 0]).then_inc(w1_loaded, 16)
                sp.dma_start(b1_sb[:, :, :], b1.rearrange("e (m f) -> f e m", f=P), allow_slow_non_contiguous=True).then_inc(b1_loaded, 16)
                sp.dma_start(gate[:, :], g.gates_dram[0:1, :].partition_broadcast(P)).then_inc(gate_loaded, 16)
                sp.dma_start(w2_sb[:, :, :], w2_v[:, 0]).then_inc(w2_loaded, 16)
                with sp.Fori(1, NE) as e:
                    sp.wait_ge(up, HT * e)
                    sp.dma_start(w1_sb[:, :, :], w1_v[:, bass.ds(e, 1)].squeeze(1)).then_inc(w1_loaded, 16)
                    sp.wait_ge(gated, HT * e)
                    sp.dma_start(gate[:, :], g.gates_dram[bass.ds(e, 1), :].partition_broadcast(P)).then_inc(gate_loaded, 16)
                    sp.wait_ge(down, KT * e + 1)
                    sp.dma_start(w2_sb[:, :, :], w2_v[:, bass.ds(e, 1)].squeeze(1)).then_inc(w2_loaded, 16)

            @block.gpsimd
            def _(pool):
                pool.sem_inc(down, 1)
                pool.sem_inc(drained, 2)

            @block.tensor
            def _(pe):
                with pe.Fori(0, NE) as e:
                    pe.wait_ge(w1_loaded, 16 * e + 16)
                    for m in range(HT):
                        b = 3 * (m % 2)
                        if m == 0:
                            pe.wait_ge(drained, KT * e + 2)
                        if m == 2:
                            pe.wait_ge(made, HT * e + 1)
                        for k in range(KT):
                            for n, (c0, wd) in enumerate(CHUNKS):
                                op = pe.matmul(ps[b + n][:, 0:wd], w1_sb[:, k, m * P:(m + 1) * P], src[:, k, c0:c0 + wd],
                                               start=(k == 0), stop=(k == KT - 1))
                        op.then_inc(up, 1)
                    pe.wait_ge(w2_loaded, 16 * e + 16)
                    for m in range(KT):
                        b = 3 * ((HT + m) % 2)
                        if m < 2:
                            pe.wait_ge(gated, HT * e + HT)
                        else:
                            pe.wait_ge(drained, KT * e + m + 1)
                        for k in range(HT):
                            for n, (c0, wd) in enumerate(CHUNKS):
                                op = pe.matmul(ps[b + n][:, 0:wd], w2_sb[:, k, m * P:(m + 1) * P], gated_sb[:, k, c0:c0 + wd],
                                               start=(k == 0), stop=(k == HT - 1))
                        op.then_inc(down, 1)

            @block.scalar
            def _(act):
                act.wait_ge(b1_loaded, 16)
                with act.Fori(0, NE) as e:
                    for m in range(HT):
                        act.wait_ge(up, HT * e + m + 1)
                        for n, (c0, wd) in enumerate(CHUNKS):
                            op = act.activation(hid[:, m, c0:c0 + wd], ps[3 * (m % 2) + n][:, 0:wd], ACT.Gelu,
                                                bias=b1_sb[:, bass.ds(e, 1), m:m + 1].squeeze(1))
                        op.then_inc(made, 1)

            @block.vector
            def _(dve):
                with dve.Fori(0, NE) as e:
                    dve.wait_ge(gate_loaded, 16 * e + 16)
                    for m in range(HT):
                        dve.wait_ge(made, HT * e + m + 1)
                        dve.wait_ge(down, KT * e + 1)
                        dve.tensor_tensor(gated_sb[:, m], hid[:, m], gate[:, :], ALU.mult).then_inc(gated, 1)
                    for m in range(KT):
                        dve.wait_ge(down, KT * e + m + 2)
                        dve.wait_ge(drained, KT * e + m + 2)
                        for n, (c0, wd) in enumerate(CHUNKS):
                            op = dve.tensor_tensor(z_T[:, m, c0:c0 + wd], z_T[:, m, c0:c0 + wd],
                                                   ps[3 * ((HT + m) % 2) + n][:, 0:wd], ALU.add)
                        op.then_inc(drained, 1)


class Ground:

    def __init__(self, nc, ctx):
        self.nc = nc
        self.stage_sems, self.cleared_sems = [], []
        self.psum = [ctx.enter_context(nc.psum_tensor(f"bank{i}", [P, 512], F32)) for i in range(8)]
        self.ident = self.sb(ctx, "ident", [P, P], F32)
        self.ones = self.sb(ctx, "ones", [P, P], F32)
        self.pair_mask = self.sb(ctx, "pair_mask", [P, P], F32)
        self.eps5 = self.sb(ctx, "eps5", [P, 1], F32)
        self.no_edge = None

    def sb(self, ctx, name, shape, dt):
        return ctx.enter_context(self.nc.sbuf_tensor(name, shape, dt))

    def sem(self, name):
        s = self.nc.alloc_semaphore(name)
        self.stage_sems.append(s)
        return s

    def new_stage(self):
        for s in self.cleared_sems:
            self.nc.release_semaphore(s)
        for s in self.stage_sems:
            self.nc.gpsimd.sem_clear(s)
        self.cleared_sems, self.stage_sems = self.stage_sems, []


def program(nc, x, src, dst, W, out, until=None):
    with ExitStack() as ctx:
        g = Ground(nc, ctx)
        stage_constants(nc, g)
        g.x_T = g.sb(ctx, "x_T", [P, KT, N], F32)
        g.y_T = g.sb(ctx, "y_T", [P, KT, N], F32)
        counts_memory, gat_memory, no_edge_memory = (ctx.enter_context(ExitStack()) for _ in range(3))
        g.counts_T = g.sb(counts_memory, "counts_T", [TT, NT, N], F32)
        g.ft = g.sb(gat_memory, "ft", [TT, NT, KT, P], F32)
        g.a_cols = g.sb(gat_memory, "a_cols", [TT, NT, 2, H], F32)
        g.a1_fifth = g.sb(gat_memory, "a1_fifth", [TT, NT, H], F32)
        g.w_res = g.sb(gat_memory, "w_res", [P, P], F32)
        g.no_edge = g.sb(no_edge_memory, "no_edge", [TT, NT, N], BF16)
        stage_adjacency(nc, g, src, dst)
        stage_load(nc, g, x)
        stage_norm(nc, g, "ln0", g.x_T, g.y_T)
        if until == "ln0":
            g.x_T = g.y_T
            return stage_store(nc, g, out)
        g.a1_dram = nc.dram_tensor("a1_rows_dram", (H, N), F32).ap()
        g.uv_dram = nc.dram_tensor("uv_rows_dram", (2 * H, N), F32).ap()
        stage_gat_project(nc, g, W)
        stage_gat_max(nc, g)
        no_edge_memory.close()
        stage_gat_attend(nc, g)
        gat_memory.close()
        if until == "gat":
            return stage_store(nc, g, out)
        with ExitStack() as c:
            o_T = g.sb(c, "o_T", [P, KT, N], F32)
            stage_mix0(nc, g, W["L0_mix_w_qkv"], g.y_T, o_T)
            stage_linear(nc, g, "mix0_proj", W["L0_mix_w_proj"], W["L0_mix_b_proj"], o_T, KT, KT, ACT.Identity, add_to=g.x_T)
        if until == "mix0":
            return stage_store(nc, g, out)
        stage_norm(nc, g, "ln1", g.x_T, g.y_T)
        with ExitStack() as c:
            weight = g.sb(c, "ffn0_weight", [P, 1], F32)
            expert = g.sb(c, "ffn0_expert", [P, 1], I32)
            hid_T = g.sb(c, "ffn0_hid_T", [P, 3, N], F32)
            stage_choose(nc, g, W["L0_ffn_Wg"], g.y_T, weight[:, :], expert[:, :])
            stage_linear(nc, g, "ffn0_up", W["L0_ffn_W1"], W["L0_ffn_b1"], g.y_T, KT, 3, ACT.Gelu, dst=hid_T, expert=expert[0:1, 0:1])
            stage_linear(nc, g, "ffn0_down", W["L0_ffn_W2"], W["L0_ffn_b2"], hid_T, 3, KT, ACT.Identity, add_to=g.x_T,
                         times=weight[:, 0:1], expert=expert[0:1, 0:1])
        if until == "ffn0":
            return stage_store(nc, g, out)
        stage_norm(nc, g, "ln2", g.x_T, g.y_T)
        stage_gcn(nc, g, W["L1_gnn_W"], W["L1_gnn_b"], g.y_T, g.x_T)
        if until == "gcn":
            return stage_store(nc, g, out)
        counts_memory.close()
        with ExitStack() as c:
            o_T = g.sb(c, "o_T1", [P, KT, N], F32)
            stage_mix1(nc, g, W["L1_mix_W_qkv"], W["L1_mix_b_qkv"], g.y_T, o_T)
            stage_linear(nc, g, "mix1_proj", W["L1_mix_W_proj"], W["L1_mix_b_proj"], o_T, KT, KT, ACT.Sigmoid, add_to=g.x_T, scale=2.0)
        if until == "mix1":
            return stage_store(nc, g, out)
        g.z_T = g.sb(ctx, "z_T", [P, KT, N], F32)
        stage_norm(nc, g, "ln3", g.x_T, g.z_T)
        stage_norm(nc, g, "ln4", g.z_T, g.y_T, W["L1_ffn_ln1_g"], W["L1_ffn_ln1_b"])
        with ExitStack() as c:
            o_T = g.sb(c, "o_T2", [P, KT, N], F32)
            stage_attention(nc, g, W["L1_ffn_qkv_w"], W["L1_ffn_qkv_b"], g.y_T, o_T)
            stage_linear(nc, g, "att_proj", W["L1_ffn_proj_w"], W["L1_ffn_proj_b"], o_T, KT, KT, ACT.Identity, add_to=g.z_T)
        stage_norm(nc, g, "ln5", g.z_T, g.y_T, W["L1_ffn_ln2_g"], W["L1_ffn_ln2_b"])
        g.gates_dram = nc.dram_tensor("gates_dram", (8, N), F32).ap()
        stage_gates(nc, g, W["L1_ffn_gate_w"], W["L1_ffn_b2"], g.y_T, g.z_T)
        stage_experts(nc, g, W["L1_ffn_w1"], W["L1_ffn_b1"], W["L1_ffn_w2"], g.y_T, g.z_T)
        stage_store(nc, g, out, add=g.z_T)


_INS = ['x', 'src', 'dst', 'L0_gnn_W_fc', 'L0_gnn_attn_l', 'L0_gnn_attn_r', 'L0_gnn_W_res', 'L0_mix_w_qkv', 'L0_mix_w_proj', 'L0_mix_b_proj', 'L0_ffn_Wg', 'L0_ffn_W1', 'L0_ffn_b1', 'L0_ffn_W2', 'L0_ffn_b2', 'L1_gnn_W', 'L1_gnn_b', 'L1_mix_W_qkv', 'L1_mix_b_qkv', 'L1_mix_W_proj', 'L1_mix_b_proj', 'L1_ffn_ln1_g', 'L1_ffn_ln1_b', 'L1_ffn_qkv_w', 'L1_ffn_qkv_b', 'L1_ffn_proj_w', 'L1_ffn_proj_b', 'L1_ffn_ln2_g', 'L1_ffn_ln2_b', 'L1_ffn_gate_w', 'L1_ffn_w1', 'L1_ffn_b1', 'L1_ffn_w2', 'L1_ffn_b2']


def kernel(**inputs):
    import numpy as _np
    import concourse.bacc as _bacc
    from concourse import mybir as _mybir
    from concourse.bass_utils import run_bass_kernel_spmd as _run

    nc = _bacc.Bacc("TRN2", target_bir_lowering=False, num_devices=1)
    arrays, W = {}, {}
    for name in _INS:
        a = _np.ascontiguousarray(inputs[name])
        arrays[f"in_{name}_dram"] = a
        W[name] = nc.dram_tensor(f"in_{name}_dram", a.shape, _mybir.dt.from_np(a.dtype), kind="ExternalInput").ap()
    out = nc.dram_tensor("out_0_dram", (N, D), F32, kind="ExternalOutput").ap()
    program(nc, W["x"], W["src"], W["dst"], W, out)
    r = _run(nc, [arrays], core_ids=[0])
    return r.results[0]["out_0_dram"]
```

```python
from contextlib import ExitStack

import concourse.bass as bass
from concourse import mybir

F32 = mybir.dt.float32
F16 = mybir.dt.float16
F32R = mybir.dt.float32r
BF16 = mybir.dt.bfloat16
I32 = mybir.dt.int32
ALU = mybir.AluOpType
ACT = mybir.ActivationFunctionType
AX_X = mybir.AxisListType.X

P = 128
N = 1250
D = 768
KT = D // P
TT = 125
NT = N // TT
H = 12
E = 41250
EG = 3
ES = E // (TT * EG)
CHUNKS = ((0, 418), (418, 416), (834, 416))
CW = 418
BIG = 3.0e38
LN_EPS = 1e-5


def bank(banks, i):
    return banks[i]


def wide(ap, n):
    return ap.unsqueeze(1).broadcast_to([ap.shape[0], n, ap.shape[1]])


def stage_constants(nc, g):
    g.new_stage()
    with nc.Block() as block:
        filled = g.sem("const_filled")
        done = g.sem("const_done")

        @block.gpsimd
        def _(pool):
            pool.memset(g.ident[:, :], 0.0).then_inc(filled, 1)
            pool.memset(g.ones[:, :], 1.0).then_inc(filled, 1)
            pool.memset(g.pair_mask[:, :], 0.0).then_inc(filled, 1)
            pool.memset(g.eps5[:, :], LN_EPS).then_inc(filled, 1)
            pool.wait_ge(filled, 4)
            pool.affine_select(out=g.ident[:, :], in_=g.ident[:, :], compare_op=ALU.not_equal, fill=1.0,
                               base=0, pattern=[[-1, P]], channel_multiplier=1).then_inc(done, 1)

        @block.vector
        def _(dve):
            dve.wait_ge(filled, 4)
            dve.memset(g.pair_mask[0:64, 0:64], 1.0).then_inc(done, 1)
            dve.memset(g.pair_mask[64:128, 64:128], 1.0).then_inc(done, 1)


def stage_adjacency(nc, g, src, dst):
    g.new_stage()
    with ExitStack() as c:
        edge_rows = g.sb(c, "edge_rows", [ES, 2, EG, TT], I32)
        edge_f = g.sb(c, "edge_f", [ES, 2, EG, TT], F32)
        edge_cols = g.sb(c, "edge_cols", [TT, 2, EG, ES], F32)
        node_ids = g.sb(c, "node_ids", [TT, N], I32)
        node_ids16 = g.sb(c, "node_ids16", [TT, N], F16)
        tile_range = g.sb(c, "tile_range", [ES, 2], F32)
        range_rows = g.sb(c, "range_rows", [NT, 2, ES], F32)
        tile_ids = g.sb(c, "tile_ids", [NT, 2, ES], I32)
        tile_idf = g.sb(c, "tile_idf", [NT, 2, ES], F32)
        block_lo_i = g.sb(c, "block_lo_i", [NT, 2], I32)
        block_lo = g.sb(c, "block_lo", [NT, 2], F32)
        touches = g.sb(c, "touches", [NT, ES], F32)
        first_last = g.sb(c, "first_last", [NT, 6], F32)
        before = g.sb(c, "before", [NT, NT], F32)
        loop_f = g.sb(c, "loop_f", [NT, 3], F32)
        loop_i = g.sb(c, "loop_i", [NT, 3], I32)
        loop_row = g.sb(c, "loop_row", [1, NT * 3], I32)
        zeros = g.sb(c, "zeros", [TT, TT], BF16)
        SLOTS = 2
        hot_dst = g.sb(c, "hot_dst", [TT, SLOTS, EG, TT], BF16)
        hot_src = g.sb(c, "hot_src", [TT, SLOTS, EG, N], BF16)
        staged = g.sb(c, "staged", [TT, N], F32)
        no_edge_row = node_ids[:, 0:N // 2].bitcast(BF16)

        loaded = g.sem("adj_loaded")
        made = g.sem("adj_ids_made")
        floats = g.sem("adj_floats")
        turned = g.sem("adj_turned")
        vec = g.sem("adj_vec")
        cnt = g.sem("adj_cumulative")
        ranged = g.sem("adj_ranges_stored")
        hots = g.sem("adj_onehots")
        used = g.sem("adj_onehots_used")
        counted = g.sem("adj_counted")
        staged_s = g.sem("adj_staged")
        turned_t = g.sem("adj_counts_turned")
        kept = g.sem("adj_kept")
        masked_s = g.sem("adj_masked")
        mask_kept = g.sem("adj_mask_kept")
        mask_turn = g.sem("adj_mask_turn")
        ps = g.psum

        with nc.Block() as block:
            @block.sync
            def _(sp):
                for n, e in ((0, src), (1, dst)):
                    sp.dma_start(edge_rows[:, n], e.rearrange("(r g e) -> r g e", g=EG, e=TT)).then_inc(loaded, 16)
                sp.wait_ge(vec, 12)
                sp.dma_start(loop_row[0:1, :], loop_i[:, :]).then_inc(ranged, 16)

            @block.gpsimd
            def _(pool):
                pool.iota(node_ids[:, :], pattern=[[1, N]], base=0, channel_multiplier=0).then_inc(made, 1)
                pool.iota(tile_ids[:, 0], pattern=[[1, ES]], base=1, channel_multiplier=0).then_inc(made, 1)
                pool.iota(tile_ids[:, 1], pattern=[[-1, ES]], base=ES, channel_multiplier=0).then_inc(made, 1)
                pool.iota(block_lo_i[:, 0:1], pattern=[[0, 1]], base=0, channel_multiplier=TT).then_inc(made, 1)
                pool.iota(block_lo_i[:, 1:2], pattern=[[0, 1]], base=TT, channel_multiplier=TT).then_inc(made, 1)
                pool.memset(before[:, :], 1.0).then_inc(made, 1)
                pool.memset(zeros[:, :], 0.0).then_inc(made, 1)
                pool.wait_ge(made, 7)
                pool.affine_select(out=before[:, :], in_=before[:, :], compare_op=ALU.is_gt, fill=0.0,
                                   base=0, pattern=[[1, NT]], channel_multiplier=-1).then_inc(made, 1)
                pool.sem_inc(masked_s, 1)
                with pool.Fori(0, NT) as b:
                    pool.wait_ge(staged_s, b + 1)
                    pool.sem_inc(mask_turn, 1)
                    pool.tensor_scalar(no_edge_row, staged[:, :], 0.5, -BIG, ALU.is_lt, ALU.mult).then_inc(masked_s, 1)
                    pool.wait_ge(masked_s, b + 2)
                    pool.tensor_copy(g.no_edge[:, bass.ds(b, 1)].squeeze(1), no_edge_row).then_inc(mask_kept, 1)
                    pool.wait_ge(mask_kept, b + 1)

            @block.vector
            def _(dve):
                dve.wait_ge(loaded, 32)
                dve.tensor_copy(edge_f[:, :, :, :], edge_rows[:, :, :, :]).then_inc(floats, 1)
                dve.wait_ge(floats, 1)
                dve.tensor_reduce(tile_range[:, 0:1], edge_f[:, 1].rearrange("r g e -> r (g e)"), AX_X, ALU.min).then_inc(floats, 1)
                dve.tensor_reduce(tile_range[:, 1:2], edge_f[:, 1].rearrange("r g e -> r (g e)"), AX_X, ALU.max).then_inc(floats, 1)
                dve.wait_ge(made, 8)
                dve.tensor_copy(node_ids16[:, :], node_ids[:, :]).then_inc(vec, 1)
                dve.tensor_copy(tile_idf[:, :, :], tile_ids[:, :, :]).then_inc(vec, 1)
                dve.tensor_copy(block_lo[:, :], block_lo_i[:, :]).then_inc(vec, 1)
                dve.wait_ge(turned, 1)
                dve.tensor_copy(edge_cols[:, 0], ps[0][0:TT, 0:ES * EG].rearrange("p (g r) -> p g r", g=EG)).then_inc(vec, 1)
                dve.tensor_copy(edge_cols[:, 1], ps[1][0:TT, 0:ES * EG].rearrange("p (g r) -> p g r", g=EG)).then_inc(vec, 1)
                dve.wait_ge(turned, 2)
                dve.tensor_copy(range_rows[:, 0], ps[2][0:NT, 0:ES]).then_inc(vec, 1)
                dve.tensor_copy(range_rows[:, 1], ps[3][0:NT, 0:ES]).then_inc(vec, 1)
                dve.wait_ge(vec, 7)
                dve.tensor_scalar(touches[:, :], range_rows[:, 0], block_lo[:, 1:2], None, ALU.is_lt).then_inc(vec, 1)
                dve.wait_ge(vec, 8)
                dve.scalar_tensor_tensor(out=touches[:, :], in0=range_rows[:, 1], scalar=block_lo[:, 0:1],
                                         in1=touches[:, :], op0=ALU.is_ge, op1=ALU.mult).then_inc(vec, 1)
                dve.wait_ge(vec, 9)
                dve.tensor_tensor(range_rows[:, :, :], tile_idf[:, :, :], wide(touches[:, :], 2), ALU.mult).then_inc(vec, 1)
                dve.wait_ge(vec, 10)
                dve.tensor_reduce(first_last[:, 0:2], range_rows[:, :, :], AX_X, ALU.max).then_inc(vec, 1)
                dve.wait_ge(vec, 11)
                dve.tensor_scalar(first_last[:, 2:3], first_last[:, 1:2], -1.0, float(ES), ALU.mult, ALU.add).then_inc(cnt, 1)
                dve.wait_ge(cnt, 1)
                dve.tensor_scalar(first_last[:, 3:4], first_last[:, 2:3], float(ES - 1), None, ALU.min).then_inc(cnt, 1)
                dve.wait_ge(cnt, 2)
                dve.tensor_tensor(first_last[:, 4:5], first_last[:, 0:1], first_last[:, 3:4], ALU.subtract).then_inc(cnt, 1)
                dve.wait_ge(cnt, 3)
                dve.tensor_scalar(first_last[:, 5:6], first_last[:, 4:5], 1.0, None, ALU.max).then_inc(cnt, 1)
                dve.wait_ge(turned, 3)
                dve.tensor_copy(loop_f[:, 0:1], ps[4][0:NT, 0:1]).then_inc(cnt, 1)
                dve.wait_ge(cnt, 5)
                dve.tensor_tensor(loop_f[:, 1:2], loop_f[:, 0:1], first_last[:, 5:6], ALU.add).then_inc(cnt, 1)
                dve.tensor_tensor(loop_f[:, 2:3], first_last[:, 3:4], loop_f[:, 0:1], ALU.subtract).then_inc(cnt, 1)
                dve.wait_ge(cnt, 7)
                dve.tensor_copy(loop_i[:, :], loop_f[:, :]).then_inc(vec, 1)
                dve.wait_ge(ranged, 16)
                dve.sem_inc(used, SLOTS)
                with dve.Fori(0, NT) as b:
                    lo = dve.value_load(loop_row[0:1, bass.ds(b * 3, 1)], min_val=0, max_val=ES * NT - 1)
                    hi = dve.value_load(loop_row[0:1, bass.ds(b * 3 + 1, 1)], min_val=1, max_val=ES * NT)
                    shift = dve.value_load(loop_row[0:1, bass.ds(b * 3 + 2, 1)], min_val=-ES * NT, max_val=ES)
                    with dve.Fori(lo, hi) as i:
                        t = nc.s_assert_within(dve.snap(i + shift), 0, ES - 1)
                        slot = dve.snap(i % SLOTS)
                        dve.wait_ge(used, i + 1)
                        for e in range(EG):
                            dve.tensor_scalar(hot_dst[:, bass.ds(slot, 1), e].squeeze(1), node_ids16[:, bass.ds(b * TT, TT)],
                                              edge_cols[:, 1, e, bass.ds(t, 1)], None, ALU.is_equal)
                            op = dve.tensor_scalar(hot_src[:, bass.ds(slot, 1), e].squeeze(1), node_ids16[:, :],
                                                   edge_cols[:, 0, e, bass.ds(t, 1)], None, ALU.is_equal)
                        op.then_inc(hots, 1)

            @block.scalar
            def _(act):
                act.sem_inc(kept, 1)
                with act.Fori(0, NT) as b:
                    act.wait_ge(counted, b + 1)
                    act.wait_ge(masked_s, b + 1)
                    for n, (c0, w) in enumerate(CHUNKS):
                        op = act.activation(staged[:, c0:c0 + w], ps[n][0:TT, 0:w], ACT.Copy)
                    op.then_inc(staged_s, 1)
                    act.wait_ge(turned_t, b + 1)
                    for j0, j1 in ((0, 4), (4, 8), (8, 10)):
                        op = act.activation(g.counts_T[:, j0:j1, bass.ds(b * TT, TT)],
                                            ps[4 + j0 // 4][0:TT, 0:(j1 - j0) * TT].rearrange("p (j d) -> p j d", j=j1 - j0), ACT.Copy)
                    op.then_inc(kept, 1)

            @block.tensor
            def _(pe):
                pe.wait_ge(floats, 1)
                for n in range(2):
                    for k in range(EG):
                        op = pe.transpose(ps[n][0:TT, k * ES:(k + 1) * ES], edge_f[:, n, k], g.ident[0:ES, 0:ES])
                op.then_inc(turned, 1)
                pe.wait_ge(floats, 3)
                for n in range(2):
                    op = pe.matmul(ps[2 + n][0:NT, 0:ES], tile_range[:, n:n + 1].broadcast_to([ES, NT]), g.ident[0:ES, 0:ES],
                                   start=True, stop=True)
                op.then_inc(turned, 1)
                pe.wait_ge(cnt, 4)
                pe.matmul(ps[4][0:NT, 0:1], before[:, :], first_last[:, 5:6], start=True, stop=True).then_inc(turned, 1)
                pe.wait_ge(vec, 12)
                pe.wait_ge(ranged, 16)
                with pe.Fori(0, NT) as b:
                    lo = pe.value_load(loop_row[0:1, bass.ds(b * 3, 1)], min_val=0, max_val=ES * NT - 1)
                    hi = pe.value_load(loop_row[0:1, bass.ds(b * 3 + 1, 1)], min_val=1, max_val=ES * NT)
                    pe.wait_ge(made, 8)
                    for n, (c0, w) in enumerate(CHUNKS):
                        pe.matmul(ps[n][0:TT, 0:w], zeros[:, :], node_ids16[:, 0:w], start=True, stop=False,
                                  skip_group_check=True)
                    with pe.Fori(lo, hi) as i:
                        slot = pe.snap(i % SLOTS)
                        pe.wait_ge(hots, i + 1)
                        for e in range(EG):
                            for n, (c0, w) in enumerate(CHUNKS):
                                op = pe.matmul(ps[n][0:TT, 0:w], hot_dst[:, bass.ds(slot, 1), e].squeeze(1),
                                               hot_src[:, bass.ds(slot, 1), e, c0:c0 + w].squeeze(1),
                                               start=False, stop=False, skip_group_check=True)
                        op.then_inc(used, 1)
                    for n, (c0, w) in enumerate(CHUNKS):
                        op = pe.matmul(ps[n][0:TT, 0:w], zeros[:, :], node_ids16[:, 0:w], start=False, stop=True,
                                       skip_group_check=True)
                    op.then_inc(counted, 1)
                    pe.wait_ge(staged_s, b + 1)
                    pe.wait_ge(kept, b + 1)
                    for j in range(NT):
                        op = pe.transpose(ps[4 + j // 4][0:TT, (j % 4) * TT:(j % 4 + 1) * TT],
                                          staged[:, j * TT:(j + 1) * TT], g.ident[0:TT, 0:TT])
                    op.then_inc(turned_t, 1)


def stage_load(nc, g, x):
    g.new_stage()
    with ExitStack() as c:
        x_rows = g.sb(c, "x_rows", [TT, NT, D], F32)
        loaded = [g.sem(f"x_loaded{i}") for i in range(NT)]
        turned = g.sem("x_turned")
        kept = g.sem("x_kept")
        ps = g.psum
        with nc.Block() as block:
            @block.sync
            def _(sp):
                for t in range(NT):
                    sp.dma_start(x_rows[:, t], x[t * TT:(t + 1) * TT, :]).then_inc(loaded[t], 16)

            @block.tensor
            def _(pe):
                for t in range(NT):
                    pe.wait_ge(loaded[t], 16)
                    if t >= 4:
                        pe.wait_ge(kept, t - 3)
                    for k in range(KT):
                        op = pe.transpose(ps[2 * (t % 4) + k // 3][:, (k % 3) * TT:(k % 3 + 1) * TT],
                                          x_rows[:, t, k * P:(k + 1) * P], g.ident[0:TT, 0:TT])
                    op.then_inc(turned, 1)

            @block.vector
            def _(dve):
                for t in range(NT):
                    dve.wait_ge(turned, t + 1)
                    for h in range(2):
                        op = dve.tensor_copy(g.x_T[:, 3 * h:3 * h + 3, t * TT:(t + 1) * TT],
                                             ps[2 * (t % 4) + h][:, 0:3 * TT].rearrange("p (k n) -> p k n", k=3))
                    op.then_inc(kept, 1)


def stage_store(nc, g, out, add=None):
    g.new_stage()
    with ExitStack() as c:
        rows = g.sb(c, "out_rows", [TT, 2, D], F32)
        turned = g.sem("out_turned")
        kept = g.sem("out_kept")
        whole = g.sem("out_whole")
        stored = [g.sem(f"out_stored{i}") for i in range(2)]
        ps = g.psum
        with nc.Block() as block:
            @block.tensor
            def _(pe):
                if add is not None:
                    pe.wait_ge(whole, KT)
                for t in range(NT):
                    if t >= 4:
                        pe.wait_ge(kept, t - 3)
                    for k in range(KT):
                        op = pe.transpose(ps[2 * (t % 4) + k // 3][0:TT, (k % 3) * P:(k % 3 + 1) * P],
                                          g.x_T[:, k, t * TT:(t + 1) * TT], g.ident[:, :])
                    op.then_inc(turned, 1)

            @block.vector
            def _(dve):
                if add is not None:
                    for k in range(KT):
                        dve.tensor_tensor(g.x_T[:, k], g.x_T[:, k], add[:, k], ALU.add).then_inc(whole, 1)
                for t in range(NT):
                    dve.wait_ge(turned, t + 1)
                    if t >= 2:
                        dve.wait_ge(stored[t % 2], 16 * (t // 2))
                    for h in range(2):
                        op = dve.tensor_copy(rows[:, t % 2, h * 384:(h + 1) * 384], ps[2 * (t % 4) + h][0:TT, 0:3 * P])
                    op.then_inc(kept, 1)

            @block.sync
            def _(sp):
                for t in range(NT):
                    sp.wait_ge(kept, t + 1)
                    sp.dma_start(out[t * TT:(t + 1) * TT, :], rows[:, t % 2]).then_inc(stored[t % 2], 16)
                for s in range(2):
                    sp.wait_ge(stored[s], 16 * (NT // 2))


def stage_norm(nc, g, name, src, dst, gamma=None, beta=None):
    g.new_stage()
    with ExitStack() as c:
        mean = g.sb(c, f"{name}_mean", [P, 2, CW], F32)
        square = g.sb(c, f"{name}_square", [P, 2, KT, CW], F32)
        std = g.sb(c, f"{name}_std", [P, 2, CW], F32)
        rstd = g.sb(c, f"{name}_rstd", [P, 2, CW], F32)
        gb = g.sb(c, f"{name}_gb", [P, 2, KT], F32)
        summed = g.sem(f"{name}_summed")
        meaned = g.sem(f"{name}_meaned")
        centred = g.sem(f"{name}_centred")
        squared = g.sem(f"{name}_squared")
        varied = g.sem(f"{name}_varied")
        rooted = g.sem(f"{name}_rooted")
        inverted = g.sem(f"{name}_inverted")
        scaled = g.sem(f"{name}_scaled")
        gb_loaded = g.sem(f"{name}_gb_loaded")
        ps = g.psum
        n_ch = len(CHUNKS)
        with nc.Block() as block:
            if gamma is not None:
                @block.sync
                def _(sp):
                    sp.dma_start(gb[:, 0], gamma.rearrange("(k p) -> p k", p=P), allow_slow_non_contiguous=True).then_inc(gb_loaded, 16)
                    sp.dma_start(gb[:, 1], beta.rearrange("(k p) -> p k", p=P), allow_slow_non_contiguous=True).then_inc(gb_loaded, 16)

            @block.tensor
            def _(pe):
                def total(n, tensor, b, sem):
                    c0, w = CHUNKS[n]
                    for k in range(KT):
                        op = pe.matmul(ps[b][:, 0:w], g.ones[:, :], tensor(k), start=(k == 0), stop=(k == KT - 1))
                    op.then_inc(sem, 1)

                for n, (c0, w) in enumerate(CHUNKS):
                    total(n, lambda k: src[:, k, c0:c0 + w], n, summed)
                for n, (c0, w) in enumerate(CHUNKS):
                    pe.wait_ge(squared, n + 1)
                    total(n, lambda k: square[:, n % 2, k, 0:w], 3 + n, varied)

            @block.scalar
            def _(act):
                def to_mean(n):
                    c0, w = CHUNKS[n]
                    act.wait_ge(summed, n + 1)
                    if n >= 2:
                        act.wait_ge(centred, n - 1)
                    act.activation(mean[:, n % 2, 0:w], ps[n][:, 0:w], ACT.Copy, scale=1.0 / D).then_inc(meaned, 1)

                def to_square(n):
                    c0, w = CHUNKS[n]
                    act.wait_ge(centred, n + 1)
                    if n >= 2:
                        act.wait_ge(varied, n - 1)
                    act.activation(square[:, n % 2, :, 0:w], dst[:, :, c0:c0 + w], ACT.Square).then_inc(squared, 1)

                def to_std(n):
                    c0, w = CHUNKS[n]
                    act.wait_ge(varied, n + 1)
                    if n >= 2:
                        act.wait_ge(inverted, n - 1)
                    act.activation(std[:, n % 2, 0:w], ps[3 + n][:, 0:w], ACT.Sqrt, bias=g.eps5[:, 0:1],
                                   scale=1.0 / D).then_inc(rooted, 1)

                to_mean(0)
                to_mean(1)
                to_square(0)
                to_mean(2)
                to_square(1)
                to_square(2)
                for n in range(n_ch):
                    to_std(n)
                if gamma is not None:
                    act.wait_ge(gb_loaded, 32)
                    act.wait_ge(scaled, n_ch)
                    for k in range(KT):
                        act.activation(dst[:, k, :], dst[:, k, :], ACT.Identity, bias=gb[:, 1, k:k + 1], scale=gb[:, 0, k:k + 1])

            @block.vector
            def _(dve):
                for n, (c0, w) in enumerate(CHUNKS):
                    dve.wait_ge(meaned, n + 1)
                    dve.tensor_tensor(dst[:, :, c0:c0 + w], src[:, :, c0:c0 + w], wide(mean[:, n % 2, 0:w], KT),
                                      ALU.subtract).then_inc(centred, 1)
                for n, (c0, w) in enumerate(CHUNKS):
                    dve.wait_ge(rooted, n + 1)
                    if n >= 2:
                        dve.wait_ge(scaled, n - 1)
                    dve.reciprocal(rstd[:, n % 2, 0:w], std[:, n % 2, 0:w]).then_inc(inverted, 1)
                    dve.wait_ge(inverted, n + 1)
                    dve.wait_ge(squared, n + 1)
                    dve.tensor_tensor(dst[:, :, c0:c0 + w], dst[:, :, c0:c0 + w], wide(rstd[:, n % 2, 0:w], KT),
                                      ALU.mult).then_inc(scaled, 1)


def stage_gat_project(nc, g, W):
    g.new_stage()
    with ExitStack() as c:
        w_rows = g.sb(c, "gat_w_rows", [P, 2, P], F32)
        attn_rows = g.sb(c, "gat_attn_rows", [KT, 2, P], F32)
        attn_T = g.sb(c, "gat_attn_T", [P, 2, KT], F32)
        attn_pair = g.sb(c, "gat_attn_pair", [P, KT, 4], F32)
        rhs = g.sb(c, "gat_rhs", [P, KT, P + 4], F32)
        a1_rows = g.sb(c, "gat_a1_rows", [H, N], F32)
        cleared = g.sem("gatp_cleared")
        loaded = g.sem("gatp_loaded")
        turned = g.sem("gatp_turned")
        kept = g.sem("gatp_kept")
        folded = g.sem("gatp_folded")
        rhs_ready = g.sem("gatp_rhs_ready")
        projected = g.sem("gatp_projected")
        ft_kept = g.sem("gatp_ft_kept")
        a_kept = g.sem("gatp_a_kept")
        a_turned = g.sem("gatp_a_turned")
        row_kept = g.sem("gatp_row_kept")
        stored = g.sem("gatp_stored")
        ps = g.psum
        with nc.Block() as block:
            @block.gpsimd
            def _(pool):
                pool.memset(w_rows[:, :, :], 0.0).then_inc(cleared, 1)
                pool.memset(attn_pair[:, :, :], 0.0).then_inc(cleared, 1)

            @block.sync
            def _(sp):
                sp.wait_ge(cleared, 2)
                for n, w in enumerate((W["L0_gnn_W_fc"], W["L0_gnn_W_res"])):
                    for h in range(2):
                        sp.dma_start(w_rows[64 * h:64 * h + 64, n, 64 * h:64 * h + 64], w).then_inc(loaded, 16)
                for n, a in enumerate((W["L0_gnn_attn_l"], W["L0_gnn_attn_r"])):
                    sp.dma_start(attn_rows[:, n], a.rearrange("(p h) e -> p (h e)", h=2)).then_inc(loaded, 16)
                sp.wait_ge(row_kept, NT)
                sp.dma_start(g.a1_dram, a1_rows[:, :]).then_inc(stored, 16)
                sp.wait_ge(stored, 16)

            @block.tensor
            def _(pe):
                pe.wait_ge(loaded, 96)
                for n in range(2):
                    pe.transpose(ps[0][:, n * P:(n + 1) * P], w_rows[:, n], g.ident[:, :])
                    op = pe.transpose(ps[1][:, n * KT:(n + 1) * KT], attn_rows[:, n], g.ident[0:KT, 0:KT])
                op.then_inc(turned, 1)
                pe.wait_ge(kept, 6)
                for k in range(KT):
                    op = pe.matmul(ps[2][:, 4 * k:4 * k + 4], w_rows[:, 0], attn_pair[:, k], start=True, stop=True)
                op.then_inc(folded, 1)
                pe.wait_ge(rhs_ready, 2)
                for t in range(NT):
                    if t >= 3:
                        pe.wait_ge(ft_kept, t - 2)
                    for k in range(KT):
                        op = pe.matmul(ps[2 * (t % 3) + k // 3][0:TT, (k % 3) * (P + 4):(k % 3 + 1) * (P + 4)],
                                       g.y_T[:, k, t * TT:(t + 1) * TT], rhs[:, k], start=True, stop=True)
                    op.then_inc(projected, 1)
                for t in range(NT):
                    pe.wait_ge(a_kept, t + 1)
                    if t >= 2:
                        pe.wait_ge(row_kept, t - 1)
                    pe.transpose(ps[6 + t % 2][0:H, 0:TT], g.a_cols[:, t, 0], g.ident[0:TT, 0:TT]).then_inc(a_turned, 1)

            @block.vector
            def _(dve):
                dve.wait_ge(turned, 1)
                dve.wait_ge(cleared, 2)
                dve.tensor_copy(g.w_res[:, :], ps[0][:, P:2 * P]).then_inc(kept, 1)
                dve.tensor_copy(attn_T[:, :, :], ps[1][:, 0:2 * KT].rearrange("p (n k) -> p n k", n=2)).then_inc(kept, 1)
                dve.wait_ge(kept, 2)
                for n in range(2):
                    for h in range(2):
                        dve.tensor_copy(attn_pair[64 * h:64 * h + 64, :, 2 * n + h], attn_T[64 * h:64 * h + 64, n]).then_inc(kept, 1)
                dve.tensor_copy(rhs[:, :, 0:P], wide(ps[0][:, 0:P], KT)).then_inc(rhs_ready, 1)
                dve.wait_ge(folded, 1)
                dve.tensor_copy(rhs[:, :, P:P + 4], ps[2][:, 0:4 * KT].rearrange("p (k j) -> p k j", k=KT)).then_inc(rhs_ready, 1)
                for t in range(NT):
                    dve.wait_ge(projected, t + 1)
                    for h in range(2):
                        part = ps[2 * (t % 3) + h][0:TT, 0:3 * (P + 4)].rearrange("p (k j) -> p k j", k=3)
                        for n in range(2):
                            op = dve.tensor_copy(g.a_cols[:, t, n, 6 * h:6 * h + 6].rearrange("p (k j) -> p k j", k=3),
                                                 part[:, :, P + 2 * n:P + 2 * n + 2])
                    op.then_inc(a_kept, 1)
                for t in range(NT):
                    dve.wait_ge(a_turned, t + 1)
                    dve.tensor_copy(a1_rows[:, t * TT:(t + 1) * TT], ps[6 + t % 2][0:H, 0:TT]).then_inc(row_kept, 1)

            @block.scalar
            def _(act):
                for t in range(NT):
                    act.wait_ge(a_kept, t + 1)
                    for h in range(2):
                        part = ps[2 * (t % 3) + h][0:TT, 0:3 * (P + 4)].rearrange("p (k j) -> p k j", k=3)
                        op = act.activation(g.ft[:, t, 3 * h:3 * h + 3, :], part[:, :, 0:P], ACT.Copy)
                    op.then_inc(ft_kept, 1)


def stage_gat_max(nc, g):
    g.new_stage()
    with ExitStack() as c:
        a1_wide = g.sb(c, "a1_wide", [TT, 2, N], F32)
        masked = g.sb(c, "masked", [TT, 2, N], F32)
        a1_max = g.sb(c, "a1_max", [TT, NT, H], F32)
        e_max = g.sb(c, "e_max", [TT, NT, H], F32)
        e_sum = g.sb(c, "e_sum", [TT, NT, H], F32)
        uv = g.sb(c, "uv", [TT, NT, 2, H], F32)
        uv_rows = g.sb(c, "uv_rows", [2 * H, N], F32)
        wide_s = [g.sem(f"gatm_wide{i}") for i in range(2)]
        maxed = g.sem("gatm_maxed")
        chain = g.sem("gatm_chain")
        turned = g.sem("gatm_turned")
        row_kept = g.sem("gatm_row_kept")
        stored = g.sem("gatm_stored")
        ps = g.psum
        with nc.Block() as block:
            @block.sync
            def _(sp):
                for h in range(2):
                    sp.dma_start(a1_wide[:, h], g.a1_dram[h:h + 1, :].partition_broadcast(TT)).then_inc(wide_s[h], 16)
                with sp.Fori(1, KT) as p:
                    for h in range(2):
                        sp.wait_ge(maxed, NT * (2 * p + h - 1))
                        sp.dma_start(a1_wide[:, h], g.a1_dram[bass.ds(2 * p + h, 1), :].partition_broadcast(TT)).then_inc(wide_s[h], 16)
                sp.wait_ge(row_kept, NT)
                sp.dma_start(g.uv_dram, uv_rows[:, :]).then_inc(stored, 16)
                sp.wait_ge(stored, 16)

            @block.vector
            def _(dve):
                for h in range(H):
                    dve.wait_ge(wide_s[h % 2], 16 * (h // 2) + 16)
                    for b in range(NT):
                        if h * NT + b >= 2:
                            dve.wait_ge(maxed, h * NT + b - 1)
                        dve.tensor_tensor_reduce(masked[:, b % 2], a1_wide[:, h % 2], g.no_edge[:, b], 1.0, -BIG,
                                                 ALU.add, ALU.max, a1_max[:, b, h:h + 1]).then_inc(maxed, 1)
                a1, a2 = g.a_cols[:, :, 0], g.a_cols[:, :, 1]
                dve.wait_ge(maxed, H * NT)
                dve.tensor_tensor(e_sum[:, :, :], a2, a1_max[:, :, :], ALU.add).then_inc(chain, 1)
                dve.wait_ge(chain, 1)
                dve.scalar_tensor_tensor(out=e_max[:, :, :], in0=e_sum[:, :, :], scalar=0.2, in1=e_sum[:, :, :],
                                         op0=ALU.mult, op1=ALU.max).then_inc(chain, 1)
                dve.wait_ge(chain, 2)
                dve.tensor_tensor(uv[:, :, 0], a2, e_max[:, :, :], ALU.subtract).then_inc(chain, 1)
                dve.scalar_tensor_tensor(out=uv[:, :, 1], in0=a2, scalar=0.2, in1=e_max[:, :, :],
                                         op0=ALU.mult, op1=ALU.subtract).then_inc(chain, 1)
                dve.tensor_scalar(g.a1_fifth[:, :, :], a1, 0.2, None, ALU.mult).then_inc(chain, 1)
                for t in range(NT):
                    dve.wait_ge(turned, t + 1)
                    dve.tensor_copy(uv_rows[:, t * TT:(t + 1) * TT], ps[t % 2][0:2 * H, 0:TT]).then_inc(row_kept, 1)

            @block.tensor
            def _(pe):
                pe.wait_ge(chain, 4)
                for t in range(NT):
                    if t >= 2:
                        pe.wait_ge(row_kept, t - 1)
                    pe.transpose(ps[t % 2][0:2 * H, 0:TT], uv[:, t].rearrange("p n h -> p (n h)"),
                                 g.ident[0:TT, 0:TT]).then_inc(turned, 1)


def stage_gat_attend(nc, g):
    g.new_stage()
    with ExitStack() as c:
        u_wide = g.sb(c, "u_wide", [TT, 2, N], F32)
        v_wide = g.sb(c, "v_wide", [TT, 2, N], F32)
        ft_pair = g.sb(c, "ft_pair", [TT, NT, 192], F32)
        low = g.sb(c, "gat_low", [TT, 2, N], F32)
        high = g.sb(c, "gat_high", [TT, 2, N], F32)
        prob = g.sb(c, "gat_prob", [TT, 2, N], F32)
        den = g.sb(c, "gat_den", [P, N], F32)
        inv = g.sb(c, "gat_inv", [P, N], F32)
        agg = den
        ones_s = g.sem("gata_ones")
        uv_loaded = [g.sem(f"gata_uv{i}") for i in range(2)]
        ft_s = g.sem("gata_ft")
        low_s = g.sem("gata_low")
        high_s = g.sem("gata_high")
        exp_s = g.sem("gata_exp")
        prob_s = g.sem("gata_prob")
        used = g.sem("gata_used")
        den_s = g.sem("gata_den")
        fin = g.sem("gata_finish")
        freed = g.sem("gata_freed")
        res_s = g.sem("gata_res")
        ps = g.psum
        n2 = 2 * NT
        with nc.Block() as block:
            @block.sync
            def _(sp):
                for h in range(2):
                    for wide_t, o in ((u_wide, 0), (v_wide, H)):
                        sp.dma_start(wide_t[:, h], g.uv_dram[h + o:h + o + 1, :].partition_broadcast(TT)).then_inc(uv_loaded[h], 16)
                with sp.Fori(1, KT) as p:
                    for h in range(2):
                        sp.wait_ge(high_s, n2 * p - n2 + NT * (h + 1) + 2)
                        for wide_t, o in ((u_wide, 0), (v_wide, H)):
                            sp.dma_start(wide_t[:, h], g.uv_dram[bass.ds(p * 2 + h + o, 1), :].partition_broadcast(TT)).then_inc(uv_loaded[h], 16)

            @block.gpsimd
            def _(pool):
                pool.memset(ft_pair[:, :, 64:128], 1.0).then_inc(ones_s, 1)
                with pool.Fori(0, KT) as p:
                    pool.wait_ge(used, n2 * p + 2)
                    ftp = g.ft[:, :, bass.ds(p, 1), :].squeeze(2)
                    pool.tensor_copy(ft_pair[:, :, 0:64], ftp[:, :, 0:64]).then_inc(ft_s, 1)
                    pool.tensor_copy(ft_pair[:, :, 128:192], ftp[:, :, 64:128]).then_inc(ft_s, 1)

            @block.scalar
            def _(act):
                with act.Fori(0, KT) as p:
                    def lower(i):
                        h, j = i // NT, i % NT
                        act.wait_ge(uv_loaded[h], 32 * p + 32)
                        act.wait_ge(high_s, n2 * p + i + 1)
                        act.activation(low[:, i % 2], v_wide[:, h], ACT.Identity,
                                       bias=g.a1_fifth[:, j, bass.ds(2 * p + h, 1)]).then_inc(low_s, 1)

                    def expo(i):
                        act.wait_ge(high_s, n2 * p + i + 3)
                        act.activation(high[:, i % 2], high[:, i % 2], ACT.Exp).then_inc(exp_s, 1)

                    lower(0)
                    for i in range(n2):
                        if i + 1 < n2:
                            lower(i + 1)
                        expo(i)
                    for h in range(2):
                        act.wait_ge(used, n2 * p + NT * (h + 1) + 2)
                        act.wait_ge(fin, 3 * p + 1)
                        for n, (c0, w) in enumerate(CHUNKS):
                            op = act.activation(den[64 * h:64 * h + 64, c0:c0 + w], ps[3 * h + n][64 - 64 * h:128 - 64 * h, 0:w], ACT.Copy)
                        op.then_inc(den_s, 1)

            @block.vector
            def _(dve):
                dve.sem_inc(high_s, 2)
                dve.sem_inc(fin, 1)
                dve.sem_inc(used, 2)
                dve.sem_inc(freed, 1)
                with dve.Fori(0, KT) as p:
                    def raise_(i):
                        h, j = i // NT, i % NT
                        dve.wait_ge(uv_loaded[h], 32 * p + 32)
                        dve.wait_ge(low_s, n2 * p + i + 1)
                        if i >= 2:
                            dve.wait_ge(prob_s, n2 * p + i - 1)
                        dve.scalar_tensor_tensor(out=high[:, i % 2], in0=u_wide[:, h],
                                                 scalar=g.a_cols[:, j, 0, bass.ds(2 * p + h, 1)],
                                                 in1=low[:, i % 2], op0=ALU.add, op1=ALU.max).then_inc(high_s, 1)

                    def weigh(i):
                        j = i % NT
                        dve.wait_ge(exp_s, n2 * p + i + 1)
                        dve.wait_ge(used, n2 * p + i + 1)
                        dve.scalar_tensor_tensor(out=prob[:, i % 2], in0=high[:, i % 2], scalar=1.0, in1=g.counts_T[:, j],
                                                 op0=ALU.min, op1=ALU.mult).then_inc(prob_s, 1)

                    raise_(0)
                    for i in range(n2):
                        if i + 1 < n2:
                            raise_(i + 1)
                        weigh(i)
                    dve.wait_ge(den_s, 2 * p + 2)
                    dve.tensor_scalar(den[:, :], den[:, :], 0.5, None, ALU.max).then_inc(fin, 1)
                    dve.wait_ge(fin, 3 * p + 2)
                    dve.reciprocal(inv[:, :], den[:, :]).then_inc(fin, 1)
                    dve.wait_ge(fin, 3 * p + 3)
                    for h in range(2):
                        r = slice(64 * h, 64 * h + 64)
                        for n, (c0, w) in enumerate(CHUNKS):
                            op = dve.tensor_tensor(agg[r, c0:c0 + w], ps[3 * h + n][r, 0:w], inv[r, c0:c0 + w], ALU.mult)
                    op.then_inc(freed, 1)
                    dve.wait_ge(freed, 4 * p + 2)
                    for n, (c0, w) in enumerate(CHUNKS):
                        dve.wait_ge(res_s, 3 * p + n + 1)
                        dve.tensor_tensor(agg[:, c0:c0 + w], agg[:, c0:c0 + w], ps[6 + n % 2][:, 0:w], ALU.add).then_inc(freed, 1)
                    dve.wait_ge(freed, 4 * p + 5)
                    xp = g.x_T[:, bass.ds(p, 1), :].squeeze(1)
                    dve.scalar_tensor_tensor(out=xp, in0=agg[:, :], scalar=0.0, in1=xp, op0=ALU.max, op1=ALU.add).then_inc(fin, 1)

            @block.tensor
            def _(pe):
                with pe.Fori(0, KT) as p:
                    pe.wait_ge(freed, 4 * p + 1)
                    pe.wait_ge(ones_s, 1)
                    pe.wait_ge(ft_s, 2 * p + 2)
                    for i in range(n2):
                        h, j = i // NT, i % NT
                        pe.wait_ge(prob_s, n2 * p + i + 1)
                        for n, (c0, w) in enumerate(CHUNKS):
                            op = pe.matmul(ps[3 * h + n][:, 0:w], ft_pair[:, j, 64 * h:64 * h + 128],
                                           prob[:, i % 2, c0:c0 + w], start=(j == 0), stop=(j == NT - 1))
                        op.then_inc(used, 1)
                    for n, (c0, w) in enumerate(CHUNKS):
                        if n == 2:
                            pe.wait_ge(freed, 4 * p + 3)
                        pe.matmul(ps[6 + n % 2][:, 0:w], g.w_res[:, :], g.y_T[:, bass.ds(p, 1), c0:c0 + w].squeeze(1),
                                  start=True, stop=True).then_inc(res_s, 1)


def project_T(pe, banks, w, src):
    for k in range(KT):
        for n, (c0, wd) in enumerate(CHUNKS):
            op = pe.matmul(banks[n][:, 0:wd], w[:, k], src[:, k, c0:c0 + wd], start=(k == 0), stop=(k == KT - 1))
    return op


def stage_mix0(nc, g, w_qkv, src, o_T):
    g.new_stage()
    with ExitStack() as c:
        w = g.sb(c, "mix0_w", [P, KT, 3, P], F32)
        q = g.sb(c, "mix0_q", [P, N], F32)
        q_low = g.sb(c, "mix0_q_low", [P, N], F32)
        k = g.sb(c, "mix0_k", [TT, NT, P], F32)
        k_low = g.sb(c, "mix0_k_low", [TT, NT, P], F32)
        v1 = g.sb(c, "mix0_v1", [TT, NT, 2 * P], F32)
        kv = g.sb(c, "mix0_kv", [P, 2, P], F32)
        inv = g.sb(c, "mix0_inv", [P, N], F32)
        ones_s = g.sem("mix0_ones")
        loaded = g.sem("mix0_w_loaded")
        w_used = g.sem("mix0_w_used")
        projected = g.sem("mix0_projected")
        lows = g.sem("mix0_lows")
        exps = g.sem("mix0_exps")
        elus = g.sem("mix0_elus")
        kv_sum = g.sem("mix0_kv_sum")
        kv_s = g.sem("mix0_kv")
        outs = g.sem("mix0_outs")
        inv_s = g.sem("mix0_inv")
        done = g.sem("mix0_done")
        ps = g.psum
        with nc.Block() as block:
            @block.sync
            def _(sp):
                with sp.Fori(0, KT) as p:
                    sp.wait_ge(w_used, p + 1)
                    for n in range(3):
                        sp.dma_start(w[:, :, n], w_qkv.rearrange("(k f) (n m) -> f k n m", f=P, n=3)[:, :, n, bass.ds(p * P, P)]).then_inc(loaded, 16)

            @block.gpsimd
            def _(pool):
                pool.memset(v1[:, :, P:2 * P], 1.0).then_inc(ones_s, 1)
                pool.sem_inc(w_used, 1)
                pool.sem_inc(done, 1)

            @block.tensor
            def _(pe):
                pe.wait_ge(ones_s, 1)
                with pe.Fori(0, KT) as p:
                    pe.wait_ge(loaded, 48 * p + 48)
                    pe.wait_ge(done, p + 1)
                    project_T(pe, ps[0:3], w[:, :, 0], src).then_inc(projected, 1)
                    for t in range(NT):
                        for kk in range(KT):
                            op = pe.matmul(ps[3 + t // 2][0:TT, (t % 2) * 256:(t % 2) * 256 + 256],
                                           src[:, kk, t * TT:(t + 1) * TT], w[:, kk, 1:3, :],
                                           start=(kk == 0), stop=(kk == KT - 1))
                        if t % 2:
                            op.then_inc(projected, 1)
                    pe.wait_ge(projected, 6 * p + 6)
                    pe.sem_inc(w_used, 1)
                    pe.wait_ge(elus, 8 * p + 8)
                    for t in range(NT):
                        op = pe.matmul(ps[3][:, 0:256], k[:, t], v1[:, t], start=(t == 0), stop=(t == NT - 1))
                    op.then_inc(kv_sum, 1)
                    pe.wait_ge(kv_s, 2 * p + 2)
                    for n, (c0, wd) in enumerate(CHUNKS):
                        pe.matmul(ps[4 + n][:, 0:wd], kv[:, 1], q[:, c0:c0 + wd], start=True, stop=True)
                        pe.matmul(ps[n][:, 0:wd], kv[:, 0], q[:, c0:c0 + wd], start=True, stop=True).then_inc(outs, 1)

            @block.scalar
            def _(act):
                with act.Fori(0, KT) as p:
                    for n, (c0, wd) in enumerate(CHUNKS):
                        act.wait_ge(lows, 8 * p + n + 1)
                        act.activation(q_low[:, c0:c0 + wd], q_low[:, c0:c0 + wd], ACT.Exp).then_inc(exps, 1)
                    for b in range(5):
                        act.wait_ge(lows, 8 * p + b + 4)
                        act.activation(k_low[:, 2 * b:2 * b + 2], k_low[:, 2 * b:2 * b + 2], ACT.Exp).then_inc(exps, 1)

            @block.vector
            def _(dve):
                with dve.Fori(0, KT) as p:
                    dve.wait_ge(projected, 6 * p + 1)
                    for n, (c0, wd) in enumerate(CHUNKS):
                        dve.tensor_scalar(q_low[:, c0:c0 + wd], ps[n][:, 0:wd], 0.0, None, ALU.min).then_inc(lows, 1)
                    for n, (c0, wd) in enumerate(CHUNKS):
                        dve.wait_ge(exps, 8 * p + n + 1)
                        dve.scalar_tensor_tensor(out=q[:, c0:c0 + wd], in0=ps[n][:, 0:wd], scalar=0.0, in1=q_low[:, c0:c0 + wd],
                                                 op0=ALU.max, op1=ALU.add).then_inc(elus, 1)
                    for b in range(5):
                        dve.wait_ge(projected, 6 * p + b + 2)
                        kvb = ps[3 + b][0:TT, 0:512].rearrange("p (t n m) -> p t n m", t=2, n=2)
                        dve.tensor_scalar(k_low[:, 2 * b:2 * b + 2], kvb[:, :, 0], 0.0, None, ALU.min).then_inc(lows, 1)
                        dve.tensor_copy(v1[:, 2 * b:2 * b + 2, 0:P], kvb[:, :, 1])
                    for b in range(5):
                        kvb = ps[3 + b][0:TT, 0:512].rearrange("p (t n m) -> p t n m", t=2, n=2)
                        dve.wait_ge(exps, 8 * p + b + 4)
                        dve.scalar_tensor_tensor(out=k[:, 2 * b:2 * b + 2], in0=kvb[:, :, 0], scalar=0.0, in1=k_low[:, 2 * b:2 * b + 2],
                                                 op0=ALU.max, op1=ALU.add).then_inc(elus, 1)
                    dve.wait_ge(kv_sum, p + 1)
                    for n in range(2):
                        dve.tensor_tensor(kv[:, n], ps[3][:, n * P:(n + 1) * P], g.pair_mask[:, :], ALU.mult).then_inc(kv_s, 1)
                    for n, (c0, wd) in enumerate(CHUNKS):
                        dve.wait_ge(outs, 3 * p + n + 1)
                        dve.reciprocal(inv[:, c0:c0 + wd], ps[4 + n][:, 0:wd]).then_inc(inv_s, 1)
                        dve.wait_ge(inv_s, 3 * p + n + 1)
                        op = dve.tensor_tensor(o_T[:, bass.ds(p, 1), c0:c0 + wd].squeeze(1), ps[n][:, 0:wd], inv[:, c0:c0 + wd], ALU.mult)
                    op.then_inc(done, 1)


def stage_linear(nc, g, name, w, bias, src, kt, mt, func, dst=None, add_to=None, scale=1.0, times=None, expert=None):
    g.new_stage()
    with ExitStack() as c:
        w_sb = g.sb(c, f"{name}_w", [P, 2, kt, P], F32)
        bias_sb = g.sb(c, f"{name}_bias", [P, mt], F32)
        bias_x = g.sb(c, f"{name}_bias_x", [P, mt], F32)
        t_sb = g.sb(c, f"{name}_t", [P, 2, N], F32) if add_to is not None else None
        loaded = [g.sem(f"{name}_w_loaded{i}") for i in range(2)]
        bias_loaded = g.sem(f"{name}_bias_loaded")
        bias_s = g.sem(f"{name}_bias_scaled")
        summed = g.sem(f"{name}_summed")
        taken = g.sem(f"{name}_taken")
        added = g.sem(f"{name}_added")
        ps = g.psum
        with nc.Block() as block:
            @block.sync
            def _(sp):
                if expert is None:
                    w_of, b_of = w, bias
                else:
                    e = sp.value_load(expert, min_val=0, max_val=w.shape[0] - 1)
                    w_of = w[bass.ds(e, 1)].squeeze(0)
                    b_of = bias[bass.ds(e, 1)].squeeze(0)
                w_v = w_of.rearrange("(k f) m -> f k m", f=P)
                sp.dma_start(w_sb[:, 0], w_v[:, :, 0:P]).then_inc(loaded[0], 16)
                sp.dma_start(bias_sb[:, :], b_of.rearrange("(m f) -> f m", f=P), allow_slow_non_contiguous=True).then_inc(bias_loaded, 16)
                for m in range(1, mt):
                    if m >= 2:
                        sp.wait_ge(summed, m - 1)
                    sp.dma_start(w_sb[:, m % 2], w_v[:, :, m * P:(m + 1) * P]).then_inc(loaded[m % 2], 16)

            @block.tensor
            def _(pe):
                for m in range(mt):
                    pe.wait_ge(loaded[m % 2], 16 * (m // 2) + 16)
                    if m >= 2:
                        pe.wait_ge(taken, m - 1)
                    for k in range(kt):
                        for n, (c0, wd) in enumerate(CHUNKS):
                            op = pe.matmul(ps[3 * (m % 2) + n][:, 0:wd], w_sb[:, m % 2, k], src[:, k, c0:c0 + wd],
                                           start=(k == 0), stop=(k == kt - 1))
                    op.then_inc(summed, 1)

            @block.scalar
            def _(act):
                act.wait_ge(bias_loaded, 16)
                act.activation(bias_x[:, :], bias_sb[:, :], ACT.Copy, scale=scale).then_inc(bias_s, 1)
                act.wait_ge(bias_s, 1)
                for m in range(mt):
                    act.wait_ge(summed, m + 1)
                    if add_to is not None and m >= 2:
                        act.wait_ge(added, m - 1)
                    for n, (c0, wd) in enumerate(CHUNKS):
                        out = dst[:, m, c0:c0 + wd] if add_to is None else t_sb[:, m % 2, c0:c0 + wd]
                        op = act.activation(out, ps[3 * (m % 2) + n][:, 0:wd], func, bias=bias_x[:, m:m + 1], scale=scale)
                    op.then_inc(taken, 1)

            if add_to is not None:
                @block.vector
                def _(dve):
                    for m in range(mt):
                        dve.wait_ge(taken, m + 1)
                        if times is None:
                            op = dve.tensor_tensor(add_to[:, m], add_to[:, m], t_sb[:, m % 2], ALU.add)
                        else:
                            op = dve.scalar_tensor_tensor(out=add_to[:, m], in0=t_sb[:, m % 2], scalar=times,
                                                          in1=add_to[:, m], op0=ALU.mult, op1=ALU.add)
                        op.then_inc(added, 1)


def stage_choose(nc, g, w_gate, src, weight, expert):
    g.new_stage()
    NE = 3
    with ExitStack() as c:
        wg = g.sb(c, "choose_wg", [P, KT, NE], F32)
        mean = g.sb(c, "choose_mean", [P, KT], F32)
        mean_wide = g.sb(c, "choose_mean_wide", [P, KT, P], F32)
        s = g.sb(c, "choose_s", [P, 16], F32)
        loaded = g.sem("choose_loaded")
        mean_s = g.sem("choose_mean_s")
        logits = g.sem("choose_logits")
        top_s = g.sem("choose_top")
        exp_s = g.sem("choose_exp")
        chain = g.sem("choose_chain")
        ps = g.psum
        top, exps, total, inv, prob, is1, is2, nof = (slice(0, 1), slice(1, 4), slice(4, 5), slice(5, 6),
                                                      slice(6, 9), slice(9, 10), slice(10, 11), slice(11, 12))
        with nc.Block() as block:
            @block.sync
            def _(sp):
                for e in range(NE):
                    sp.dma_start(wg[:, :, e], w_gate[e].rearrange("(k f) -> f k", f=P), allow_slow_non_contiguous=True).then_inc(loaded, 16)

            @block.vector
            def _(dve):
                n = [0]

                def step(op):
                    n[0] += 1
                    op.then_inc(chain, 1)
                    dve.wait_ge(chain, n[0])

                step(dve.tensor_reduce(mean[:, :], src[:, :, :], AX_X, ALU.add))
                dve.tensor_scalar(mean_wide[:, :, :], mean[:, :].unsqueeze(2).broadcast_to([P, KT, P]), 1.0 / N, None,
                                  ALU.mult).then_inc(mean_s, 1)
                dve.wait_ge(logits, 1)
                dve.tensor_reduce(s[:, top], ps[0][:, 0:NE], AX_X, ALU.max, negate=True).then_inc(top_s, 1)
                dve.wait_ge(exp_s, 1)
                step(dve.reciprocal(s[:, inv], s[:, total]))
                step(dve.tensor_scalar(s[:, prob], s[:, exps], s[:, inv], None, ALU.mult))
                step(dve.tensor_reduce(weight, s[:, prob], AX_X, ALU.max))
                step(dve.tensor_tensor(s[:, nof], s[:, 6:7], s[:, 7:8], ALU.max))
                step(dve.tensor_tensor(s[:, is2], s[:, 8:9], s[:, nof], ALU.is_gt))
                step(dve.tensor_tensor(s[:, is1], s[:, 7:8], s[:, 6:7], ALU.is_gt))
                step(dve.scalar_tensor_tensor(out=s[:, nof], in0=s[:, is2], scalar=2.0, in1=s[:, is1], op0=ALU.mult, op1=ALU.max))
                dve.tensor_copy(expert, s[:, nof])

            @block.scalar
            def _(act):
                act.wait_ge(top_s, 1)
                act.activation(s[:, exps], ps[0][:, 0:NE], ACT.Exp, bias=s[:, top], accum_out=s[:, total]).then_inc(exp_s, 1)

            @block.tensor
            def _(pe):
                pe.wait_ge(loaded, 16 * NE)
                pe.wait_ge(mean_s, 1)
                for k in range(KT):
                    op = pe.matmul(ps[0][:, 0:NE], mean_wide[:, k], wg[:, k], start=(k == 0), stop=(k == KT - 1))
                op.then_inc(logits, 1)


def stage_gcn(nc, g, w_gcn, bias, src, x_T):
    g.new_stage()
    HALF = D // 2
    with ExitStack() as c:
        w = g.sb(c, "gcn_w", [P, 2, KT, HALF], F32)
        bias_sb = g.sb(c, "gcn_bias", [P, KT], F32)
        root = g.sb(c, "gcn_root", [P, N], F32)
        norm = g.sb(c, "gcn_norm", [P, N], F32)
        norm_cols = g.sb(c, "gcn_norm_cols", [TT, NT], F32)
        h = g.sb(c, "gcn_h", [TT, NT, D], F32)
        t_sb = g.sb(c, "gcn_t", [P, 2, N], F32)
        loaded = g.sem("gcn_loaded")
        looped = g.sem("gcn_looped")
        degrees = g.sem("gcn_degrees")
        rooted = g.sem("gcn_rooted")
        normed = g.sem("gcn_normed")
        cols = g.sem("gcn_cols")
        cols_s = g.sem("gcn_cols_kept")
        projected = g.sem("gcn_projected")
        h_s = g.sem("gcn_h_s")
        summed = g.sem("gcn_summed")
        scaled = g.sem("gcn_scaled")
        added = g.sem("gcn_added")
        ps = g.psum
        with nc.Block() as block:
            @block.sync
            def _(sp):
                for i in range(2):
                    sp.dma_start(w[:, i], w_gcn.rearrange("(k f) m -> f k m", f=P)[:, :, i * HALF:(i + 1) * HALF]).then_inc(loaded, 16)
                sp.dma_start(bias_sb[:, :], bias.rearrange("(m f) -> f m", f=P), allow_slow_non_contiguous=True).then_inc(loaded, 16)

            @block.tensor
            def _(pe):
                pe.wait_ge(looped, NT)
                for n, (c0, wd) in enumerate(CHUNKS):
                    for j in range(NT):
                        op = pe.matmul(ps[n][:, 0:wd], g.ones[0:TT, :], g.counts_T[:, j, c0:c0 + wd], start=(j == 0), stop=(j == NT - 1))
                    op.then_inc(degrees, 1)
                pe.wait_ge(normed, 3)
                for t in range(NT):
                    op = pe.matmul(ps[3][0:TT, t:t + 1], norm[0:1, t * TT:(t + 1) * TT], g.ones[0:1, 0:1], start=True, stop=True)
                op.then_inc(cols, 1)
                pe.wait_ge(loaded, 48)
                for i in range(2 * NT):
                    t = i % NT
                    if i >= 4:
                        pe.wait_ge(h_s, i - 3)
                    for k in range(KT):
                        op = pe.matmul(ps[4 + i % 4][0:TT, 0:HALF], src[:, k, t * TT:(t + 1) * TT], w[:, i // NT, k],
                                       start=(k == 0), stop=(k == KT - 1))
                    op.then_inc(projected, 1)
                pe.wait_ge(h_s, 2 * NT)
                for m in range(KT):
                    if m >= 2:
                        pe.wait_ge(scaled, m - 1)
                    for j in range(NT):
                        for n, (c0, wd) in enumerate(CHUNKS):
                            op = pe.matmul(ps[3 * (m % 2) + n][:, 0:wd], h[:, j, m * P:(m + 1) * P], g.counts_T[:, j, c0:c0 + wd],
                                           start=(j == 0), stop=(j == NT - 1))
                    op.then_inc(summed, 1)

            @block.scalar
            def _(act):
                for n, (c0, wd) in enumerate(CHUNKS):
                    act.wait_ge(degrees, n + 1)
                    act.activation(root[:, c0:c0 + wd], ps[n][:, 0:wd], ACT.Sqrt).then_inc(rooted, 1)
                act.wait_ge(cols_s, 1)
                for i in range(2 * NT):
                    t, half = i % NT, i // NT
                    act.wait_ge(projected, i + 1)
                    act.activation(h[:, t, half * HALF:(half + 1) * HALF], ps[4 + i % 4][0:TT, 0:HALF], ACT.Copy,
                                   scale=norm_cols[:, t:t + 1]).then_inc(h_s, 1)

            @block.vector
            def _(dve):
                for j in range(NT):
                    own = g.counts_T[:, j, j * TT:(j + 1) * TT]
                    dve.tensor_tensor(own, own, g.ident[0:TT, 0:TT], ALU.add).then_inc(looped, 1)
                for n, (c0, wd) in enumerate(CHUNKS):
                    dve.wait_ge(rooted, n + 1)
                    dve.reciprocal(norm[:, c0:c0 + wd], root[:, c0:c0 + wd]).then_inc(normed, 1)
                dve.wait_ge(cols, 1)
                dve.tensor_copy(norm_cols[:, :], ps[3][0:TT, 0:NT]).then_inc(cols_s, 1)
                dve.wait_ge(normed, 3)
                dve.wait_ge(loaded, 48)
                for m in range(KT):
                    dve.wait_ge(summed, m + 1)
                    if m >= 2:
                        dve.wait_ge(added, m - 1)
                    for n, (c0, wd) in enumerate(CHUNKS):
                        op = dve.tensor_tensor(t_sb[:, m % 2, c0:c0 + wd], ps[3 * (m % 2) + n][:, 0:wd], norm[:, c0:c0 + wd], ALU.mult)
                    op.then_inc(scaled, 1)
                    dve.wait_ge(scaled, m + 1)
                    dve.scalar_tensor_tensor(out=x_T[:, m], in0=t_sb[:, m % 2], scalar=bias_sb[:, m:m + 1], in1=x_T[:, m],
                                             op0=ALU.add, op1=ALU.add).then_inc(added, 1)


def stage_mix1(nc, g, w_qkv, b_qkv, src, o_T):
    g.new_stage()
    EPS = 1e-6
    with ExitStack() as c:
        w = g.sb(c, "mix1_w", [P, KT, 3, P], F32)
        bias_q = g.sb(c, "mix1_bias_q", [P, KT], F32)
        bias_kv = g.sb(c, "mix1_bias_kv", [TT, 2, P], F32)
        eps = g.sb(c, "mix1_eps", [P, 1], F32)
        q = g.sb(c, "mix1_q", [P, N], F32)
        q_eps = g.sb(c, "mix1_q_eps", [P, N], F32)
        q_sums = g.sb(c, "mix1_q_sums", [P, 3], F32)
        q_sum = g.sb(c, "mix1_q_sum", [P, 2], F32)
        col_wide = g.sb(c, "mix1_col_wide", [P, 2, TT], F32)
        row = g.sb(c, "mix1_row", [TT, 2, P], F32)
        k = g.sb(c, "mix1_k", [TT, NT, P], F32)
        k_eps = g.sb(c, "mix1_k_eps", [TT, NT, P], F32)
        prod = g.sb(c, "mix1_prod", [TT, NT, P], F32)
        v = g.sb(c, "mix1_v", [TT, NT, P], F32)
        outgoing = g.sb(c, "mix1_outgoing", [TT, 4, NT, 2], F32)
        outgoing_wide = g.sb(c, "mix1_outgoing_wide", [TT, NT, P], F32)
        comp = g.sb(c, "mix1_comp", [TT, 3, NT, 2], F32)
        ends = g.sb(c, "mix1_ends", [P, 3, P], F32)
        factor = g.sb(c, "mix1_factor", [P, 3], F32)
        sink_den = g.sb(c, "mix1_sink_den", [P, N], F32)
        sink = g.sb(c, "mix1_sink", [P, N], F32)
        alloc = g.sb(c, "mix1_alloc", [P, N], F32)
        junk = g.sb(c, "mix1_junk", [P, N], F32)
        eps_s = g.sem("mix1_eps_s")
        bias_loaded = g.sem("mix1_bias_loaded")
        loaded = g.sem("mix1_w_loaded")
        kv_bias_loaded = g.sem("mix1_kv_bias_loaded")
        kv_bias_free = g.sem("mix1_kv_bias_free")
        w_used = g.sem("mix1_w_used")
        projected = g.sem("mix1_projected")
        pe_s = g.sem("mix1_products")
        act_s = g.sem("mix1_acts")
        dve_s = g.sem("mix1_dve")
        ps = g.psum
        STEPS = 44
        at = {}
        with nc.Block() as block:
            @block.vector
            def _(dve):
                dve.sem_inc(dve_s, 1)
                with dve.Fori(0, KT) as p:
                    n = [0]

                    def step(op, name):
                        op.then_inc(dve_s, 1)
                        n[0] += 1
                        at[name] = n[0] + 1

                    def after(name):
                        dve.wait_ge(dve_s, STEPS * p + at[name])

                    dve.wait_ge(kv_bias_loaded, 32 * p + 32)
                    for b in range(5):
                        dve.wait_ge(projected, 6 * p + b + 2)
                        kvb = ps[3 + b][0:TT, 0:512].rearrange("p (t n m) -> p t n m", t=2, n=2)
                        for i, to in ((0, k), (1, v)):
                            step(dve.tensor_tensor(to[:, 2 * b:2 * b + 2], kvb[:, :, i], wide(bias_kv[:, i], 2), ALU.add), f"kv{b}")
                    dve.wait_ge(act_s, 10 * p + 3)
                    step(dve.tensor_scalar(q_eps[:, :], q[:, :], EPS, None, ALU.add), "q_eps")
                    step(dve.tensor_reduce(q_sum[:, 0:1], q_sums[:, :], AX_X, ALU.add), "q_sum")
                    after("q_sum")
                    step(dve.tensor_scalar(col_wide[:, 0], g.ones[:, 0:TT], q_sum[:, 0:1], None, ALU.mult), "q_sum_wide")
                    dve.wait_ge(act_s, 10 * p + 8)
                    step(dve.tensor_scalar(k_eps[:, :, :], k[:, :, :], EPS, None, ALU.add), "k_eps")
                    dve.wait_ge(pe_s, 12 * p + 1)
                    step(dve.scalar_tensor_tensor(out=ends[:, 0], in0=ps[3][:, 0:P], scalar=EPS, in1=g.pair_mask[:, :],
                                                  op0=ALU.add, op1=ALU.mult), "k_sum")
                    dve.wait_ge(pe_s, 12 * p + 2)
                    step(dve.tensor_scalar(row[:, 0], ps[4][0:TT, 0:P], EPS, None, ALU.add), "q_row")
                    after("q_row")
                    step(dve.tensor_tensor(prod[:, :, :], k_eps[:, :, :], wide(row[:, 0], NT), ALU.mult), "prod0")
                    after("prod0")
                    step(dve.tensor_reduce(outgoing[:, 0], prod[:, :, :].rearrange("p t (h d) -> p t h d", h=2), AX_X, ALU.add), "out0")
                    after("out0")
                    step(dve.tensor_scalar(outgoing[:, 1], outgoing[:, 0], EPS, None, ALU.add), "out1")
                    after("out1")
                    step(dve.reciprocal(outgoing[:, 2], outgoing[:, 1]), "out2")
                    after("out2")
                    for hh in range(2):
                        step(dve.tensor_copy(outgoing_wide[:, :, 64 * hh:64 * hh + 64],
                                             outgoing[:, 2, :, hh:hh + 1].broadcast_to([TT, NT, 64])), "outgoing")
                    for i, (c0, wd) in enumerate(CHUNKS):
                        dve.wait_ge(pe_s, 12 * p + 3 + i)
                        step(dve.tensor_scalar(sink_den[:, c0:c0 + wd], ps[5 + i][:, 0:wd], EPS, None, ALU.add), "sink_den")
                    after("sink_den")
                    step(dve.reciprocal(sink[:, :], sink_den[:, :]), "sink")
                    after("sink")
                    step(dve.tensor_tensor_reduce(junk[:, :], q[:, :], sink[:, :], 1.0, 0.0, ALU.mult, ALU.add, q_sum[:, 1:2]), "q_sink")
                    after("q_sink")
                    step(dve.tensor_scalar(col_wide[:, 1], g.ones[:, 0:TT], q_sum[:, 1:2], None, ALU.mult), "q_sink_wide")
                    dve.wait_ge(pe_s, 12 * p + 6)
                    step(dve.scalar_tensor_tensor(out=ends[:, 1], in0=ps[3][:, 0:P], scalar=EPS, in1=g.pair_mask[:, :],
                                                  op0=ALU.add, op1=ALU.mult), "k_out_sum")
                    dve.wait_ge(pe_s, 12 * p + 7)
                    step(dve.tensor_scalar(row[:, 1], ps[4][0:TT, 0:P], EPS, None, ALU.add), "q_sink_row")
                    after("q_sink_row")
                    step(dve.tensor_tensor(prod[:, :, :], k_eps[:, :, :], wide(row[:, 1], NT), ALU.mult), "prod1")
                    after("prod1")
                    step(dve.tensor_reduce(comp[:, 0], prod[:, :, :].rearrange("p t (h d) -> p t h d", h=2), AX_X, ALU.add), "comp0")
                    after("comp0")
                    step(dve.tensor_scalar(comp[:, 1], comp[:, 0], EPS, 1.0, ALU.add, ALU.min), "comp1")
                    after("comp1")
                    step(dve.tensor_scalar(comp[:, 2], comp[:, 1], -1.0, None, ALU.max), "comp2")
                    dve.wait_ge(act_s, 10 * p + 9)
                    for hh in range(2):
                        vh = v[:, :, 64 * hh:64 * hh + 64]
                        step(dve.tensor_tensor(vh, vh, outgoing[:, 3, :, hh:hh + 1].broadcast_to([TT, NT, 64]), ALU.mult), "v")
                    dve.wait_ge(pe_s, 12 * p + 8)
                    step(dve.reciprocal(factor[:, 0:2], ps[3][:, 0:2]), "inv")
                    after("inv")
                    for hh in range(2):
                        r = slice(64 * hh, 64 * hh + 64)
                        step(dve.tensor_scalar(factor[r, 2:3], factor[r, hh:hh + 1], float(N), None, ALU.mult), "factor")
                    after("factor")
                    dve.wait_ge(pe_s, 12 * p + 9)
                    step(dve.scalar_tensor_tensor(out=ends[:, 2], in0=ps[4][:, 0:P], scalar=factor[:, 2:3], in1=g.pair_mask[:, :],
                                                  op0=ALU.mult, op1=ALU.mult), "kv")
                    dve.wait_ge(act_s, 10 * p + 10)
                    step(dve.tensor_tensor(junk[:, :], sink[:, :], alloc[:, :], ALU.mult), "gain")
                    after("gain")
                    for i, (c0, wd) in enumerate(CHUNKS):
                        dve.wait_ge(pe_s, 12 * p + 10 + i)
                        step(dve.tensor_tensor(o_T[:, bass.ds(p, 1), c0:c0 + wd].squeeze(1), ps[i][:, 0:wd], junk[:, c0:c0 + wd], ALU.mult), "o")
                    assert n[0] == STEPS, n[0]

            @block.sync
            def _(sp):
                sp.dma_start(bias_q[:, :], b_qkv[0:D].rearrange("(m f) -> f m", f=P), allow_slow_non_contiguous=True).then_inc(bias_loaded, 16)
                with sp.Fori(0, KT) as p:
                    sp.wait_ge(w_used, p + 1)
                    for n in range(3):
                        sp.dma_start(w[:, :, n], w_qkv.rearrange("(k f) (n m) -> f k n m", f=P, n=3)[:, :, n, bass.ds(p * P, P)]).then_inc(loaded, 16)
                    sp.wait_ge(kv_bias_free, p + 1)
                    for n in range(2):
                        sp.dma_start(bias_kv[:, n], b_qkv.rearrange("(n m) -> n m", n=3)[n + 1:n + 2, bass.ds(p * P, P)].partition_broadcast(TT)).then_inc(kv_bias_loaded, 16)

            @block.gpsimd
            def _(pool):
                pool.memset(eps[:, :], EPS).then_inc(eps_s, 1)
                pool.sem_inc(w_used, 1)
                pool.sem_inc(kv_bias_free, 1)
                with pool.Fori(0, KT) as p:
                    pool.wait_ge(dve_s, STEPS * p + at["kv4"])
                    pool.sem_inc(kv_bias_free, 1)

            @block.tensor
            def _(pe):
                pe.wait_ge(eps_s, 1)
                with pe.Fori(0, KT) as p:
                    pe.wait_ge(loaded, 48 * p + 48)
                    pe.wait_ge(dve_s, STEPS * p + 1)
                    project_T(pe, ps[0:3], w[:, :, 0], src).then_inc(projected, 1)
                    for t in range(NT):
                        for kk in range(KT):
                            op = pe.matmul(ps[3 + t // 2][0:TT, (t % 2) * 256:(t % 2) * 256 + 256],
                                           src[:, kk, t * TT:(t + 1) * TT], w[:, kk, 1:3, :],
                                           start=(kk == 0), stop=(kk == KT - 1))
                        if t % 2:
                            op.then_inc(projected, 1)
                    pe.wait_ge(projected, 6 * p + 6)
                    pe.sem_inc(w_used, 1)

                    def made(name):
                        pe.wait_ge(dve_s, STEPS * p + at[name])

                    def by_tokens(bank_, rhs, width):
                        for t in range(NT):
                            op = pe.matmul(ps[bank_][:, 0:width], k[:, t], rhs(t), start=(t == 0), stop=(t == NT - 1))
                        op.then_inc(pe_s, 1)

                    pe.wait_ge(act_s, 10 * p + 8)
                    by_tokens(3, lambda t: g.ones[0:TT, :], P)
                    made("q_sum_wide")
                    pe.matmul(ps[4][0:TT, 0:P], col_wide[:, 0], g.ident[:, :], start=True, stop=True).then_inc(pe_s, 1)
                    made("k_sum")
                    for i, (c0, wd) in enumerate(CHUNKS):
                        pe.matmul(ps[5 + i][:, 0:wd], ends[:, 0], q_eps[:, c0:c0 + wd], start=True, stop=True).then_inc(pe_s, 1)
                    made("outgoing")
                    by_tokens(3, lambda t: outgoing_wide[:, t], P)
                    made("q_sink_wide")
                    pe.matmul(ps[4][0:TT, 0:P], col_wide[:, 1], g.ident[:, :], start=True, stop=True).then_inc(pe_s, 1)
                    made("k_out_sum")
                    for i, (c0, wd) in enumerate(CHUNKS):
                        op = pe.matmul(ps[5 + i][:, 0:wd], ends[:, 1], q_eps[:, c0:c0 + wd], start=True, stop=True)
                    pe.wait_ge(act_s, 10 * p + 9)
                    for t in range(NT):
                        op = pe.matmul(ps[3][:, 0:2], g.ones[0:TT, :], outgoing[:, 3, t], start=(t == 0), stop=(t == NT - 1))
                    op.then_inc(pe_s, 1)
                    made("v")
                    by_tokens(4, lambda t: v[:, t], P)
                    made("kv")
                    for i, (c0, wd) in enumerate(CHUNKS):
                        pe.matmul(ps[i][:, 0:wd], ends[:, 2], q[:, c0:c0 + wd], start=True, stop=True).then_inc(pe_s, 1)

            @block.scalar
            def _(act):
                act.wait_ge(bias_loaded, 16)
                act.wait_ge(eps_s, 1)
                with act.Fori(0, KT) as p:
                    act.wait_ge(projected, 6 * p + 1)
                    for i, (c0, wd) in enumerate(CHUNKS):
                        act.activation(q[:, c0:c0 + wd], ps[i][:, 0:wd], ACT.Sigmoid, bias=bias_q[:, bass.ds(p, 1)],
                                       accum_out=q_sums[:, i:i + 1]).then_inc(act_s, 1)
                    for b in range(5):
                        act.wait_ge(dve_s, STEPS * p + at[f"kv{b}"])
                        act.activation(k[:, 2 * b:2 * b + 2], k[:, 2 * b:2 * b + 2], ACT.Sigmoid).then_inc(act_s, 1)
                    act.wait_ge(dve_s, STEPS * p + at["comp2"])
                    act.activation(outgoing[:, 3], comp[:, 2], ACT.Exp).then_inc(act_s, 1)
                    act.wait_ge(pe_s, 12 * p + 8)
                    for i, (c0, wd) in enumerate(CHUNKS):
                        op = act.activation(alloc[:, c0:c0 + wd], ps[5 + i][:, 0:wd], ACT.Sigmoid, bias=eps[:, 0:1])
                    op.then_inc(act_s, 1)


def stage_attention(nc, g, w_qkv, b_qkv, src, o_T):
    g.new_stage()
    STEPS = 2 * NT
    NC = len(CHUNKS)
    CH = STEPS * NC
    MC = NT * NC
    with ExitStack() as c:
        w = g.sb(c, "att_w", [P, KT, 3, P], F32)
        bias_qk = g.sb(c, "att_bias_qk", [P, 2, KT], F32)
        bias_v = g.sb(c, "att_bias_v", [TT, 2, 64], F32)
        q_a = g.sb(c, "att_q_a", [P, 2, N], F32R)
        q_b = g.sb(c, "att_q_b", [P, 2, N], F32R)
        k_a = g.sb(c, "att_k_a", [P, 2, N], F32R)
        k_b = g.sb(c, "att_k_b", [P, 2, N], F32R)
        v = g.sb(c, "att_v", [TT, NT, 3, 64], F32)
        block_mask = g.sb(c, "att_block_mask", [NT, NT, TT], BF16)
        top = g.sb(c, "att_top", [TT, NT, NC], F32)
        neg_top = g.sb(c, "att_neg_top", [TT, NT], F32)
        prob = g.sb(c, "att_prob", [TT, 2, N], F32)
        raw = g.sb(c, "att_raw", [P, 2, N], F32)
        inv = g.sb(c, "att_inv", [P, N], F32)
        filled = g.sem("att_filled")
        bias_loaded = g.sem("att_bias_loaded")
        loaded = g.sem("att_w_loaded")
        v_bias_loaded = g.sem("att_v_bias_loaded")
        w_used = g.sem("att_w_used")
        projected = g.sem("att_projected")
        highs = g.sem("att_highs")
        copied = g.sem("att_q_b_copied")
        copy_turn = g.sem("att_copy_turn")
        lows = g.sem("att_lows")
        v_s = g.sem("att_v_s")
        sampled = g.sem("att_sampled")
        reduced = g.sem("att_reduced")
        maxed = g.sem("att_maxed")
        turned = g.sem("att_max_turned")
        shifts = g.sem("att_shifts")
        scored = g.sem("att_scored")
        exped = g.sem("att_exped")
        summed = g.sem("att_summed")
        taken = g.sem("att_taken")
        inverted = g.sem("att_inverted")
        done = g.sem("att_done")
        ps = g.psum
        THIRDS = ((0, 4), (4, 8), (8, 10))
        own = (slice(0, 64), slice(64, 128))
        other = (slice(64, 128), slice(0, 64))
        shift_rows = (slice(64, 64 + NT), slice(0, NT))
        with nc.Block() as block:
            @block.sync
            def _(sp):
                sp.dma_start(bias_qk[:, :, :], b_qkv[0:2 * D].rearrange("(n m f) -> f n m", f=P, n=2), allow_slow_non_contiguous=True).then_inc(bias_loaded, 16)
                with sp.Fori(0, KT) as p:
                    sp.wait_ge(w_used, p + 1)
                    for n in range(3):
                        sp.dma_start(w[:, :, n], w_qkv.rearrange("(k f) (n m) -> f k n m", f=P, n=3)[:, :, n, bass.ds(p * P, P)]).then_inc(loaded, 16)
                    sp.wait_ge(v_s, 3 * p + 1)
                    sp.dma_start(bias_v[:, :, :].rearrange("p h e -> p (h e)"),
                                 b_qkv.rearrange("(n m) -> n m", n=3)[2:3, bass.ds(p * P, P)].partition_broadcast(TT)).then_inc(v_bias_loaded, 16)

            @block.gpsimd
            def _(pool):
                pool.sem_inc(w_used, 1)
                fills = [(v[:, :, 1], 1.0), (block_mask[:, :, :], 0.0)]
                for h in range(2):
                    fills += [(q_b[other[h], h].bitcast(F32), 0.0), (k_b[other[h], h].bitcast(F32), 0.0),
                              (k_b[shift_rows[h], h].bitcast(F32), 1.0)]
                for n, (to, value) in enumerate(fills):
                    pool.memset(to, value).then_inc(filled, 1)
                    pool.wait_ge(filled, n + 1)
                pool.affine_select(out=block_mask[:, :, :], in_=block_mask[:, :, :], compare_op=ALU.not_equal, fill=1.0,
                                   base=0, pattern=[[-1, NT], [0, TT]], channel_multiplier=1).then_inc(filled, 1)
                pool.wait_ge(filled, 9)
                with pool.Fori(0, KT) as p:
                    pool.wait_ge(highs, 2 * p + 1)
                    pool.sem_inc(copy_turn, 1)
                    for h in range(2):
                        pool.tensor_copy(q_b[own[h], h], q_a[own[h], h]).then_inc(copied, 1)
                    pool.wait_ge(copied, 2 * p + 2)

            @block.tensor
            def _(pe):
                pe.wait_ge(filled, 9)
                with pe.Fori(0, KT) as p:
                    pe.wait_ge(loaded, 48 * p + 48)
                    pe.wait_ge(exped, CH * p + NC)
                    project_T(pe, ps[3:6], w[:, :, 0], src).then_inc(projected, 1)
                    pe.wait_ge(taken, 2 * p + 1)
                    project_T(pe, ps[0:3], w[:, :, 1], src).then_inc(projected, 1)
                    pe.wait_ge(lows, 3 * p + 1)

                    def project_v(t):
                        b = t // 4
                        for kk in range(KT):
                            op = pe.matmul(ps[3 + b][0:TT, (t % 4) * P:(t % 4 + 1) * P], src[:, kk, t * TT:(t + 1) * TT],
                                           w[:, kk, 2], start=(kk == 0), stop=(kk == KT - 1))
                        if t + 1 == THIRDS[b][1]:
                            op.then_inc(projected, 1)

                    def sample(s):
                        h, t, n = s // MC, s % MC // NC, s % NC
                        c0, wd = CHUNKS[n]
                        if s == 0:
                            pe.wait_ge(lows, 3 * p + 2)
                        if s == MC:
                            pe.wait_ge(shifts, 2 * p + 1)
                        pe.wait_ge(reduced, CH * p + s + 1)
                        pe.matmul(ps[6 + s % 2][0:TT, 0:wd], q_a[:, h, t * TT:(t + 1) * TT], k_a[:, h, c0:c0 + wd],
                                  start=True, stop=True).then_inc(sampled, 1)

                    def turn_maxima(h):
                        pe.wait_ge(maxed, 2 * p + h + 1)
                        pe.matmul(ps[6][0:NT, 0:TT], neg_top[:, :], g.ident[0:TT, 0:TT], start=True, stop=True).then_inc(turned, 1)

                    def scores(i):
                        h, j = i // NT, i % NT
                        if i == 0:
                            pe.wait_ge(lows, 3 * p + 3)
                            pe.wait_ge(copied, 2 * p + 2)
                            pe.wait_ge(v_s, 3 * p + 4)
                        if j == 0:
                            pe.wait_ge(shifts, 2 * p + h + 1)
                        for n, (c0, wd) in enumerate(CHUNKS):
                            pe.wait_ge(exped, CH * p + NC * i + n + 1)
                            pe.matmul(ps[3 + n][0:TT, 0:wd], k_a[:, h, j * TT:(j + 1) * TT], q_a[:, h, c0:c0 + wd], start=True, stop=False)
                            pe.matmul(ps[3 + n][0:TT, 0:wd], k_b[:, h, j * TT:(j + 1) * TT], q_b[:, h, c0:c0 + wd],
                                      start=False, stop=True).then_inc(scored, 1)

                    def weigh(i, n):
                        h, j = i // NT, i % NT
                        c0, wd = CHUNKS[n]
                        if n == 0:
                            pe.wait_ge(exped, CH * p + NC * i + 2 * NC)
                            if j == 0:
                                pe.wait_ge(taken, 2 * p + h + 1)
                        op = pe.matmul(ps[n][:, 0:wd], v[:, j, h:h + 2], prob[:, i % 2, c0:c0 + wd], start=(j == 0), stop=(j == NT - 1))
                        if n == NC - 1:
                            op.then_inc(summed, 1)

                    AHEAD = 4
                    for t in range(AHEAD):
                        project_v(t)
                    for t in range(NT):
                        for n in range(NC):
                            sample(t * NC + n)
                        if t + AHEAD < NT:
                            project_v(t + AHEAD)
                        if t + AHEAD == NT:
                            pe.wait_ge(projected, 5 * p + 5)
                            pe.sem_inc(w_used, 1)
                    turn_maxima(0)
                    s = MC
                    scores(0)
                    for i in range(STEPS):
                        if i + 1 < STEPS:
                            scores(i + 1)
                        for n in range(NC):
                            for _ in range(2 if n == 1 else 1):
                                if s < CH:
                                    sample(s)
                                    s += 1
                            weigh(i, n)
                        if i == NT - 3:
                            turn_maxima(1)

            @block.scalar
            def _(act):
                act.sem_inc(exped, NC)
                act.sem_inc(taken, 1)
                act.wait_ge(bias_loaded, 16)
                with act.Fori(0, KT) as p:
                    for i, (to, b0) in enumerate(((q_a, 3), (k_a, 0))):
                        act.wait_ge(projected, 5 * p + i + 1)
                        for n, (c0, wd) in enumerate(CHUNKS):
                            for h in range(2):
                                op = act.activation(to[own[h], h, c0:c0 + wd], ps[b0 + n][own[h], 0:wd], ACT.Identity,
                                                    bias=bias_qk[own[h], i, bass.ds(p, 1)])
                        op.then_inc(highs, 1)

                    def take(h):
                        act.wait_ge(summed, STEPS * p + NT * (h + 1) + 2)
                        act.wait_ge(done, 2 * p + h + 1)
                        for n, (c0, wd) in enumerate(CHUNKS):
                            op = act.activation(raw[:, h, c0:c0 + wd], ps[n][:, 0:wd], ACT.Copy)
                        op.then_inc(taken, 1)

                    for i in range(STEPS):
                        act.wait_ge(summed, STEPS * p + i + 1)
                        for n, (c0, wd) in enumerate(CHUNKS):
                            act.wait_ge(scored, CH * p + NC * i + n + 1)
                            act.activation(prob[:, i % 2, c0:c0 + wd], ps[3 + n][0:TT, 0:wd], ACT.Exp, scale=0.125).then_inc(exped, 1)
                        if i == NT:
                            take(0)
                    take(1)

            @block.vector
            def _(dve):
                dve.sem_inc(reduced, 2)
                dve.sem_inc(summed, 2)
                dve.sem_inc(v_s, 1)
                dve.sem_inc(done, 2)
                dve.wait_ge(bias_loaded, 16)
                dve.wait_ge(filled, 9)
                with dve.Fori(0, KT) as p:
                    def low(i, to, high, b0, half):
                        for n, (c0, wd) in enumerate(CHUNKS):
                            for h in range(2):
                                op = dve.scalar_tensor_tensor(out=to[half[h], h, c0:c0 + wd], in0=ps[b0 + n][own[h], 0:wd],
                                                              scalar=bias_qk[own[h], i, bass.ds(p, 1)],
                                                              in1=high[own[h], h, c0:c0 + wd].bitcast(F32),
                                                              op0=ALU.add, op1=ALU.subtract)
                        op.then_inc(lows, 1)

                    dve.wait_ge(highs, 2 * p + 1)
                    low(0, q_a, q_a, 3, other)
                    dve.wait_ge(highs, 2 * p + 2)
                    for h in range(2):
                        op = dve.tensor_copy(k_a[other[h], h], k_a[own[h], h])
                    op.then_inc(lows, 1)
                    low(1, k_b, k_a, 0, own)
                    dve.wait_ge(v_bias_loaded, 16 * p + 16)

                    def keep_v(b):
                        t0, t1 = THIRDS[b]
                        dve.wait_ge(projected, 5 * p + b + 3)
                        dve.tensor_tensor(v[:, t0:t1, 0:3:2], ps[3 + b][0:TT, 0:(t1 - t0) * P].rearrange("p (t h e) -> p t h e", h=2, e=64),
                                          bias_v[:, :, :].unsqueeze(1).broadcast_to([TT, t1 - t0, 2, 64]), ALU.add).then_inc(v_s, 1)

                    def most(s):
                        wd = CHUNKS[s % NC][1]
                        dve.wait_ge(sampled, CH * p + s + 1)
                        dve.tensor_reduce(top[:, s % MC // NC, s % NC:s % NC + 1], ps[6 + s % 2][0:TT, 0:wd], AX_X, ALU.max).then_inc(reduced, 1)

                    def shift(h):
                        dve.wait_ge(reduced, CH * p + MC * (h + 1) + 2)
                        dve.tensor_reduce(neg_top[:, :], top[:, :, :], AX_X, ALU.max, negate=True).then_inc(maxed, 1)
                        dve.wait_ge(turned, 2 * p + h + 1)
                        dve.tensor_tensor(q_b[shift_rows[h], h].rearrange("p (t n) -> p t n", n=TT), wide(ps[6][0:NT, 0:TT], NT),
                                          block_mask[:, :, :], ALU.mult).then_inc(shifts, 1)

                    def finish(h):
                        dve.wait_ge(taken, 2 * p + h + 2)
                        dve.reciprocal(inv[own[h], :], raw[other[h], h]).then_inc(inverted, 1)
                        dve.wait_ge(inverted, 2 * p + h + 1)
                        dve.tensor_tensor(o_T[own[h], bass.ds(p, 1), :].squeeze(1), raw[own[h], h], inv[own[h], :], ALU.mult).then_inc(done, 1)

                    keep_v(0)
                    for s in range(MC):
                        most(s)
                        if s == 4 * NC:
                            keep_v(1)
                        if s == 7 * NC:
                            keep_v(2)
                    shift(0)
                    for s in range(MC, CH):
                        most(s)
                    shift(1)
                    finish(0)
                    finish(1)


def stage_gates(nc, g, gate_w, b2, src, z_T):
    g.new_stage()
    NE = 8
    with ExitStack() as c:
        wg = g.sb(c, "gates_w", [P, KT, NE], F32)
        b2_sb = g.sb(c, "gates_b2", [NE, D], F32)
        logit = g.sb(c, "gates_logit", [TT, NT, NE], F32)
        above = g.sb(c, "gates_above", [TT, NT, NE, NE], F32)
        equal = g.sb(c, "gates_equal", [TT, NT, NE, NE], F32)
        lower = g.sb(c, "gates_lower", [TT, NE, NE], F32)
        rank = g.sb(c, "gates_rank", [TT, NT, NE], F32)
        top = g.sb(c, "gates_top", [TT, NT, 3], F32)
        diff = g.sb(c, "gates_diff", [TT, NT, NE], F32)
        gate = g.sb(c, "gates_gate", [TT, NT, NE], F32)
        rows = g.sb(c, "gates_rows", [NE, N], F32)
        loaded = g.sem("gates_loaded")
        lower_s = g.sem("gates_lower_s")
        logits = g.sem("gates_logits")
        chain = g.sem("gates_chain")
        diffed = g.sem("gates_diffed")
        exped = g.sem("gates_exped")
        gated = g.sem("gates_gated")
        turned = g.sem("gates_turned")
        row_kept = g.sem("gates_row_kept")
        stored = g.sem("gates_stored")
        biased = g.sem("gates_biased")
        added = g.sem("gates_added")
        ps = g.psum
        with nc.Block() as block:
            @block.sync
            def _(sp):
                sp.dma_start(wg[:, :, :], gate_w.rearrange("(k f) e -> f k e", f=P)).then_inc(loaded, 16)
                sp.dma_start(b2_sb[:, :], b2).then_inc(loaded, 16)
                sp.wait_ge(row_kept, NT)
                sp.dma_start(g.gates_dram, rows[:, :]).then_inc(stored, 16)
                sp.wait_ge(stored, 16)

            @block.gpsimd
            def _(pool):
                pool.memset(lower[:, :, :], 1.0).then_inc(lower_s, 1)
                pool.wait_ge(lower_s, 1)
                pool.affine_select(out=lower[:, :, :], in_=lower[:, :, :], compare_op=ALU.is_gt, fill=0.0,
                                   base=0, pattern=[[1, NE], [-1, NE]], channel_multiplier=0).then_inc(lower_s, 1)

            @block.tensor
            def _(pe):
                pe.wait_ge(loaded, 32)
                for t in range(NT):
                    for k in range(KT):
                        op = pe.matmul(ps[0][0:TT, t * NE:(t + 1) * NE], src[:, k, t * TT:(t + 1) * TT], wg[:, k],
                                       start=(k == 0), stop=(k == KT - 1))
                op.then_inc(logits, 1)
                pe.wait_ge(gated, 1)
                for t in range(NT):
                    if t >= 2:
                        pe.wait_ge(row_kept, t - 1)
                    pe.transpose(ps[t % 2][0:NE, 0:TT], gate[:, t], g.ident[0:TT, 0:TT]).then_inc(turned, 1)
                pe.wait_ge(row_kept, NT)
                for m in range(KT):
                    if m >= 2:
                        pe.wait_ge(added, m - 1)
                    for n, (c0, wd) in enumerate(CHUNKS):
                        op = pe.matmul(ps[2 + 3 * (m % 2) + n][:, 0:wd], b2_sb[:, m * P:(m + 1) * P], rows[:, c0:c0 + wd], start=True, stop=True)
                    op.then_inc(biased, 1)

            @block.scalar
            def _(act):
                act.wait_ge(diffed, 1)
                act.activation(diff[:, :, :], diff[:, :, :], ACT.Exp).then_inc(exped, 1)

            @block.vector
            def _(dve):
                n = [0]

                def step(op):
                    n[0] += 1
                    op.then_inc(chain, 1)
                    dve.wait_ge(chain, n[0])

                dve.wait_ge(logits, 1)
                step(dve.tensor_copy(logit[:, :, :], ps[0][0:TT, 0:NT * NE].rearrange("p (t e) -> p t e", e=NE)))
                step(dve.tensor_reduce(top[:, :, 0:1], logit[:, :, :], AX_X, ALU.max))
                dve.tensor_tensor(diff[:, :, :], logit[:, :, :], top[:, :, 0:1].broadcast_to([TT, NT, NE]), ALU.subtract).then_inc(diffed, 1)
                of_f = logit[:, :, :].unsqueeze(2).broadcast_to([TT, NT, NE, NE])
                of_e = logit[:, :, :].unsqueeze(3).broadcast_to([TT, NT, NE, NE])
                step(dve.tensor_tensor(above[:, :, :, :], of_f, of_e, ALU.is_gt))
                step(dve.tensor_tensor(equal[:, :, :, :], of_f, of_e, ALU.is_equal))
                dve.wait_ge(lower_s, 2)
                step(dve.tensor_tensor(equal[:, :, :, :], equal[:, :, :, :], lower[:, :, :].unsqueeze(1).broadcast_to([TT, NT, NE, NE]), ALU.mult))
                step(dve.tensor_tensor(above[:, :, :, :], above[:, :, :, :], equal[:, :, :, :], ALU.add))
                step(dve.tensor_reduce(rank[:, :, :], above[:, :, :, :], AX_X, ALU.add))
                dve.wait_ge(exped, 1)
                step(dve.scalar_tensor_tensor(out=diff[:, :, :], in0=rank[:, :, :], scalar=2.0, in1=diff[:, :, :], op0=ALU.is_lt, op1=ALU.mult))
                step(dve.tensor_reduce(top[:, :, 1:2], diff[:, :, :], AX_X, ALU.add))
                step(dve.reciprocal(top[:, :, 2:3], top[:, :, 1:2]))
                dve.tensor_tensor(gate[:, :, :], diff[:, :, :], top[:, :, 2:3].broadcast_to([TT, NT, NE]), ALU.mult).then_inc(gated, 1)
                for t in range(NT):
                    dve.wait_ge(turned, t + 1)
                    dve.tensor_copy(rows[:, t * TT:(t + 1) * TT], ps[t % 2][0:NE, 0:TT]).then_inc(row_kept, 1)
                for m in range(KT):
                    dve.wait_ge(biased, m + 1)
                    for i, (c0, wd) in enumerate(CHUNKS):
                        op = dve.tensor_tensor(z_T[:, m, c0:c0 + wd], z_T[:, m, c0:c0 + wd], ps[2 + 3 * (m % 2) + i][:, 0:wd], ALU.add)
                    op.then_inc(added, 1)


def stage_experts(nc, g, w1, b1, w2, src, z_T):
    g.new_stage()
    NE, HT = 8, 3
    with ExitStack() as c:
        w1_sb = g.sb(c, "exp_w1", [P, KT, HT * P], F32)
        w2_sb = g.sb(c, "exp_w2", [P, HT, D], F32)
        b1_sb = g.sb(c, "exp_b1", [P, NE, HT], F32)
        gate = g.sb(c, "exp_gate", [P, N], F32)
        hid = g.sb(c, "exp_hid", [P, HT, N], F32)
        gated_sb = g.sb(c, "exp_gated", [P, HT, N], F32)
        b1_loaded = g.sem("exp_b1_loaded")
        w1_loaded = g.sem("exp_w1_loaded")
        w2_loaded = g.sem("exp_w2_loaded")
        gate_loaded = g.sem("exp_gate_loaded")
        up = g.sem("exp_up")
        made = g.sem("exp_made")
        gated = g.sem("exp_gated_s")
        down = g.sem("exp_down")
        drained = g.sem("exp_drained")
        ps = g.psum
        w1_v = w1.rearrange("e (k f) m -> f e k m", f=P)
        w2_v = w2.rearrange("e (k f) m -> f e k m", f=P)
        with nc.Block() as block:
            @block.sync
            def _(sp):
                sp.dma_start(w1_sb[:, :, :], w1_v[:, 0]).then_inc(w1_loaded, 16)
                sp.dma_start(b1_sb[:, :, :], b1.rearrange("e (m f) -> f e m", f=P), allow_slow_non_contiguous=True).then_inc(b1_loaded, 16)
                sp.dma_start(gate[:, :], g.gates_dram[0:1, :].partition_broadcast(P)).then_inc(gate_loaded, 16)
                sp.dma_start(w2_sb[:, :, :], w2_v[:, 0]).then_inc(w2_loaded, 16)
                with sp.Fori(1, NE) as e:
                    sp.wait_ge(up, HT * e)
                    sp.dma_start(w1_sb[:, :, :], w1_v[:, bass.ds(e, 1)].squeeze(1)).then_inc(w1_loaded, 16)
                    sp.wait_ge(gated, HT * e)
                    sp.dma_start(gate[:, :], g.gates_dram[bass.ds(e, 1), :].partition_broadcast(P)).then_inc(gate_loaded, 16)
                    sp.wait_ge(down, KT * e + 1)
                    sp.dma_start(w2_sb[:, :, :], w2_v[:, bass.ds(e, 1)].squeeze(1)).then_inc(w2_loaded, 16)

            @block.gpsimd
            def _(pool):
                pool.sem_inc(down, 1)
                pool.sem_inc(drained, 2)

            @block.tensor
            def _(pe):
                with pe.Fori(0, NE) as e:
                    pe.wait_ge(w1_loaded, 16 * e + 16)
                    for m in range(HT):
                        b = 3 * (m % 2)
                        if m == 0:
                            pe.wait_ge(drained, KT * e + 2)
                        if m == 2:
                            pe.wait_ge(made, HT * e + 1)
                        for k in range(KT):
                            for n, (c0, wd) in enumerate(CHUNKS):
                                op = pe.matmul(ps[b + n][:, 0:wd], w1_sb[:, k, m * P:(m + 1) * P], src[:, k, c0:c0 + wd],
                                               start=(k == 0), stop=(k == KT - 1))
                        op.then_inc(up, 1)
                    pe.wait_ge(w2_loaded, 16 * e + 16)
                    for m in range(KT):
                        b = 3 * ((HT + m) % 2)
                        if m < 2:
                            pe.wait_ge(gated, HT * e + HT)
                        else:
                            pe.wait_ge(drained, KT * e + m + 1)
                        for k in range(HT):
                            for n, (c0, wd) in enumerate(CHUNKS):
                                op = pe.matmul(ps[b + n][:, 0:wd], w2_sb[:, k, m * P:(m + 1) * P], gated_sb[:, k, c0:c0 + wd],
                                               start=(k == 0), stop=(k == HT - 1))
                        op.then_inc(down, 1)

            @block.scalar
            def _(act):
                act.wait_ge(b1_loaded, 16)
                with act.Fori(0, NE) as e:
                    for m in range(HT):
                        act.wait_ge(up, HT * e + m + 1)
                        for n, (c0, wd) in enumerate(CHUNKS):
                            op = act.activation(hid[:, m, c0:c0 + wd], ps[3 * (m % 2) + n][:, 0:wd], ACT.Gelu,
                                                bias=b1_sb[:, bass.ds(e, 1), m:m + 1].squeeze(1))
                        op.then_inc(made, 1)

            @block.vector
            def _(dve):
                with dve.Fori(0, NE) as e:
                    dve.wait_ge(gate_loaded, 16 * e + 16)
                    for m in range(HT):
                        dve.wait_ge(made, HT * e + m + 1)
                        dve.wait_ge(down, KT * e + 1)
                        dve.tensor_tensor(gated_sb[:, m], hid[:, m], gate[:, :], ALU.mult).then_inc(gated, 1)
                    for m in range(KT):
                        dve.wait_ge(down, KT * e + m + 2)
                        dve.wait_ge(drained, KT * e + m + 2)
                        for n, (c0, wd) in enumerate(CHUNKS):
                            op = dve.tensor_tensor(z_T[:, m, c0:c0 + wd], z_T[:, m, c0:c0 + wd],
                                                   ps[3 * ((HT + m) % 2) + n][:, 0:wd], ALU.add)
                        op.then_inc(drained, 1)


class Ground:

    def __init__(self, nc, ctx):
        self.nc = nc
        self.stage_sems, self.cleared_sems = [], []
        self.psum = [ctx.enter_context(nc.psum_tensor(f"bank{i}", [P, 512], F32)) for i in range(8)]
        self.ident = self.sb(ctx, "ident", [P, P], F32)
        self.ones = self.sb(ctx, "ones", [P, P], F32)
        self.pair_mask = self.sb(ctx, "pair_mask", [P, P], F32)
        self.eps5 = self.sb(ctx, "eps5", [P, 1], F32)
        self.no_edge = None

    def sb(self, ctx, name, shape, dt):
        return ctx.enter_context(self.nc.sbuf_tensor(name, shape, dt))

    def sem(self, name):
        s = self.nc.alloc_semaphore(name)
        self.stage_sems.append(s)
        return s

    def new_stage(self):
        for s in self.cleared_sems:
            self.nc.release_semaphore(s)
        for s in self.stage_sems:
            self.nc.gpsimd.sem_clear(s)
        self.cleared_sems, self.stage_sems = self.stage_sems, []


def program(nc, x, src, dst, W, out, until=None):
    with ExitStack() as ctx:
        g = Ground(nc, ctx)
        stage_constants(nc, g)
        g.x_T = g.sb(ctx, "x_T", [P, KT, N], F32)
        g.y_T = g.sb(ctx, "y_T", [P, KT, N], F32)
        counts_memory, gat_memory, no_edge_memory = (ctx.enter_context(ExitStack()) for _ in range(3))
        g.counts_T = g.sb(counts_memory, "counts_T", [TT, NT, N], F32)
        g.ft = g.sb(gat_memory, "ft", [TT, NT, KT, P], F32)
        g.a_cols = g.sb(gat_memory, "a_cols", [TT, NT, 2, H], F32)
        g.a1_fifth = g.sb(gat_memory, "a1_fifth", [TT, NT, H], F32)
        g.w_res = g.sb(gat_memory, "w_res", [P, P], F32)
        g.no_edge = g.sb(no_edge_memory, "no_edge", [TT, NT, N], BF16)
        stage_adjacency(nc, g, src, dst)
        stage_load(nc, g, x)
        stage_norm(nc, g, "ln0", g.x_T, g.y_T)
        if until == "ln0":
            g.x_T = g.y_T
            return stage_store(nc, g, out)
        g.a1_dram = nc.dram_tensor("a1_rows_dram", (H, N), F32).ap()
        g.uv_dram = nc.dram_tensor("uv_rows_dram", (2 * H, N), F32).ap()
        stage_gat_project(nc, g, W)
        stage_gat_max(nc, g)
        no_edge_memory.close()
        stage_gat_attend(nc, g)
        gat_memory.close()
        if until == "gat":
            return stage_store(nc, g, out)
        with ExitStack() as c:
            o_T = g.sb(c, "o_T", [P, KT, N], F32)
            stage_mix0(nc, g, W["L0_mix_w_qkv"], g.y_T, o_T)
            stage_linear(nc, g, "mix0_proj", W["L0_mix_w_proj"], W["L0_mix_b_proj"], o_T, KT, KT, ACT.Identity, add_to=g.x_T)
        if until == "mix0":
            return stage_store(nc, g, out)
        stage_norm(nc, g, "ln1", g.x_T, g.y_T)
        with ExitStack() as c:
            weight = g.sb(c, "ffn0_weight", [P, 1], F32)
            expert = g.sb(c, "ffn0_expert", [P, 1], I32)
            hid_T = g.sb(c, "ffn0_hid_T", [P, 3, N], F32)
            stage_choose(nc, g, W["L0_ffn_Wg"], g.y_T, weight[:, :], expert[:, :])
            stage_linear(nc, g, "ffn0_up", W["L0_ffn_W1"], W["L0_ffn_b1"], g.y_T, KT, 3, ACT.Gelu, dst=hid_T, expert=expert[0:1, 0:1])
            stage_linear(nc, g, "ffn0_down", W["L0_ffn_W2"], W["L0_ffn_b2"], hid_T, 3, KT, ACT.Identity, add_to=g.x_T,
                         times=weight[:, 0:1], expert=expert[0:1, 0:1])
        if until == "ffn0":
            return stage_store(nc, g, out)
        stage_norm(nc, g, "ln2", g.x_T, g.y_T)
        stage_gcn(nc, g, W["L1_gnn_W"], W["L1_gnn_b"], g.y_T, g.x_T)
        if until == "gcn":
            return stage_store(nc, g, out)
        counts_memory.close()
        with ExitStack() as c:
            o_T = g.sb(c, "o_T1", [P, KT, N], F32)
            stage_mix1(nc, g, W["L1_mix_W_qkv"], W["L1_mix_b_qkv"], g.y_T, o_T)
            stage_linear(nc, g, "mix1_proj", W["L1_mix_W_proj"], W["L1_mix_b_proj"], o_T, KT, KT, ACT.Sigmoid, add_to=g.x_T, scale=2.0)
        if until == "mix1":
            return stage_store(nc, g, out)
        g.z_T = g.sb(ctx, "z_T", [P, KT, N], F32)
        stage_norm(nc, g, "ln3", g.x_T, g.z_T)
        stage_norm(nc, g, "ln4", g.z_T, g.y_T, W["L1_ffn_ln1_g"], W["L1_ffn_ln1_b"])
        with ExitStack() as c:
            o_T = g.sb(c, "o_T2", [P, KT, N], F32)
            stage_attention(nc, g, W["L1_ffn_qkv_w"], W["L1_ffn_qkv_b"], g.y_T, o_T)
            stage_linear(nc, g, "att_proj", W["L1_ffn_proj_w"], W["L1_ffn_proj_b"], o_T, KT, KT, ACT.Identity, add_to=g.z_T)
        stage_norm(nc, g, "ln5", g.z_T, g.y_T, W["L1_ffn_ln2_g"], W["L1_ffn_ln2_b"])
        g.gates_dram = nc.dram_tensor("gates_dram", (8, N), F32).ap()
        stage_gates(nc, g, W["L1_ffn_gate_w"], W["L1_ffn_b2"], g.y_T, g.z_T)
        stage_experts(nc, g, W["L1_ffn_w1"], W["L1_ffn_b1"], W["L1_ffn_w2"], g.y_T, g.z_T)
        stage_store(nc, g, out, add=g.z_T)


_INS = ['x', 'src', 'dst', 'L0_gnn_W_fc', 'L0_gnn_attn_l', 'L0_gnn_attn_r', 'L0_gnn_W_res', 'L0_mix_w_qkv', 'L0_mix_w_proj', 'L0_mix_b_proj', 'L0_ffn_Wg', 'L0_ffn_W1', 'L0_ffn_b1', 'L0_ffn_W2', 'L0_ffn_b2', 'L1_gnn_W', 'L1_gnn_b', 'L1_mix_W_qkv', 'L1_mix_b_qkv', 'L1_mix_W_proj', 'L1_mix_b_proj', 'L1_ffn_ln1_g', 'L1_ffn_ln1_b', 'L1_ffn_qkv_w', 'L1_ffn_qkv_b', 'L1_ffn_proj_w', 'L1_ffn_proj_b', 'L1_ffn_ln2_g', 'L1_ffn_ln2_b', 'L1_ffn_gate_w', 'L1_ffn_w1', 'L1_ffn_b1', 'L1_ffn_w2', 'L1_ffn_b2']


def kernel(**inputs):
    import numpy as _np
    import concourse.bacc as _bacc
    from concourse import mybir as _mybir
    from concourse.bass_utils import run_bass_kernel_spmd as _run

    nc = _bacc.Bacc("TRN2", target_bir_lowering=False, num_devices=1)
    arrays, W = {}, {}
    for name in _INS:
        a = _np.ascontiguousarray(inputs[name])
        arrays[f"in_{name}_dram"] = a
        W[name] = nc.dram_tensor(f"in_{name}_dram", a.shape, _mybir.dt.from_np(a.dtype), kind="ExternalInput").ap()
    out = nc.dram_tensor("out_0_dram", (N, D), F32, kind="ExternalOutput").ap()
    program(nc, W["x"], W["src"], W["dst"], W, out)
    r = _run(nc, [arrays], core_ids=[0])
    return r.results[0]["out_0_dram"]
```

```python
from contextlib import ExitStack

import concourse.bass as bass
from concourse import mybir

F32 = mybir.dt.float32
F16 = mybir.dt.float16
F32R = mybir.dt.float32r
BF16 = mybir.dt.bfloat16
I32 = mybir.dt.int32
ALU = mybir.AluOpType
ACT = mybir.ActivationFunctionType
AX_X = mybir.AxisListType.X

P = 128
N = 1250
D = 768
KT = D // P
TT = 125
NT = N // TT
H = 12
E = 41250
EG = 5
ES = E // (TT * EG)
CHUNKS = ((0, 418), (418, 416), (834, 416))
CW = 418
BIG = 3.0e38
FAR = 2.0 ** 110
LN_EPS = 1e-5


def bank(banks, i):
    return banks[i]


def wide(ap, n):
    return ap.unsqueeze(1).broadcast_to([ap.shape[0], n, ap.shape[1]])


def stage_constants(nc, g):
    g.new_stage()
    with nc.Block() as block:
        filled = g.sem("const_filled")
        done = g.sem("const_done")

        @block.gpsimd
        def _(pool):
            pool.memset(g.ident[:, :], 0.0).then_inc(filled, 1)
            pool.memset(g.ones[:, :], 1.0).then_inc(filled, 1)
            pool.memset(g.pair_mask[:, :], 0.0).then_inc(filled, 1)
            pool.memset(g.eps5[:, :], LN_EPS).then_inc(filled, 1)
            pool.memset(g.far[:, :], FAR).then_inc(filled, 1)
            pool.wait_ge(filled, 5)
            pool.affine_select(out=g.ident[:, :], in_=g.ident[:, :], compare_op=ALU.not_equal, fill=1.0,
                               base=0, pattern=[[-1, P]], channel_multiplier=1).then_inc(done, 1)

        @block.vector
        def _(dve):
            dve.wait_ge(filled, 5)
            dve.memset(g.pair_mask[0:64, 0:64], 1.0).then_inc(done, 1)
            dve.memset(g.pair_mask[64:128, 64:128], 1.0).then_inc(done, 1)


def stage_adjacency(nc, g, src, dst, x):
    g.new_stage()
    with ExitStack() as c:
        edge_rows = g.sb(c, "edge_rows", [ES, 2, EG, TT], I32)
        edge_f = g.sb(c, "edge_f", [ES, 2, EG, TT], F32)
        edge_cols = g.sb(c, "edge_cols", [TT, 2, EG, ES], F32)
        node_ids = g.sb(c, "node_ids", [TT, N], I32)
        node_ids16 = g.sb(c, "node_ids16", [TT, N], F16)
        tile_range = g.sb(c, "tile_range", [ES, 2], F32)
        range_rows = g.sb(c, "range_rows", [NT, 2, ES], F32)
        tile_ids = g.sb(c, "tile_ids", [NT, 2, ES], I32)
        tile_idf = g.sb(c, "tile_idf", [NT, 2, ES], F32)
        block_lo_i = g.sb(c, "block_lo_i", [NT, 2], I32)
        block_lo = g.sb(c, "block_lo", [NT, 2], F32)
        touches = g.sb(c, "touches", [NT, ES], F32)
        first_last = g.sb(c, "first_last", [NT, 6], F32)
        before = g.sb(c, "before", [NT, NT], F32)
        loop_f = g.sb(c, "loop_f", [NT, 3], F32)
        loop_i = g.sb(c, "loop_i", [NT, 3], I32)
        loop_row = g.sb(c, "loop_row", [1, NT * 3], I32)
        zeros = g.sb(c, "zeros", [TT, TT], BF16)
        SLOTS = 2
        hot_dst = g.sb(c, "hot_dst", [TT, SLOTS, EG, TT], BF16)
        hot_src = g.y_T[:, :, :].rearrange("p k n -> p (k n)")[0:TT, 0:SLOTS * EG * N // 2].bitcast(BF16).rearrange(
            "p (s e n) -> p s e n", s=SLOTS, e=EG)
        staged = g.sb(c, "staged", [TT, N], F32)

        loaded = g.sem("adj_loaded")
        made = g.sem("adj_ids_made")
        floats = g.sem("adj_floats")
        turned = g.sem("adj_turned")
        vec = g.sem("adj_vec")
        cnt = g.sem("adj_cumulative")
        ranged = g.sem("adj_ranges_stored")
        hots = g.sem("adj_onehots")
        used = g.sem("adj_onehots_used")
        counted = g.sem("adj_counted")
        staged_s = g.sem("adj_staged")
        turned_t = g.sem("adj_counts_turned")
        kept = g.sem("adj_kept")
        masked_s = g.sem("adj_masked")
        x_loaded = g.sem("adj_x_loaded")
        ps = g.psum

        with nc.Block() as block:
            @block.sync
            def _(sp):
                for n, e in ((0, src), (1, dst)):
                    sp.dma_start(edge_rows[:, n], e.rearrange("(r g e) -> r g e", g=EG, e=TT)).then_inc(loaded, 16)
                sp.wait_ge(vec, 12)
                sp.dma_start(loop_row[0:1, :], loop_i[:, :]).then_inc(ranged, 16)
                sp.dma_start(g.ft[:, :, :, :].rearrange("p t k f -> p t (k f)"), x.rearrange("(t p) f -> p t f", p=TT)).then_inc(x_loaded, 16)
                sp.wait_ge(x_loaded, 16)

            @block.gpsimd
            def _(pool):
                pool.iota(node_ids[:, :], pattern=[[1, N]], base=0, channel_multiplier=0).then_inc(made, 1)
                pool.iota(tile_ids[:, 0], pattern=[[1, ES]], base=1, channel_multiplier=0).then_inc(made, 1)
                pool.iota(tile_ids[:, 1], pattern=[[-1, ES]], base=ES, channel_multiplier=0).then_inc(made, 1)
                pool.iota(block_lo_i[:, 0:1], pattern=[[0, 1]], base=0, channel_multiplier=TT).then_inc(made, 1)
                pool.iota(block_lo_i[:, 1:2], pattern=[[0, 1]], base=TT, channel_multiplier=TT).then_inc(made, 1)
                pool.memset(before[:, :], 1.0).then_inc(made, 1)
                pool.memset(zeros[:, :], 0.0).then_inc(made, 1)
                pool.wait_ge(made, 7)
                pool.affine_select(out=before[:, :], in_=before[:, :], compare_op=ALU.is_gt, fill=0.0,
                                   base=0, pattern=[[1, NT]], channel_multiplier=-1).then_inc(made, 1)

            @block.vector
            def _(dve):
                dve.wait_ge(loaded, 32)
                dve.tensor_copy(edge_f[:, :, :, :], edge_rows[:, :, :, :]).then_inc(floats, 1)
                dve.wait_ge(floats, 1)
                dve.tensor_reduce(tile_range[:, 0:1], edge_f[:, 1].rearrange("r g e -> r (g e)"), AX_X, ALU.min).then_inc(floats, 1)
                dve.tensor_reduce(tile_range[:, 1:2], edge_f[:, 1].rearrange("r g e -> r (g e)"), AX_X, ALU.max).then_inc(floats, 1)
                dve.wait_ge(made, 8)
                dve.tensor_copy(node_ids16[:, :], node_ids[:, :]).then_inc(vec, 1)
                dve.tensor_copy(tile_idf[:, :, :], tile_ids[:, :, :]).then_inc(vec, 1)
                dve.tensor_copy(block_lo[:, :], block_lo_i[:, :]).then_inc(vec, 1)
                dve.wait_ge(turned, 1)
                dve.tensor_copy(edge_cols[:, 0], ps[0][0:TT, 0:ES * EG].rearrange("p (g r) -> p g r", g=EG)).then_inc(vec, 1)
                dve.tensor_copy(edge_cols[:, 1], ps[1][0:TT, 0:ES * EG].rearrange("p (g r) -> p g r", g=EG)).then_inc(vec, 1)
                dve.wait_ge(turned, 2)
                dve.tensor_copy(range_rows[:, 0], ps[2][0:NT, 0:ES]).then_inc(vec, 1)
                dve.tensor_copy(range_rows[:, 1], ps[3][0:NT, 0:ES]).then_inc(vec, 1)
                dve.wait_ge(vec, 7)
                dve.tensor_scalar(touches[:, :], range_rows[:, 0], block_lo[:, 1:2], None, ALU.is_lt).then_inc(vec, 1)
                dve.wait_ge(vec, 8)
                dve.scalar_tensor_tensor(out=touches[:, :], in0=range_rows[:, 1], scalar=block_lo[:, 0:1],
                                         in1=touches[:, :], op0=ALU.is_ge, op1=ALU.mult).then_inc(vec, 1)
                dve.wait_ge(vec, 9)
                dve.tensor_tensor(range_rows[:, :, :], tile_idf[:, :, :], wide(touches[:, :], 2), ALU.mult).then_inc(vec, 1)
                dve.wait_ge(vec, 10)
                dve.tensor_reduce(first_last[:, 0:2], range_rows[:, :, :], AX_X, ALU.max).then_inc(vec, 1)
                dve.wait_ge(vec, 11)
                dve.tensor_scalar(first_last[:, 2:3], first_last[:, 1:2], -1.0, float(ES), ALU.mult, ALU.add).then_inc(cnt, 1)
                dve.wait_ge(cnt, 1)
                dve.tensor_scalar(first_last[:, 3:4], first_last[:, 2:3], float(ES - 1), None, ALU.min).then_inc(cnt, 1)
                dve.wait_ge(cnt, 2)
                dve.tensor_tensor(first_last[:, 4:5], first_last[:, 0:1], first_last[:, 3:4], ALU.subtract).then_inc(cnt, 1)
                dve.wait_ge(cnt, 3)
                dve.tensor_scalar(first_last[:, 5:6], first_last[:, 4:5], 1.0, None, ALU.max).then_inc(cnt, 1)
                dve.wait_ge(turned, 3)
                dve.tensor_copy(loop_f[:, 0:1], ps[4][0:NT, 0:1]).then_inc(cnt, 1)
                dve.wait_ge(cnt, 5)
                dve.tensor_tensor(loop_f[:, 1:2], loop_f[:, 0:1], first_last[:, 5:6], ALU.add).then_inc(cnt, 1)
                dve.tensor_tensor(loop_f[:, 2:3], first_last[:, 3:4], loop_f[:, 0:1], ALU.subtract).then_inc(cnt, 1)
                dve.wait_ge(cnt, 7)
                dve.tensor_copy(loop_i[:, :], loop_f[:, :]).then_inc(vec, 1)
                dve.wait_ge(ranged, 16)
                dve.sem_inc(used, SLOTS)
                with dve.Fori(0, NT) as b:
                    lo = dve.value_load(loop_row[0:1, bass.ds(b * 3, 1)], min_val=0, max_val=ES * NT - 1)
                    hi = dve.value_load(loop_row[0:1, bass.ds(b * 3 + 1, 1)], min_val=1, max_val=ES * NT)
                    shift = dve.value_load(loop_row[0:1, bass.ds(b * 3 + 2, 1)], min_val=-ES * NT, max_val=ES)
                    with dve.Fori(lo, hi) as i:
                        t = nc.s_assert_within(dve.snap(i + shift), 0, ES - 1)
                        slot = dve.snap(i % SLOTS)
                        dve.wait_ge(used, i + 1)
                        for e in range(EG):
                            dve.tensor_scalar(hot_dst[:, bass.ds(slot, 1), e].squeeze(1), node_ids16[:, bass.ds(b * TT, TT)],
                                              edge_cols[:, 1, e, bass.ds(t, 1)], None, ALU.is_equal)
                            op = dve.tensor_scalar(hot_src[:, bass.ds(slot, 1), e].squeeze(1), node_ids16[:, :],
                                                   edge_cols[:, 0, e, bass.ds(t, 1)], None, ALU.is_equal)
                        op.then_inc(hots, 1)

            @block.scalar
            def _(act):
                act.sem_inc(kept, 1)
                act.sem_inc(masked_s, 1)
                with act.Fori(0, NT) as b:
                    act.wait_ge(counted, b + 1)
                    act.wait_ge(masked_s, b + 1)
                    for n, (c0, w) in enumerate(CHUNKS):
                        op = act.activation(staged[:, c0:c0 + w], ps[n][0:TT, 0:w], ACT.Copy)
                    op.then_inc(staged_s, 1)
                    act.wait_ge(turned_t, b + 1)
                    for j0, j1 in ((0, 4), (4, 8), (8, 10)):
                        op = act.activation(g.counts_T[:, j0:j1, bass.ds(b * TT, TT)],
                                            ps[4 + j0 // 4][0:TT, 0:(j1 - j0) * TT].rearrange("p (j d) -> p j d", j=j1 - j0), ACT.Copy)
                    op.then_inc(kept, 1)
                    act.activation(g.no_edge[:, bass.ds(b, 1)].squeeze(1), staged[:, :], ACT.Relu,
                                   bias=g.far[0:TT, 0:1], scale=-FAR).then_inc(masked_s, 1)

            @block.tensor
            def _(pe):
                pe.wait_ge(floats, 1)
                for n in range(2):
                    for k in range(EG):
                        op = pe.transpose(ps[n][0:TT, k * ES:(k + 1) * ES], edge_f[:, n, k], g.ident[0:ES, 0:ES])
                op.then_inc(turned, 1)
                pe.wait_ge(floats, 3)
                for n in range(2):
                    op = pe.matmul(ps[2 + n][0:NT, 0:ES], tile_range[:, n:n + 1].broadcast_to([ES, NT]), g.ident[0:ES, 0:ES],
                                   start=True, stop=True)
                op.then_inc(turned, 1)
                pe.wait_ge(cnt, 4)
                pe.matmul(ps[4][0:NT, 0:1], before[:, :], first_last[:, 5:6], start=True, stop=True).then_inc(turned, 1)
                pe.wait_ge(vec, 12)
                pe.wait_ge(ranged, 16)
                with pe.Fori(0, NT) as b:
                    lo = pe.value_load(loop_row[0:1, bass.ds(b * 3, 1)], min_val=0, max_val=ES * NT - 1)
                    hi = pe.value_load(loop_row[0:1, bass.ds(b * 3 + 1, 1)], min_val=1, max_val=ES * NT)
                    pe.wait_ge(made, 8)
                    for n, (c0, w) in enumerate(CHUNKS):
                        pe.matmul(ps[n][0:TT, 0:w], zeros[:, :], node_ids16[:, 0:w], start=True, stop=False,
                                  skip_group_check=True)
                    with pe.Fori(lo, hi) as i:
                        slot = pe.snap(i % SLOTS)
                        pe.wait_ge(hots, i + 1)
                        for e in range(EG):
                            for n, (c0, w) in enumerate(CHUNKS):
                                op = pe.matmul(ps[n][0:TT, 0:w], hot_dst[:, bass.ds(slot, 1), e].squeeze(1),
                                               hot_src[:, bass.ds(slot, 1), e, c0:c0 + w].squeeze(1),
                                               start=False, stop=False, skip_group_check=True)
                        op.then_inc(used, 1)
                    for n, (c0, w) in enumerate(CHUNKS):
                        op = pe.matmul(ps[n][0:TT, 0:w], zeros[:, :], node_ids16[:, 0:w], start=False, stop=True,
                                       skip_group_check=True)
                    op.then_inc(counted, 1)
                    pe.wait_ge(staged_s, b + 1)
                    pe.wait_ge(kept, b + 1)
                    for j in range(NT):
                        op = pe.transpose(ps[4 + j // 4][0:TT, (j % 4) * TT:(j % 4 + 1) * TT],
                                          staged[:, j * TT:(j + 1) * TT], g.ident[0:TT, 0:TT])
                    op.then_inc(turned_t, 1)


def stage_load(nc, g):
    g.new_stage()
    with ExitStack() as c:
        x_rows = g.ft[:, :, :, :].rearrange("p t k f -> p t (k f)")
        turned = g.sem("x_turned")
        kept = g.sem("x_kept")
        ps = g.psum
        with nc.Block() as block:
            @block.tensor
            def _(pe):
                for t in range(NT):
                    if t >= 4:
                        pe.wait_ge(kept, t - 3)
                    for k in range(KT):
                        op = pe.transpose(ps[2 * (t % 4) + k // 3][:, (k % 3) * TT:(k % 3 + 1) * TT],
                                          x_rows[:, t, k * P:(k + 1) * P], g.ident[0:TT, 0:TT])
                    op.then_inc(turned, 1)

            @block.vector
            def _(dve):
                for t in range(NT):
                    dve.wait_ge(turned, t + 1)
                    for h in range(2):
                        op = dve.tensor_copy(g.x_T[:, 3 * h:3 * h + 3, t * TT:(t + 1) * TT],
                                             ps[2 * (t % 4) + h][:, 0:3 * TT].rearrange("p (k n) -> p k n", k=3))
                    op.then_inc(kept, 1)


def stage_store(nc, g, out, add=None):
    g.new_stage()
    with ExitStack() as c:
        rows = g.sb(c, "out_rows", [TT, 2, D], F32)
        turned = g.sem("out_turned")
        kept = g.sem("out_kept")
        whole = g.sem("out_whole")
        stored = [g.sem(f"out_stored{i}") for i in range(2)]
        ps = g.psum
        with nc.Block() as block:
            @block.tensor
            def _(pe):
                if add is not None:
                    pe.wait_ge(whole, KT)
                for t in range(NT):
                    if t >= 4:
                        pe.wait_ge(kept, t - 3)
                    for k in range(KT):
                        op = pe.transpose(ps[2 * (t % 4) + k // 3][0:TT, (k % 3) * P:(k % 3 + 1) * P],
                                          g.x_T[:, k, t * TT:(t + 1) * TT], g.ident[:, :])
                    op.then_inc(turned, 1)

            @block.vector
            def _(dve):
                if add is not None:
                    for k in range(KT):
                        dve.tensor_tensor(g.x_T[:, k], g.x_T[:, k], add[:, k], ALU.add).then_inc(whole, 1)
                for t in range(NT):
                    dve.wait_ge(turned, t + 1)
                    if t >= 2:
                        dve.wait_ge(stored[t % 2], 16 * (t // 2))
                    for h in range(2):
                        op = dve.tensor_copy(rows[:, t % 2, h * 384:(h + 1) * 384], ps[2 * (t % 4) + h][0:TT, 0:3 * P])
                    op.then_inc(kept, 1)

            @block.sync
            def _(sp):
                for t in range(NT):
                    sp.wait_ge(kept, t + 1)
                    sp.dma_start(out[t * TT:(t + 1) * TT, :], rows[:, t % 2]).then_inc(stored[t % 2], 16)
                for s in range(2):
                    sp.wait_ge(stored[s], 16 * (NT // 2))


def stage_norm(nc, g, name, src, dst, gamma=None, beta=None, acc=None):
    g.new_stage()
    with ExitStack() as c:
        mean = g.sb(c, f"{name}_mean", [P, 2, CW], F32)
        square = g.sb(c, f"{name}_square", [P, 2, KT, CW], F32)
        std = g.sb(c, f"{name}_std", [P, 2, CW], F32)
        rstd = g.sb(c, f"{name}_rstd", [P, 2, CW], F32)
        gb = g.sb(c, f"{name}_gb", [P, 2, KT], F32)
        summed = g.sem(f"{name}_summed")
        meaned = g.sem(f"{name}_meaned")
        centred = g.sem(f"{name}_centred")
        squared = g.sem(f"{name}_squared")
        varied = g.sem(f"{name}_varied")
        rooted = g.sem(f"{name}_rooted")
        inverted = g.sem(f"{name}_inverted")
        scaled = g.sem(f"{name}_scaled")
        gb_loaded = g.sem(f"{name}_gb_loaded")
        acc_added = g.sem(f"{name}_acc_added")
        ps = g.psum
        n_ch = len(CHUNKS)
        with nc.Block() as block:
            if gamma is not None:
                @block.sync
                def _(sp):
                    sp.dma_start(gb[:, 0], gamma.rearrange("(k p) -> p k", p=P), allow_slow_non_contiguous=True).then_inc(gb_loaded, 16)
                    sp.dma_start(gb[:, 1], beta.rearrange("(k p) -> p k", p=P), allow_slow_non_contiguous=True).then_inc(gb_loaded, 16)

            @block.tensor
            def _(pe):
                def total(n, tensor, b, sem):
                    c0, w = CHUNKS[n]
                    for k in range(KT):
                        op = pe.matmul(ps[b][:, 0:w], g.ones[:, :], tensor(k), start=(k == 0), stop=(k == KT - 1))
                    op.then_inc(sem, 1)

                for n, (c0, w) in enumerate(CHUNKS):
                    total(n, lambda k: src[:, k, c0:c0 + w], n, summed)
                for n, (c0, w) in enumerate(CHUNKS):
                    pe.wait_ge(squared, n + 1)
                    total(n, lambda k: square[:, n % 2, k, 0:w], 3 + n, varied)

            @block.scalar
            def _(act):
                def to_mean(n):
                    c0, w = CHUNKS[n]
                    act.wait_ge(summed, n + 1)
                    if n >= 2:
                        act.wait_ge(centred, n - 1)
                    act.activation(mean[:, n % 2, 0:w], ps[n][:, 0:w], ACT.Copy, scale=1.0 / D).then_inc(meaned, 1)

                def to_square(n):
                    c0, w = CHUNKS[n]
                    act.wait_ge(centred, n + 1)
                    if n >= 2:
                        act.wait_ge(varied, n - 1)
                    act.activation(square[:, n % 2, :, 0:w], dst[:, :, c0:c0 + w], ACT.Square).then_inc(squared, 1)

                def to_std(n):
                    c0, w = CHUNKS[n]
                    act.wait_ge(varied, n + 1)
                    if n >= 2:
                        act.wait_ge(inverted, n - 1)
                    act.activation(std[:, n % 2, 0:w], ps[3 + n][:, 0:w], ACT.Sqrt, bias=g.eps5[:, 0:1],
                                   scale=1.0 / D).then_inc(rooted, 1)

                to_mean(0)
                to_mean(1)
                to_square(0)
                to_mean(2)
                to_square(1)
                to_square(2)
                for n in range(n_ch):
                    to_std(n)
                if gamma is not None:
                    act.wait_ge(gb_loaded, 32)
                    for n, (c0, w) in enumerate(CHUNKS):
                        act.wait_ge(scaled, n + 1)
                        for k in range(KT):
                            act.activation(dst[:, k, c0:c0 + w], dst[:, k, c0:c0 + w], ACT.Identity,
                                           bias=gb[:, 1, k:k + 1], scale=gb[:, 0, k:k + 1])

            @block.vector
            def _(dve):
                if acc is not None:
                    dve.tensor_tensor(acc[:, :, :], acc[:, :, :], src[:, :, :], ALU.add).then_inc(acc_added, 1)
                    dve.wait_ge(acc_added, 1)
                for n, (c0, w) in enumerate(CHUNKS):
                    dve.wait_ge(meaned, n + 1)
                    dve.tensor_tensor(dst[:, :, c0:c0 + w], src[:, :, c0:c0 + w], wide(mean[:, n % 2, 0:w], KT),
                                      ALU.subtract).then_inc(centred, 1)
                for n, (c0, w) in enumerate(CHUNKS):
                    dve.wait_ge(rooted, n + 1)
                    if n >= 2:
                        dve.wait_ge(scaled, n - 1)
                    dve.reciprocal(rstd[:, n % 2, 0:w], std[:, n % 2, 0:w]).then_inc(inverted, 1)
                    dve.wait_ge(inverted, n + 1)
                    dve.wait_ge(squared, n + 1)
                    dve.tensor_tensor(dst[:, :, c0:c0 + w], dst[:, :, c0:c0 + w], wide(rstd[:, n % 2, 0:w], KT),
                                      ALU.mult).then_inc(scaled, 1)


def stage_gat_project(nc, g, W):
    g.new_stage()
    with ExitStack() as c:
        w_rows = g.sb(c, "gat_w_rows", [P, 2, P], F32)
        attn_rows = g.sb(c, "gat_attn_rows", [KT, 2, P], F32)
        attn_T = g.sb(c, "gat_attn_T", [P, 2, KT], F32)
        attn_pair = g.sb(c, "gat_attn_pair", [P, KT, 4], F32)
        rhs = g.sb(c, "gat_rhs", [P, KT, P + 4], F32)
        a1_rows = g.sb(c, "gat_a1_rows", [H, N], F32)
        cleared = g.sem("gatp_cleared")
        loaded = g.sem("gatp_loaded")
        turned = g.sem("gatp_turned")
        kept = g.sem("gatp_kept")
        folded = g.sem("gatp_folded")
        rhs_ready = g.sem("gatp_rhs_ready")
        projected = g.sem("gatp_projected")
        ft_kept = g.sem("gatp_ft_kept")
        a_kept = g.sem("gatp_a_kept")
        a_turned = g.sem("gatp_a_turned")
        row_kept = g.sem("gatp_row_kept")
        stored = g.sem("gatp_stored")
        spilled = g.sem("gatp_counts_spilled")
        ps = g.psum
        with nc.Block() as block:
            @block.gpsimd
            def _(pool):
                pool.memset(w_rows[:, :, :], 0.0).then_inc(cleared, 1)
                pool.memset(attn_pair[:, :, :], 0.0).then_inc(cleared, 1)

            @block.sync
            def _(sp):
                sp.wait_ge(cleared, 2)
                for n, w in enumerate((W["L0_gnn_W_fc"], W["L0_gnn_W_res"])):
                    for h in range(2):
                        sp.dma_start(w_rows[64 * h:64 * h + 64, n, 64 * h:64 * h + 64], w).then_inc(loaded, 16)
                for n, a in enumerate((W["L0_gnn_attn_l"], W["L0_gnn_attn_r"])):
                    sp.dma_start(attn_rows[:, n], a.rearrange("(p h) e -> p (h e)", h=2)).then_inc(loaded, 16)
                sp.dma_start(g.counts_dram, g.counts_T[:, :, :]).then_inc(spilled, 16)
                sp.wait_ge(row_kept, NT)
                sp.dma_start(g.a1_dram, a1_rows[:, :]).then_inc(stored, 16)
                sp.wait_ge(stored, 16)
                sp.wait_ge(spilled, 16)

            @block.tensor
            def _(pe):
                pe.wait_ge(loaded, 96)
                for n in range(2):
                    pe.transpose(ps[0][:, n * P:(n + 1) * P], w_rows[:, n], g.ident[:, :])
                    op = pe.transpose(ps[1][:, n * KT:(n + 1) * KT], attn_rows[:, n], g.ident[0:KT, 0:KT])
                op.then_inc(turned, 1)
                pe.wait_ge(kept, 6)
                for k in range(KT):
                    op = pe.matmul(ps[2][:, 4 * k:4 * k + 4], w_rows[:, 0], attn_pair[:, k], start=True, stop=True)
                op.then_inc(folded, 1)
                pe.wait_ge(rhs_ready, 2)
                for t in range(NT):
                    if t >= 3:
                        pe.wait_ge(ft_kept, t - 2)
                    for k in range(KT):
                        op = pe.matmul(ps[2 * (t % 3) + k // 3][0:TT, (k % 3) * (P + 4):(k % 3 + 1) * (P + 4)],
                                       g.y_T[:, k, t * TT:(t + 1) * TT], rhs[:, k], start=True, stop=True)
                    op.then_inc(projected, 1)
                for t in range(NT):
                    pe.wait_ge(a_kept, t + 1)
                    if t >= 2:
                        pe.wait_ge(row_kept, t - 1)
                    pe.transpose(ps[6 + t % 2][0:H, 0:TT], g.a_cols[:, t, 0], g.ident[0:TT, 0:TT]).then_inc(a_turned, 1)

            @block.vector
            def _(dve):
                dve.wait_ge(turned, 1)
                dve.wait_ge(cleared, 2)
                dve.tensor_copy(g.w_res[:, :], ps[0][:, P:2 * P]).then_inc(kept, 1)
                dve.tensor_copy(attn_T[:, :, :], ps[1][:, 0:2 * KT].rearrange("p (n k) -> p n k", n=2)).then_inc(kept, 1)
                dve.wait_ge(kept, 2)
                for n in range(2):
                    for h in range(2):
                        dve.tensor_copy(attn_pair[64 * h:64 * h + 64, :, 2 * n + h], attn_T[64 * h:64 * h + 64, n]).then_inc(kept, 1)
                dve.tensor_copy(rhs[:, :, 0:P], wide(ps[0][:, 0:P], KT)).then_inc(rhs_ready, 1)
                dve.wait_ge(folded, 1)
                dve.tensor_copy(rhs[:, :, P:P + 4], ps[2][:, 0:4 * KT].rearrange("p (k j) -> p k j", k=KT)).then_inc(rhs_ready, 1)
                for t in range(NT):
                    dve.wait_ge(projected, t + 1)
                    for h in range(2):
                        part = ps[2 * (t % 3) + h][0:TT, 0:3 * (P + 4)].rearrange("p (k j) -> p k j", k=3)
                        for n in range(2):
                            op = dve.tensor_copy(g.a_cols[:, t, n, 6 * h:6 * h + 6].rearrange("p (k j) -> p k j", k=3),
                                                 part[:, :, P + 2 * n:P + 2 * n + 2])
                    op.then_inc(a_kept, 1)
                for t in range(NT):
                    dve.wait_ge(a_turned, t + 1)
                    dve.tensor_copy(a1_rows[:, t * TT:(t + 1) * TT], ps[6 + t % 2][0:H, 0:TT]).then_inc(row_kept, 1)

            @block.scalar
            def _(act):
                for t in range(NT):
                    act.wait_ge(a_kept, t + 1)
                    for h in range(2):
                        part = ps[2 * (t % 3) + h][0:TT, 0:3 * (P + 4)].rearrange("p (k j) -> p k j", k=3)
                        op = act.activation(g.ft[:, t, 3 * h:3 * h + 3, :], part[:, :, 0:P], ACT.Copy)
                    op.then_inc(ft_kept, 1)


def stage_gat_rows(nc, g):
    g.new_stage()
    with ExitStack() as c:
        e_max = g.sb(c, "e_max", [TT, NT, H], F32)
        e_sum = g.sb(c, "e_sum", [TT, NT, H], F32)
        uv = g.sb(c, "uv", [TT, NT, 2, H], F32)
        uv_rows = g.sb(c, "uv_rows", [2 * H, N], F32)
        chain = g.sem("gatm_chain")
        turned = g.sem("gatm_turned")
        row_kept = g.sem("gatm_row_kept")
        stored = g.sem("gatm_stored")
        ps = g.psum
        with nc.Block() as block:
            @block.sync
            def _(sp):
                sp.wait_ge(row_kept, NT)
                sp.dma_start(g.uv_dram, uv_rows[:, :]).then_inc(stored, 16)
                sp.wait_ge(stored, 16)

            @block.vector
            def _(dve):
                a1, a2 = g.a_cols[:, :, 0], g.a_cols[:, :, 1]
                dve.tensor_tensor(e_sum[:, :, :], a2, g.a1_max[:, :, :], ALU.add).then_inc(chain, 1)
                dve.wait_ge(chain, 1)
                dve.scalar_tensor_tensor(out=e_max[:, :, :], in0=e_sum[:, :, :], scalar=0.2, in1=e_sum[:, :, :],
                                         op0=ALU.mult, op1=ALU.max).then_inc(chain, 1)
                dve.wait_ge(chain, 2)
                dve.tensor_tensor(uv[:, :, 0], a2, e_max[:, :, :], ALU.subtract).then_inc(chain, 1)
                dve.scalar_tensor_tensor(out=uv[:, :, 1], in0=a2, scalar=0.2, in1=e_max[:, :, :],
                                         op0=ALU.mult, op1=ALU.subtract).then_inc(chain, 1)
                dve.tensor_scalar(g.a1_fifth[:, :, :], a1, 0.2, None, ALU.mult).then_inc(chain, 1)
                for t in range(NT):
                    dve.wait_ge(turned, t + 1)
                    dve.tensor_copy(uv_rows[:, t * TT:(t + 1) * TT], ps[t % 2][0:2 * H, 0:TT]).then_inc(row_kept, 1)

            @block.tensor
            def _(pe):
                pe.wait_ge(chain, 4)
                for t in range(NT):
                    if t >= 2:
                        pe.wait_ge(row_kept, t - 1)
                    pe.transpose(ps[t % 2][0:2 * H, 0:TT], uv[:, t].rearrange("p n h -> p (n h)"),
                                 g.ident[0:TT, 0:TT]).then_inc(turned, 1)


def stage_gat_attend(nc, g):
    g.new_stage()
    SLOTS = 5
    n2 = 2 * NT
    WEIGHED_BY_DVE = [i for i in range(n2) if i % 5 in (0, 2)]
    WEIGHED_BY_POOL = [i for i in range(n2) if i not in WEIGHED_BY_DVE]
    assert n2 % SLOTS == 0
    with ExitStack() as c:
        u_wide = g.sb(c, "u_wide", [TT, 2, N], F32)
        v_wide = g.sb(c, "v_wide", [TT, 2, N], F32)
        ft_one = g.sb(c, "ft_one", [TT, 2, NT, P], F32)
        ring = g.sb(c, "gat_ring", [TT, SLOTS, N], F32)
        den = g.sb(c, "gat_den", [P, N], F32)
        agg = g.sb(c, "gat_agg", [P, N], F32)
        ones_s = g.sem("gata_ones")
        uv_loaded = [g.sem(f"gata_uv{i}") for i in range(2)]
        ft_s = g.sem("gata_ft")
        low_s = g.sem("gata_low")
        raised = g.sem("gata_raised")
        high_s = g.sem("gata_high")
        exp_s = g.sem("gata_exp")
        prob_pool = g.sem("gata_prob_by_pool")
        prob_dve = g.sem("gata_prob_by_dve")
        used = g.sem("gata_used")
        taken = g.sem("gata_taken")
        clamped = g.sem("gata_clamped")
        inv_s = g.sem("gata_inverted")
        mean_s = g.sem("gata_normed")
        res_s = g.sem("gata_residual")
        res_added = g.sem("gata_residual_added")
        added = g.sem("gata_added")
        pool_turn = g.sem("gata_pool_turn")
        ps = g.psum
        own = (slice(0, 64), slice(64, 128))
        other = (slice(64, 128), slice(0, 64))

        def pairs(engine, body):
            body(0, None)
            with engine.Fori(1, KT) as p:
                body(p, p - 1)

        with nc.Block() as block:
            @block.sync
            def _(sp):
                for h in range(2):
                    for wide_t, o in ((u_wide, 0), (v_wide, H)):
                        sp.dma_start(wide_t[:, h], g.uv_dram[h + o:h + o + 1, :].partition_broadcast(TT)).then_inc(uv_loaded[h], 16)
                with sp.Fori(1, KT) as p:
                    for h in range(2):
                        sp.wait_ge(high_s, n2 * p - n2 + NT * (h + 1))
                        for wide_t, o in ((u_wide, 0), (v_wide, H)):
                            sp.dma_start(wide_t[:, h], g.uv_dram[bass.ds(p * 2 + h + o, 1), :].partition_broadcast(TT)).then_inc(uv_loaded[h], 16)

            @block.gpsimd
            def _(pool):
                def wait(sem, value):
                    pool.wait_ge(sem, value)
                    pool.sem_inc(pool_turn, 1)

                def load_ft(p, h):
                    ftp = g.ft[:, :, bass.ds(p, 1), :].squeeze(2)
                    pool.tensor_copy(ft_one[:, h, :, own[h]], ftp[:, :, own[h]]).then_inc(ft_s, 1)

                def body(p, q):
                    for i in range(n2):
                        if i == 0:
                            wait(used, n2 * p + SLOTS)
                            load_ft(p, 1)
                        if i == NT + 5:
                            wait(used, n2 * p + NT + SLOTS)
                            load_ft(nc.gpsimd.snap((p + 1) % KT) if q is not None else 1, 0)
                        if i in WEIGHED_BY_POOL:
                            wait(exp_s, n2 * p + i + 1)
                            pool.tensor_tensor(ring[:, i % SLOTS], ring[:, i % SLOTS], g.counts_T[:, i % NT], ALU.mult).then_inc(prob_pool, 1)

                pool.memset(ft_one[:, 0, :, other[0]], 1.0).then_inc(ones_s, 1)
                pool.wait_ge(ones_s, 1)
                pool.memset(ft_one[:, 1, :, other[1]], 1.0).then_inc(ones_s, 1)
                load_ft(0, 0)
                pairs(pool, body)

            @block.scalar
            def _(act):
                act.sem_inc(taken, 2)

                def lower(p, i):
                    h, j = i // NT, i % NT
                    act.wait_ge(uv_loaded[h], 32 * p + 32)
                    act.wait_ge(used, n2 * p + i + 1)
                    act.activation(ring[:, i % SLOTS], v_wide[:, h], ACT.Identity,
                                   bias=g.a1_fifth[:, j, bass.ds(2 * p + h, 1)]).then_inc(low_s, 1)

                def take(p, h):
                    act.wait_ge(used, n2 * p + NT * (h + 1) + SLOTS)
                    act.wait_ge(added, p + 1)
                    for n, (c0, w) in enumerate(CHUNKS):
                        act.activation(den[own[h], c0:c0 + w], ps[3 * h + n][other[h], 0:w], ACT.Copy)
                        op = act.activation(agg[own[h], c0:c0 + w], ps[3 * h + n][own[h], 0:w], ACT.Copy)
                    op.then_inc(taken, 1)

                def body(p, q):
                    AHEAD = 2
                    for i in range(AHEAD):
                        lower(p, i)
                    for i in range(n2):
                        act.wait_ge(high_s, n2 * p + i + 1)
                        act.activation(ring[:, i % SLOTS], ring[:, i % SLOTS], ACT.Exp).then_inc(exp_s, 1)
                        if i + AHEAD < n2:
                            lower(p, i + AHEAD)
                        if i == 3 and q is not None:
                            take(q, 1)
                    take(p, 0)

                pairs(act, body)
                take(KT - 1, 1)

            @block.vector
            def _(dve):
                dve.sem_inc(used, SLOTS)
                dve.sem_inc(added, 1)
                dve.sem_inc(res_added, 1)

                def invert(q, n):
                    c0, w = CHUNKS[n]
                    dve.wait_ge(taken, 2 * q + 4)
                    dve.tensor_scalar(den[:, c0:c0 + w], den[:, c0:c0 + w], 0.5, None, ALU.max).then_inc(clamped, 1)
                    dve.wait_ge(clamped, 3 * q + n + 1)
                    dve.reciprocal(den[:, c0:c0 + w], den[:, c0:c0 + w]).then_inc(inv_s, 1)

                def norm(q):
                    dve.wait_ge(inv_s, 3 * q + 3)
                    dve.tensor_tensor(agg[:, :], agg[:, :], den[:, :], ALU.mult).then_inc(mean_s, 1)

                def add_residual(q, n):
                    c0, w = CHUNKS[n]
                    dve.wait_ge(mean_s, q + 1)
                    dve.wait_ge(res_s, 3 * q + n + 1)
                    dve.tensor_tensor(agg[:, c0:c0 + w], agg[:, c0:c0 + w], ps[6 + n % 2][:, 0:w], ALU.add).then_inc(res_added, 1)

                def add(q):
                    dve.wait_ge(res_added, 3 * q + 4)
                    xq = g.x_T[:, bass.ds(q, 1), :].squeeze(1)
                    dve.scalar_tensor_tensor(out=xq, in0=agg[:, :], scalar=0.0, in1=xq, op0=ALU.max, op1=ALU.add).then_inc(added, 1)

                def body(p, q):
                    for i in range(n2):
                        h, j = i // NT, i % NT
                        dve.wait_ge(uv_loaded[h], 32 * p + 32)
                        dve.wait_ge(low_s, n2 * p + i + 1)
                        op = dve.scalar_tensor_tensor(out=ring[:, i % SLOTS], in0=u_wide[:, h],
                                                      scalar=g.a_cols[:, j, 0, bass.ds(2 * p + h, 1)],
                                                      in1=ring[:, i % SLOTS], op0=ALU.add, op1=ALU.max)
                        if i in WEIGHED_BY_DVE:
                            op.then_inc(high_s, 1)
                        else:
                            op.then_inc(raised, 1)
                            dve.wait_ge(raised, len(WEIGHED_BY_POOL) * p + WEIGHED_BY_POOL.index(i) + 1)
                            dve.tensor_scalar(ring[:, i % SLOTS], ring[:, i % SLOTS], 0.0, None, ALU.min).then_inc(high_s, 1)
                        if i - 2 in WEIGHED_BY_DVE:
                            dve.wait_ge(exp_s, n2 * p + i - 1)
                            dve.scalar_tensor_tensor(out=ring[:, (i - 2) % SLOTS], in0=ring[:, (i - 2) % SLOTS], scalar=1.0,
                                                     in1=g.counts_T[:, (i - 2) % NT], op0=ALU.min, op1=ALU.mult).then_inc(prob_dve, 1)
                        if q is not None:
                            if i in (5, 7, 9):
                                invert(q, (i - 5) // 2)
                            if i == 11:
                                norm(q)
                            if i in (12, 14, 17):
                                add_residual(q, {12: 0, 14: 1, 17: 2}[i])
                            if i == 18:
                                add(q)

                pairs(dve, body)
                for n in range(3):
                    invert(KT - 1, n)
                norm(KT - 1)
                for n in range(3):
                    add_residual(KT - 1, n)
                add(KT - 1)

            @block.tensor
            def _(pe):
                def residual(q, n):
                    c0, w = CHUNKS[n]
                    pe.wait_ge(res_added, 3 * q + (2 if n == 2 else 1))
                    pe.matmul(ps[6 + n % 2][:, 0:w], g.w_res[:, :], g.y_T[:, bass.ds(q, 1), c0:c0 + w].squeeze(1),
                              start=True, stop=True).then_inc(res_s, 1)

                def body(p, q):
                    for i in range(n2):
                        h, j = i // NT, i % NT
                        if j == 0:
                            pe.wait_ge(taken, 2 * p + h + 1)
                            pe.wait_ge(ft_s, 2 * p + h + 1)
                        if i in WEIGHED_BY_DVE:
                            pe.wait_ge(prob_dve, len(WEIGHED_BY_DVE) * p + WEIGHED_BY_DVE.index(i) + 1)
                        else:
                            pe.wait_ge(prob_pool, len(WEIGHED_BY_POOL) * p + WEIGHED_BY_POOL.index(i) + 1)
                        for n, (c0, w) in enumerate(CHUNKS):
                            op = pe.matmul(ps[3 * h + n][:, 0:w], ft_one[:, h, j], ring[:, i % SLOTS, c0:c0 + w],
                                           start=(j == 0), stop=(j == NT - 1))
                        op.then_inc(used, 1)
                        if q is not None and i in (2, 12):
                            for n in ((0, 1) if i == 2 else (2,)):
                                residual(q, n)

                pe.wait_ge(ones_s, 2)
                pairs(pe, body)
                for n in range(3):
                    residual(KT - 1, n)


def project_T(pe, banks, w, src):
    for k in range(KT):
        for n, (c0, wd) in enumerate(CHUNKS):
            op = pe.matmul(banks[n][:, 0:wd], w[:, k], src[:, k, c0:c0 + wd], start=(k == 0), stop=(k == KT - 1))
    return op


def stage_mix0(nc, g, w_qkv, src, o_T, spare):
    g.new_stage()
    with ExitStack() as c:
        at = [0]

        def own_part(*shape):
            n = 1
            for x in shape:
                n *= x
            at[0] += n
            flat = spare[:, at[0] - n:at[0]]
            if len(shape) == 1:
                return flat
            names = "abc"[:len(shape)]
            sizes = {k: v for k, v in zip(names, shape)}
            return flat.rearrange(f"p ({' '.join(names)}) -> p {' '.join(names)}", **sizes)

        w = own_part(KT, 3, P)
        q = own_part(N)
        q_low = own_part(N)
        k = own_part(NT, P)[0:TT]
        k_low = own_part(NT, P)[0:TT]
        v1 = own_part(NT, 2 * P)[0:TT]
        kv = own_part(2, P)
        inv = own_part(N)
        a1_wide = g.sb(c, "a1_wide", [TT, 2, N], F32)
        masked = g.sb(c, "masked", [TT, N], BF16)
        pair_max = g.sb(c, "pair_max", [TT, NT, 2], F32)
        ones_s = g.sem("mix0_ones")
        loaded = g.sem("mix0_w_loaded")
        w_used = g.sem("mix0_w_used")
        projected = g.sem("mix0_projected")
        lows = g.sem("mix0_lows")
        exps = g.sem("mix0_exps")
        elus = g.sem("mix0_elus")
        kv_sum = g.sem("mix0_kv_sum")
        kv_s = g.sem("mix0_kv")
        outs = g.sem("mix0_outs")
        taken = g.sem("mix0_taken")
        inv_s = g.sem("mix0_inv")
        done = g.sem("mix0_done")
        wide_s = [g.sem(f"gatm_wide{i}") for i in range(2)]
        maxed = g.sem("gatm_maxed")
        max_kept = g.sem("gatm_max_kept")
        max_turn = g.sem("gatm_max_turn")
        ps = g.psum
        n2 = 2 * NT
        with nc.Block() as block:
            @block.sync
            def _(sp):
                with sp.Fori(0, KT) as p:
                    sp.wait_ge(w_used, p + 1)
                    for n in range(3):
                        sp.dma_start(w[:, :, n], w_qkv.rearrange("(k f) (n m) -> f k n m", f=P, n=3)[:, :, n, bass.ds(p * P, P)]).then_inc(loaded, 16)
                    for h in range(2):
                        sp.wait_ge(maxed, n2 * p + 1)
                        sp.dma_start(a1_wide[:, h], g.a1_dram[bass.ds(2 * p + h, 1), :].partition_broadcast(TT)).then_inc(wide_s[h], 16)

            @block.gpsimd
            def _(pool):
                pool.memset(v1[:, :, P:2 * P], 1.0).then_inc(ones_s, 1)
                pool.sem_inc(w_used, 1)
                pool.sem_inc(maxed, 1)
                pool.sem_inc(taken, 1)

            @block.tensor
            def _(pe):
                pe.wait_ge(ones_s, 1)
                with pe.Fori(0, KT) as p:
                    pe.wait_ge(loaded, 48 * p + 48)
                    pe.wait_ge(taken, 3 * p + 1)
                    project_T(pe, ps[0:3], w[:, :, 0], src).then_inc(projected, 1)
                    for t in range(NT):
                        for kk in range(KT):
                            op = pe.matmul(ps[3 + t // 2][0:TT, (t % 2) * 256:(t % 2) * 256 + 256],
                                           src[:, kk, t * TT:(t + 1) * TT], w[:, kk, 1:3, :],
                                           start=(kk == 0), stop=(kk == KT - 1))
                        if t % 2:
                            op.then_inc(projected, 1)
                    pe.wait_ge(projected, 6 * p + 6)
                    pe.sem_inc(w_used, 1)
                    pe.wait_ge(elus, 8 * p + 8)
                    for t in range(NT):
                        op = pe.matmul(ps[3][:, 0:256], k[:, t], v1[:, t], start=(t == 0), stop=(t == NT - 1))
                    op.then_inc(kv_sum, 1)
                    pe.wait_ge(kv_s, 2 * p + 2)
                    for n, (c0, wd) in enumerate(CHUNKS):
                        pe.matmul(ps[4 + n][:, 0:wd], kv[:, 1], q[:, c0:c0 + wd], start=True, stop=True)
                        pe.matmul(ps[n][:, 0:wd], kv[:, 0], q[:, c0:c0 + wd], start=True, stop=True).then_inc(outs, 1)

            @block.scalar
            def _(act):
                with act.Fori(0, KT) as p:
                    for n, (c0, wd) in enumerate(CHUNKS):
                        act.wait_ge(lows, 8 * p + n + 1)
                        act.activation(q_low[:, c0:c0 + wd], q_low[:, c0:c0 + wd], ACT.Exp).then_inc(exps, 1)
                    for b in range(5):
                        act.wait_ge(lows, 8 * p + b + 4)
                        act.activation(k_low[:, 2 * b:2 * b + 2], k_low[:, 2 * b:2 * b + 2], ACT.Exp).then_inc(exps, 1)
                    for n, (c0, wd) in enumerate(CHUNKS):
                        act.wait_ge(outs, 3 * p + n + 1)
                        act.activation(inv[:, c0:c0 + wd], ps[4 + n][:, 0:wd], ACT.Copy)
                        act.activation(q_low[:, c0:c0 + wd], ps[n][:, 0:wd], ACT.Copy).then_inc(taken, 1)

            @block.vector
            def _(dve):
                with dve.Fori(0, KT) as p:
                    def most(k0, k1):
                        for i in range(k0, k1):
                            h, b = i // NT, i % NT
                            if b == 0:
                                dve.wait_ge(wide_s[h], 16 * p + 16)
                            dve.wait_ge(maxed, n2 * p + i + 1)
                            dve.sem_inc(max_turn, 1)
                            dve.tensor_tensor_reduce(masked[:, :], a1_wide[:, h], g.no_edge[:, b], 1.0, -BIG,
                                                     ALU.subtract, ALU.max, pair_max[:, b, h:h + 1]).then_inc(maxed, 1)

                    most(0, 6)
                    dve.wait_ge(projected, 6 * p + 1)
                    for n, (c0, wd) in enumerate(CHUNKS):
                        dve.tensor_scalar(q_low[:, c0:c0 + wd], ps[n][:, 0:wd], 0.0, None, ALU.min).then_inc(lows, 1)
                    for n, (c0, wd) in enumerate(CHUNKS):
                        dve.wait_ge(exps, 8 * p + n + 1)
                        dve.scalar_tensor_tensor(out=q[:, c0:c0 + wd], in0=ps[n][:, 0:wd], scalar=0.0, in1=q_low[:, c0:c0 + wd],
                                                 op0=ALU.max, op1=ALU.add).then_inc(elus, 1)
                    for b in range(5):
                        dve.wait_ge(projected, 6 * p + b + 2)
                        kvb = ps[3 + b][0:TT, 0:512].rearrange("p (t n m) -> p t n m", t=2, n=2)
                        dve.tensor_scalar(k_low[:, 2 * b:2 * b + 2], kvb[:, :, 0], 0.0, None, ALU.min).then_inc(lows, 1)
                        dve.tensor_copy(v1[:, 2 * b:2 * b + 2, 0:P], kvb[:, :, 1])
                        if b < 4:
                            most(6 + 2 * b, 8 + 2 * b)
                        dve.wait_ge(exps, 8 * p + b + 4)
                        dve.scalar_tensor_tensor(out=k[:, 2 * b:2 * b + 2], in0=kvb[:, :, 0], scalar=0.0, in1=k_low[:, 2 * b:2 * b + 2],
                                                 op0=ALU.max, op1=ALU.add).then_inc(elus, 1)
                    most(14, 17)
                    dve.wait_ge(kv_sum, p + 1)
                    for n in range(2):
                        dve.tensor_tensor(kv[:, n], ps[3][:, n * P:(n + 1) * P], g.pair_mask[:, :], ALU.mult).then_inc(kv_s, 1)
                    most(17, n2)
                    dve.wait_ge(maxed, n2 * p + n2 + 1)
                    dve.tensor_copy(g.a1_max[:, :, bass.ds(2 * p, 2)], pair_max[:, :, :]).then_inc(max_kept, 1)
                    for n, (c0, wd) in enumerate(CHUNKS):
                        dve.wait_ge(taken, 3 * p + n + 2)
                        dve.reciprocal(inv[:, c0:c0 + wd], inv[:, c0:c0 + wd]).then_inc(inv_s, 1)
                    for n, (c0, wd) in enumerate(CHUNKS):
                        dve.wait_ge(inv_s, 3 * p + n + 1)
                        op = dve.tensor_tensor(o_T[:, bass.ds(p, 1), c0:c0 + wd].squeeze(1), q_low[:, c0:c0 + wd], inv[:, c0:c0 + wd], ALU.mult)
                    op.then_inc(done, 1)
                    dve.wait_ge(max_kept, p + 1)
                    dve.wait_ge(done, p + 1)
                    dve.sem_inc(max_turn, 1)


def stage_linear(nc, g, name, w, bias, src, kt, mt, func, dst=None, add_to=None, scale=1.0, times=None, expert=None, refill=None):
    g.new_stage()
    with ExitStack() as c:
        w_sb = g.sb(c, f"{name}_w", [P, 2, kt, P], F32)
        bias_sb = g.sb(c, f"{name}_bias", [P, mt], F32)
        bias_x = g.sb(c, f"{name}_bias_x", [P, mt], F32)
        t_sb = g.sb(c, f"{name}_t", [P, N], F32) if add_to is not None else None
        loaded = [g.sem(f"{name}_w_loaded{i}") for i in range(2)]
        bias_loaded = g.sem(f"{name}_bias_loaded")
        bias_s = g.sem(f"{name}_bias_scaled")
        summed = g.sem(f"{name}_summed")
        taken = g.sem(f"{name}_taken")
        added = g.sem(f"{name}_added")
        refilled = g.sem(f"{name}_refilled")
        ps = g.psum
        with nc.Block() as block:
            @block.sync
            def _(sp):
                if expert is None:
                    w_of, b_of = w, bias
                else:
                    e = sp.value_load(expert, min_val=0, max_val=w.shape[0] - 1)
                    w_of = w[bass.ds(e, 1)].squeeze(0)
                    b_of = bias[bass.ds(e, 1)].squeeze(0)
                w_v = w_of.rearrange("(k f) m -> f k m", f=P)
                sp.dma_start(w_sb[:, 0], w_v[:, :, 0:P]).then_inc(loaded[0], 16)
                sp.dma_start(bias_sb[:, :], b_of.rearrange("(m f) -> f m", f=P), allow_slow_non_contiguous=True).then_inc(bias_loaded, 16)
                for m in range(1, mt):
                    if m >= 2:
                        sp.wait_ge(summed, m - 1)
                    sp.dma_start(w_sb[:, m % 2], w_v[:, :, m * P:(m + 1) * P]).then_inc(loaded[m % 2], 16)
                if refill is not None:
                    sp.dma_start(*refill).then_inc(refilled, 16)
                    sp.wait_ge(refilled, 16)

            @block.tensor
            def _(pe):
                for m in range(mt):
                    pe.wait_ge(loaded[m % 2], 16 * (m // 2) + 16)
                    if m >= 2:
                        pe.wait_ge(taken, m - 1)
                    for k in range(kt):
                        for n, (c0, wd) in enumerate(CHUNKS):
                            op = pe.matmul(ps[3 * (m % 2) + n][:, 0:wd], w_sb[:, m % 2, k], src[:, k, c0:c0 + wd],
                                           start=(k == 0), stop=(k == kt - 1))
                    op.then_inc(summed, 1)

            @block.scalar
            def _(act):
                act.wait_ge(bias_loaded, 16)
                act.activation(bias_x[:, :], bias_sb[:, :], ACT.Copy, scale=scale).then_inc(bias_s, 1)
                act.wait_ge(bias_s, 1)
                for m in range(mt):
                    act.wait_ge(summed, m + 1)
                    if add_to is not None and m >= 1:
                        act.wait_ge(added, m)
                    for n, (c0, wd) in enumerate(CHUNKS):
                        out = dst[:, m, c0:c0 + wd] if add_to is None else t_sb[:, c0:c0 + wd]
                        op = act.activation(out, ps[3 * (m % 2) + n][:, 0:wd], func, bias=bias_x[:, m:m + 1], scale=scale)
                    op.then_inc(taken, 1)

            if add_to is not None:
                @block.vector
                def _(dve):
                    for m in range(mt):
                        dve.wait_ge(taken, m + 1)
                        if times is None:
                            op = dve.tensor_tensor(add_to[:, m], add_to[:, m], t_sb[:, :], ALU.add)
                        else:
                            op = dve.scalar_tensor_tensor(out=add_to[:, m], in0=t_sb[:, :], scalar=times,
                                                          in1=add_to[:, m], op0=ALU.mult, op1=ALU.add)
                        op.then_inc(added, 1)


def stage_linear_split(nc, g, name, w, bias, src, func, add_to, scale=1.0):
    g.new_stage()
    with ExitStack() as c:
        src_hl = g.sb(c, f"{name}_src_hl", [P, 2, KT, N], F32R)
        w_raw = g.sb(c, f"{name}_w_raw", [P, 2, KT, P], F32)
        w_hl = g.sb(c, f"{name}_w_hl", [P, 2, 2, KT, P], F32R)
        bias_sb = g.sb(c, f"{name}_bias", [P, KT], F32)
        bias_x = g.sb(c, f"{name}_bias_x", [P, KT], F32)
        t_sb = g.sb(c, f"{name}_t", [P, N], F32)
        loaded = [g.sem(f"{name}_w_loaded{i}") for i in range(2)]
        bias_loaded = g.sem(f"{name}_bias_loaded")
        bias_s = g.sem(f"{name}_bias_scaled")
        w_high, w_low = g.sem(f"{name}_w_high"), g.sem(f"{name}_w_low")
        src_high, src_low = g.sem(f"{name}_src_high"), g.sem(f"{name}_src_low")
        summed = g.sem(f"{name}_summed")
        taken = g.sem(f"{name}_taken")
        added = g.sem(f"{name}_added")
        ps = g.psum
        with nc.Block() as block:
            @block.sync
            def _(sp):
                w_v = w.rearrange("(k f) m -> f k m", f=P)
                sp.dma_start(w_raw[:, 0], w_v[:, :, 0:P]).then_inc(loaded[0], 16)
                sp.dma_start(bias_sb[:, :], bias.rearrange("(m f) -> f m", f=P), allow_slow_non_contiguous=True).then_inc(bias_loaded, 16)
                for m in range(1, KT):
                    if m >= 2:
                        sp.wait_ge(w_low, m - 1)
                    sp.dma_start(w_raw[:, m % 2], w_v[:, :, m * P:(m + 1) * P]).then_inc(loaded[m % 2], 16)

            @block.gpsimd
            def _(pool):
                for m in range(KT):
                    pool.wait_ge(loaded[m % 2], 16 * (m // 2) + 16)
                    if m >= 2:
                        pool.wait_ge(summed, m - 1)
                    pool.tensor_copy(w_hl[:, m % 2, 0], w_raw[:, m % 2]).then_inc(w_high, 1)
                    pool.wait_ge(w_high, m + 1)
                    pool.tensor_tensor(w_hl[:, m % 2, 1], w_raw[:, m % 2], w_hl[:, m % 2, 0].bitcast(F32), ALU.subtract).then_inc(w_low, 1)

            @block.tensor
            def _(pe):
                for m in range(KT):
                    pe.wait_ge(w_low, m + 1)
                    if m >= 2:
                        pe.wait_ge(taken, m - 1)
                    for k in range(KT):
                        if m == 0:
                            pe.wait_ge(src_low, k + 1)
                        for left, right in ((0, 0), (0, 1), (1, 0)):
                            for n, (c0, wd) in enumerate(CHUNKS):
                                op = pe.matmul(ps[3 * (m % 2) + n][:, 0:wd], w_hl[:, m % 2, left, k], src_hl[:, right, k, c0:c0 + wd],
                                               start=(k == 0 and left == 0 and right == 0), stop=(k == KT - 1 and left == 1))
                    op.then_inc(summed, 1)

            @block.scalar
            def _(act):
                for k in range(KT):
                    act.activation(src_hl[:, 0, k], src[:, k], ACT.Copy).then_inc(src_high, 1)
                act.wait_ge(bias_loaded, 16)
                act.activation(bias_x[:, :], bias_sb[:, :], ACT.Copy, scale=scale).then_inc(bias_s, 1)
                act.wait_ge(bias_s, 1)
                for m in range(KT):
                    act.wait_ge(summed, m + 1)
                    if m >= 1:
                        act.wait_ge(added, m)
                    for n, (c0, wd) in enumerate(CHUNKS):
                        op = act.activation(t_sb[:, c0:c0 + wd], ps[3 * (m % 2) + n][:, 0:wd], func, bias=bias_x[:, m:m + 1], scale=scale)
                    op.then_inc(taken, 1)

            @block.vector
            def _(dve):
                for k in range(KT):
                    dve.wait_ge(src_high, k + 1)
                    dve.tensor_tensor(src_hl[:, 1, k], src[:, k], src_hl[:, 0, k].bitcast(F32), ALU.subtract).then_inc(src_low, 1)
                for m in range(KT):
                    dve.wait_ge(taken, m + 1)
                    dve.tensor_tensor(add_to[:, m], add_to[:, m], t_sb[:, :], ALU.add).then_inc(added, 1)


def stage_choose(nc, g, w_gate, src, weight, expert):
    g.new_stage()
    NE = 3
    with ExitStack() as c:
        wg = g.sb(c, "choose_wg", [P, KT, NE], F32)
        mean = g.sb(c, "choose_mean", [P, KT], F32)
        mean_wide = g.sb(c, "choose_mean_wide", [P, KT, P], F32)
        s = g.sb(c, "choose_s", [P, 16], F32)
        loaded = g.sem("choose_loaded")
        mean_s = g.sem("choose_mean_s")
        logits = g.sem("choose_logits")
        top_s = g.sem("choose_top")
        exp_s = g.sem("choose_exp")
        chain = g.sem("choose_chain")
        ps = g.psum
        top, exps, total, inv, prob, is1, is2, nof = (slice(0, 1), slice(1, 4), slice(4, 5), slice(5, 6),
                                                      slice(6, 9), slice(9, 10), slice(10, 11), slice(11, 12))
        with nc.Block() as block:
            @block.sync
            def _(sp):
                for e in range(NE):
                    sp.dma_start(wg[:, :, e], w_gate[e].rearrange("(k f) -> f k", f=P), allow_slow_non_contiguous=True).then_inc(loaded, 16)

            @block.vector
            def _(dve):
                n = [0]

                def step(op):
                    n[0] += 1
                    op.then_inc(chain, 1)
                    dve.wait_ge(chain, n[0])

                step(dve.tensor_reduce(mean[:, :], src[:, :, :], AX_X, ALU.add))
                dve.tensor_scalar(mean_wide[:, :, :], mean[:, :].unsqueeze(2).broadcast_to([P, KT, P]), 1.0 / N, None,
                                  ALU.mult).then_inc(mean_s, 1)
                dve.wait_ge(logits, 1)
                dve.tensor_reduce(s[:, top], ps[0][:, 0:NE], AX_X, ALU.max, negate=True).then_inc(top_s, 1)
                dve.wait_ge(exp_s, 1)
                step(dve.reciprocal(s[:, inv], s[:, total]))
                step(dve.tensor_scalar(s[:, prob], s[:, exps], s[:, inv], None, ALU.mult))
                step(dve.tensor_reduce(weight, s[:, prob], AX_X, ALU.max))
                step(dve.tensor_tensor(s[:, nof], s[:, 6:7], s[:, 7:8], ALU.max))
                step(dve.tensor_tensor(s[:, is2], s[:, 8:9], s[:, nof], ALU.is_gt))
                step(dve.tensor_tensor(s[:, is1], s[:, 7:8], s[:, 6:7], ALU.is_gt))
                step(dve.scalar_tensor_tensor(out=s[:, nof], in0=s[:, is2], scalar=2.0, in1=s[:, is1], op0=ALU.mult, op1=ALU.max))
                dve.tensor_copy(expert, s[:, nof])

            @block.scalar
            def _(act):
                act.wait_ge(top_s, 1)
                act.activation(s[:, exps], ps[0][:, 0:NE], ACT.Exp, bias=s[:, top], accum_out=s[:, total]).then_inc(exp_s, 1)

            @block.tensor
            def _(pe):
                pe.wait_ge(loaded, 16 * NE)
                pe.wait_ge(mean_s, 1)
                for k in range(KT):
                    op = pe.matmul(ps[0][:, 0:NE], mean_wide[:, k], wg[:, k], start=(k == 0), stop=(k == KT - 1))
                op.then_inc(logits, 1)


def stage_gcn(nc, g, w_gcn, bias, src, x_T):
    g.new_stage()
    HALF = D // 2
    with ExitStack() as c:
        w = g.sb(c, "gcn_w", [P, 2, KT, HALF], F32)
        bias_sb = g.sb(c, "gcn_bias", [P, KT], F32)
        root = g.sb(c, "gcn_root", [P, N], F32)
        norm = g.sb(c, "gcn_norm", [P, N], F32)
        norm_cols = g.sb(c, "gcn_norm_cols", [TT, NT], F32)
        h = g.sb(c, "gcn_h", [TT, NT, D], F32)
        t_sb = g.sb(c, "gcn_t", [P, 2, N], F32)
        loaded = g.sem("gcn_loaded")
        looped = g.sem("gcn_looped")
        degrees = g.sem("gcn_degrees")
        rooted = g.sem("gcn_rooted")
        normed = g.sem("gcn_normed")
        cols = g.sem("gcn_cols")
        cols_s = g.sem("gcn_cols_kept")
        projected = g.sem("gcn_projected")
        h_s = g.sem("gcn_h_s")
        summed = g.sem("gcn_summed")
        scaled = g.sem("gcn_scaled")
        added = g.sem("gcn_added")
        ps = g.psum
        with nc.Block() as block:
            @block.sync
            def _(sp):
                for i in range(2):
                    sp.dma_start(w[:, i], w_gcn.rearrange("(k f) m -> f k m", f=P)[:, :, i * HALF:(i + 1) * HALF]).then_inc(loaded, 16)
                sp.dma_start(bias_sb[:, :], bias.rearrange("(m f) -> f m", f=P), allow_slow_non_contiguous=True).then_inc(loaded, 16)

            @block.tensor
            def _(pe):
                pe.wait_ge(looped, NT)
                for n, (c0, wd) in enumerate(CHUNKS):
                    for j in range(NT):
                        op = pe.matmul(ps[n][:, 0:wd], g.ones[0:TT, :], g.counts_T[:, j, c0:c0 + wd], start=(j == 0), stop=(j == NT - 1))
                    op.then_inc(degrees, 1)
                pe.wait_ge(normed, 3)
                for t in range(NT):
                    op = pe.matmul(ps[3][0:TT, t:t + 1], norm[0:1, t * TT:(t + 1) * TT], g.ones[0:1, 0:1], start=True, stop=True)
                op.then_inc(cols, 1)
                pe.wait_ge(loaded, 48)
                for i in range(2 * NT):
                    t = i % NT
                    if i >= 4:
                        pe.wait_ge(h_s, i - 3)
                    for k in range(KT):
                        op = pe.matmul(ps[4 + i % 4][0:TT, 0:HALF], src[:, k, t * TT:(t + 1) * TT], w[:, i // NT, k],
                                       start=(k == 0), stop=(k == KT - 1))
                    op.then_inc(projected, 1)
                pe.wait_ge(h_s, 2 * NT)
                for m in range(KT):
                    if m >= 2:
                        pe.wait_ge(scaled, m - 1)
                    for j in range(NT):
                        for n, (c0, wd) in enumerate(CHUNKS):
                            op = pe.matmul(ps[3 * (m % 2) + n][:, 0:wd], h[:, j, m * P:(m + 1) * P], g.counts_T[:, j, c0:c0 + wd],
                                           start=(j == 0), stop=(j == NT - 1))
                    op.then_inc(summed, 1)

            @block.scalar
            def _(act):
                for n, (c0, wd) in enumerate(CHUNKS):
                    act.wait_ge(degrees, n + 1)
                    act.activation(root[:, c0:c0 + wd], ps[n][:, 0:wd], ACT.Sqrt).then_inc(rooted, 1)
                act.wait_ge(cols_s, 1)
                for i in range(2 * NT):
                    t, half = i % NT, i // NT
                    act.wait_ge(projected, i + 1)
                    act.activation(h[:, t, half * HALF:(half + 1) * HALF], ps[4 + i % 4][0:TT, 0:HALF], ACT.Copy,
                                   scale=norm_cols[:, t:t + 1]).then_inc(h_s, 1)

            @block.vector
            def _(dve):
                for j in range(NT):
                    own = g.counts_T[:, j, j * TT:(j + 1) * TT]
                    dve.tensor_tensor(own, own, g.ident[0:TT, 0:TT], ALU.add).then_inc(looped, 1)
                for n, (c0, wd) in enumerate(CHUNKS):
                    dve.wait_ge(rooted, n + 1)
                    dve.reciprocal(norm[:, c0:c0 + wd], root[:, c0:c0 + wd]).then_inc(normed, 1)
                dve.wait_ge(cols, 1)
                dve.tensor_copy(norm_cols[:, :], ps[3][0:TT, 0:NT]).then_inc(cols_s, 1)
                dve.wait_ge(normed, 3)
                dve.wait_ge(loaded, 48)
                for m in range(KT):
                    dve.wait_ge(summed, m + 1)
                    if m >= 2:
                        dve.wait_ge(added, m - 1)
                    for n, (c0, wd) in enumerate(CHUNKS):
                        op = dve.tensor_tensor(t_sb[:, m % 2, c0:c0 + wd], ps[3 * (m % 2) + n][:, 0:wd], norm[:, c0:c0 + wd], ALU.mult)
                    op.then_inc(scaled, 1)
                    dve.wait_ge(scaled, m + 1)
                    dve.scalar_tensor_tensor(out=x_T[:, m], in0=t_sb[:, m % 2], scalar=bias_sb[:, m:m + 1], in1=x_T[:, m],
                                             op0=ALU.add, op1=ALU.add).then_inc(added, 1)


def stage_mix1(nc, g, w_qkv, b_qkv, src, o_T):
    g.new_stage()
    EPS = 1e-6
    with ExitStack() as c:
        w = g.sb(c, "mix1_w", [P, KT, 3, P], F32)
        bias_q = g.sb(c, "mix1_bias_q", [P, KT], F32)
        bias_kv = g.sb(c, "mix1_bias_kv", [TT, 2, P], F32)
        eps = g.sb(c, "mix1_eps", [P, 1], F32)
        q_next = g.sb(c, "mix1_q_next", [P, N], F32)
        k_next = g.sb(c, "mix1_k_next", [TT, NT, P], F32)
        v_two = g.sb(c, "mix1_v_two", [TT, 2, NT, P], F32)
        q = g.sb(c, "mix1_q", [P, N], F32)
        q_eps = g.sb(c, "mix1_q_eps", [P, N], F32)
        q_sum = g.sb(c, "mix1_q_sum", [P, 2], F32)
        col_wide = g.sb(c, "mix1_col_wide", [P, 2, TT], F32)
        row = g.sb(c, "mix1_row", [TT, 2, P], F32)
        k = g.sb(c, "mix1_k", [TT, NT, P], F32)
        k_eps = g.sb(c, "mix1_k_eps", [TT, NT, P], F32)
        prod = g.sb(c, "mix1_prod", [TT, NT, P], F32)
        v = g.sb(c, "mix1_v", [TT, NT, P], F32)
        outgoing = g.sb(c, "mix1_outgoing", [TT, 4, NT, 2], F32)
        outgoing_wide = g.sb(c, "mix1_outgoing_wide", [TT, NT, P], F32)
        comp = g.sb(c, "mix1_comp", [TT, 3, NT, 2], F32)
        ends = g.sb(c, "mix1_ends", [P, 3, P], F32)
        factor = g.sb(c, "mix1_factor", [P, 3], F32)
        sink_den = g.sb(c, "mix1_sink_den", [P, N], F32)
        sink = g.sb(c, "mix1_sink", [P, N], F32)
        alloc = g.sb(c, "mix1_alloc", [P, N], F32)
        junk = g.sb(c, "mix1_junk", [P, N], F32)
        eps_s = g.sem("mix1_eps_s")
        bias_loaded = g.sem("mix1_bias_loaded")
        wq_loaded = g.sem("mix1_wq_loaded")
        wkv_loaded = g.sem("mix1_wkv_loaded")
        kv_bias_loaded = g.sem("mix1_kv_bias_loaded")
        q_projected = g.sem("mix1_q_projected")
        kv_projected = g.sem("mix1_kv_projected")
        q_kept = g.sem("mix1_q_kept")
        kv_kept = g.sem("mix1_kv_kept")
        pe_s = g.sem("mix1_products")
        act_s = g.sem("mix1_acts")
        dve_s = g.sem("mix1_dve")
        ps = g.psum
        STEPS = 33
        at = {}
        PE_OF = {n: i + 2 for i, n in enumerate(("k_sum", "q_row", "sink0", "sink1", "sink2", "k_out", "q_sink_row", "cons0",
                                                 "cons1", "cons2", "exp_sum", "kv", "o0", "o1", "o2"))}
        ACT_OF = {n: i + 1 for i, n in enumerate(("q", "k", "alloc0", "alloc1", "alloc2", "exp"))}
        KV_BANKS = (3, 0, 1, 2, 3)
        RING = (6, 7, 6)

        def pairs(engine, body):
            with engine.Fori(0, KT - 1) as p:
                body(p, True)
            body(KT - 1, False)

        with nc.Block() as block:
            @block.vector
            def _(dve):
                def keep_kv(p, b):
                    if b == 0:
                        dve.wait_ge(kv_bias_loaded, 32 * p + 32)
                    dve.wait_ge(kv_projected, 5 * p + b + 1)
                    kvb = ps[KV_BANKS[b]][0:TT, 0:512].rearrange("p (t n m) -> p t n m", t=2, n=2)
                    dve.tensor_tensor(k_next[:, 2 * b:2 * b + 2], kvb[:, :, 0], wide(bias_kv[:, 0], 2), ALU.add)
                    slot = nc.vector.snap(p % 2) if not isinstance(p, int) else p % 2
                    dve.tensor_tensor(v_two[:, bass.ds(slot, 1), 2 * b:2 * b + 2].squeeze(1), kvb[:, :, 1], wide(bias_kv[:, 1], 2),
                                      ALU.add).then_inc(kv_kept, 1)

                def body(p, more):
                    n = [0]

                    def step(op, name):
                        op.then_inc(dve_s, 1)
                        n[0] += 1
                        at[name] = n[0] + 1

                    def after(name):
                        dve.wait_ge(dve_s, STEPS * p + at[name])

                    def pe_made(name):
                        dve.wait_ge(pe_s, 15 * p + PE_OF[name])

                    def act_made(name):
                        dve.wait_ge(act_s, 6 * p + ACT_OF[name])

                    def next_kv(b):
                        if more:
                            keep_kv(p + 1, b)

                    act_made("q")
                    step(dve.tensor_scalar(col_wide[:, 0], g.ones[:, 0:TT], q_sum[:, 0:1], None, ALU.mult), "q_sum_wide")
                    step(dve.tensor_scalar(q_eps[:, :], q[:, :], EPS, None, ALU.add), "q_eps")
                    act_made("k")
                    step(dve.tensor_scalar(k_eps[:, :, :], k[:, :, :], EPS, None, ALU.add), "k_eps")
                    pe_made("k_sum")
                    step(dve.scalar_tensor_tensor(out=ends[:, 0], in0=ps[4][:, 0:P], scalar=EPS, in1=g.pair_mask[:, :],
                                                  op0=ALU.add, op1=ALU.mult), "k_sum")
                    pe_made("q_row")
                    step(dve.tensor_scalar(row[:, 0], ps[5][0:TT, 0:P], EPS, None, ALU.add), "q_row")
                    after("q_row")
                    step(dve.tensor_tensor(prod[:, :, :], k_eps[:, :, :], wide(row[:, 0], NT), ALU.mult), "prod0")
                    after("prod0")
                    step(dve.tensor_reduce(outgoing[:, 0], prod[:, :, :].rearrange("p t (h d) -> p t h d", h=2), AX_X, ALU.add), "out0")
                    after("out0")
                    step(dve.tensor_scalar(outgoing[:, 1], outgoing[:, 0], EPS, None, ALU.add), "out1")
                    after("out1")
                    step(dve.reciprocal(outgoing[:, 2], outgoing[:, 1]), "out2")
                    after("out2")
                    for hh in range(2):
                        step(dve.tensor_copy(outgoing_wide[:, :, 64 * hh:64 * hh + 64],
                                             outgoing[:, 2, :, hh:hh + 1].broadcast_to([TT, NT, 64])), "outgoing")
                    for i, (c0, wd) in enumerate(CHUNKS):
                        pe_made(f"sink{i}")
                        step(dve.tensor_scalar(sink_den[:, c0:c0 + wd], ps[RING[i]][:, 0:wd], EPS, None, ALU.add), f"sink_den{i}")
                    next_kv(0)
                    pe_made("k_out")
                    step(dve.scalar_tensor_tensor(out=ends[:, 1], in0=ps[4][:, 0:P], scalar=EPS, in1=g.pair_mask[:, :],
                                                  op0=ALU.add, op1=ALU.mult), "k_out_sum")
                    after("sink_den2")
                    step(dve.reciprocal(sink[:, :], sink_den[:, :]), "sink")
                    after("sink")
                    step(dve.tensor_tensor_reduce(junk[:, :], q[:, :], sink[:, :], 1.0, 0.0, ALU.mult, ALU.add, q_sum[:, 1:2]), "q_sink")
                    after("q_sink")
                    step(dve.tensor_scalar(col_wide[:, 1], g.ones[:, 0:TT], q_sum[:, 1:2], None, ALU.mult), "q_sink_wide")
                    next_kv(1)
                    next_kv(2)
                    pe_made("q_sink_row")
                    step(dve.tensor_scalar(row[:, 1], ps[5][0:TT, 0:P], EPS, None, ALU.add), "q_sink_row")
                    after("q_sink_row")
                    step(dve.tensor_tensor(prod[:, :, :], k_eps[:, :, :], wide(row[:, 1], NT), ALU.mult), "prod1")
                    after("prod1")
                    step(dve.tensor_reduce(comp[:, 0], prod[:, :, :].rearrange("p t (h d) -> p t h d", h=2), AX_X, ALU.add), "comp0")
                    after("comp0")
                    step(dve.tensor_scalar(comp[:, 1], comp[:, 0], EPS, 1.0, ALU.add, ALU.min), "comp1")
                    after("comp1")
                    step(dve.tensor_scalar(comp[:, 2], comp[:, 1], -1.0, None, ALU.max), "comp2")
                    act_made("exp")
                    slot = nc.vector.snap(p % 2) if more else p % 2
                    for hh in range(2):
                        cols = slice(64 * hh, 64 * hh + 64)
                        step(dve.tensor_tensor(v[:, :, cols], v_two[:, bass.ds(slot, 1), :, cols].squeeze(1),
                                               outgoing[:, 3, :, hh:hh + 1].broadcast_to([TT, NT, 64]), ALU.mult), "v")
                    next_kv(3)
                    pe_made("exp_sum")
                    step(dve.reciprocal(factor[:, 0:2], ps[4][:, 0:2]), "inv")
                    after("inv")
                    for hh in range(2):
                        r = slice(64 * hh, 64 * hh + 64)
                        step(dve.tensor_scalar(factor[r, 2:3], factor[r, hh:hh + 1], float(N), None, ALU.mult), "factor")
                    after("factor")
                    pe_made("kv")
                    step(dve.scalar_tensor_tensor(out=ends[:, 2], in0=ps[5][:, 0:P], scalar=factor[:, 2:3], in1=g.pair_mask[:, :],
                                                  op0=ALU.mult, op1=ALU.mult), "kv")
                    act_made("alloc2")
                    step(dve.tensor_tensor(junk[:, :], sink[:, :], alloc[:, :], ALU.mult), "gain")
                    next_kv(4)
                    after("gain")
                    for i, (c0, wd) in enumerate(CHUNKS):
                        pe_made(f"o{i}")
                        step(dve.tensor_tensor(o_T[:, bass.ds(p, 1), c0:c0 + wd].squeeze(1), ps[RING[i]][:, 0:wd], junk[:, c0:c0 + wd], ALU.mult), f"o{i}")
                    assert n[0] == STEPS, n[0]

                dve.sem_inc(dve_s, 1)
                for b in range(5):
                    keep_kv(0, b)
                pairs(dve, body)

            @block.sync
            def _(sp):
                def load(sem, p, parts):
                    for n in parts:
                        sp.dma_start(w[:, :, n], w_qkv.rearrange("(k f) (n m) -> f k n m", f=P, n=3)[:, :, n, bass.ds(p * P, P)]).then_inc(sem, 16)

                def load_bias(p):
                    for n in range(2):
                        sp.dma_start(bias_kv[:, n], b_qkv.rearrange("(n m) -> n m", n=3)[n + 1:n + 2, bass.ds(p * P, P)].partition_broadcast(TT)).then_inc(kv_bias_loaded, 16)

                sp.dma_start(bias_q[:, :], b_qkv[0:D].rearrange("(m f) -> f m", f=P), allow_slow_non_contiguous=True).then_inc(bias_loaded, 16)
                load(wq_loaded, 0, (0,))
                load(wkv_loaded, 0, (1, 2))
                load_bias(0)
                with sp.Fori(1, KT) as p:
                    sp.wait_ge(q_projected, p)
                    load(wq_loaded, p, (0,))
                    sp.wait_ge(kv_projected, 5 * p)
                    load(wkv_loaded, p, (1, 2))
                    sp.wait_ge(kv_kept, 5 * p)
                    load_bias(p)

            @block.gpsimd
            def _(pool):
                pool.memset(eps[:, :], EPS).then_inc(eps_s, 1)
                pool.sem_inc(pe_s, 1)

            @block.tensor
            def _(pe):
                def project_q(p):
                    pe.wait_ge(wq_loaded, 16 * p + 16)
                    project_T(pe, ps[0:3], w[:, :, 0], src).then_inc(q_projected, 1)

                def project_kv(p, b):
                    if b == 0:
                        pe.wait_ge(wkv_loaded, 32 * p + 32)
                    if b == 1:
                        pe.wait_ge(q_kept, p + 1)
                    if b == 4:
                        pe.wait_ge(kv_kept, 5 * p + 1)
                    for t in (2 * b, 2 * b + 1):
                        for kk in range(KT):
                            op = pe.matmul(ps[KV_BANKS[b]][0:TT, (t % 2) * 256:(t % 2) * 256 + 256],
                                           src[:, kk, t * TT:(t + 1) * TT], w[:, kk, 1:3, :],
                                           start=(kk == 0), stop=(kk == KT - 1))
                    op.then_inc(kv_projected, 1)

                def body(p, more):
                    def made(name):
                        pe.wait_ge(dve_s, STEPS * p + at[name])

                    def next_kv(b):
                        if more:
                            project_kv(p + 1, b)

                    def by_tokens(bank_, rhs, width):
                        for t in range(NT):
                            op = pe.matmul(ps[bank_][:, 0:width], k[:, t], rhs(t), start=(t == 0), stop=(t == NT - 1))
                        op.then_inc(pe_s, 1)

                    pe.wait_ge(kv_kept, 5 * p + 5)
                    if more:
                        project_q(p + 1)
                    pe.wait_ge(act_s, 6 * p + ACT_OF["k"])
                    by_tokens(4, lambda t: g.ones[0:TT, :], P)
                    made("q_sum_wide")
                    pe.matmul(ps[5][0:TT, 0:P], col_wide[:, 0], g.ident[:, :], start=True, stop=True).then_inc(pe_s, 1)
                    next_kv(0)
                    made("k_sum")
                    pe.wait_ge(dve_s, STEPS * p + 1)
                    for i, (c0, wd) in enumerate(CHUNKS):
                        if i == 2:
                            made("sink_den0")
                        pe.matmul(ps[RING[i]][:, 0:wd], ends[:, 0], q_eps[:, c0:c0 + wd], start=True, stop=True).then_inc(pe_s, 1)
                    made("outgoing")
                    by_tokens(4, lambda t: outgoing_wide[:, t], P)
                    next_kv(1)
                    next_kv(2)
                    made("q_sink_wide")
                    pe.matmul(ps[5][0:TT, 0:P], col_wide[:, 1], g.ident[:, :], start=True, stop=True).then_inc(pe_s, 1)
                    made("k_out_sum")
                    for i, (c0, wd) in enumerate(CHUNKS):
                        if i == 2:
                            pe.wait_ge(act_s, 6 * p + ACT_OF["alloc0"])
                        pe.matmul(ps[RING[i]][:, 0:wd], ends[:, 1], q_eps[:, c0:c0 + wd], start=True, stop=True).then_inc(pe_s, 1)
                    next_kv(3)
                    pe.wait_ge(act_s, 6 * p + ACT_OF["exp"])
                    for t in range(NT):
                        op = pe.matmul(ps[4][:, 0:2], g.ones[0:TT, :], outgoing[:, 3, t], start=(t == 0), stop=(t == NT - 1))
                    op.then_inc(pe_s, 1)
                    made("v")
                    by_tokens(5, lambda t: v[:, t], P)
                    next_kv(4)
                    made("kv")
                    for i, (c0, wd) in enumerate(CHUNKS):
                        if i == 2:
                            made("o0")
                        pe.matmul(ps[RING[i]][:, 0:wd], ends[:, 2], q[:, c0:c0 + wd], start=True, stop=True).then_inc(pe_s, 1)

                pe.wait_ge(eps_s, 1)
                project_q(0)
                for b in range(5):
                    project_kv(0, b)
                pairs(pe, body)

            @block.scalar
            def _(act):
                def keep_q(p):
                    act.wait_ge(q_projected, p + 1)
                    for i, (c0, wd) in enumerate(CHUNKS):
                        op = act.activation(q_next[:, c0:c0 + wd], ps[i][:, 0:wd], ACT.Identity, bias=bias_q[:, bass.ds(p, 1)])
                    op.then_inc(q_kept, 1)

                def body(p, more):
                    act.wait_ge(q_kept, p + 1)
                    act.wait_ge(pe_s, 15 * p + 1)
                    act.activation(q[:, :], q_next[:, :], ACT.Sigmoid, accum_out=q_sum[:, 0:1]).then_inc(act_s, 1)
                    act.wait_ge(kv_kept, 5 * p + 5)
                    act.activation(k[:, :, :], k_next[:, :, :], ACT.Sigmoid).then_inc(act_s, 1)
                    if more:
                        act.wait_ge(act_s, 6 * p + ACT_OF["q"])
                        keep_q(p + 1)
                    for i, (c0, wd) in enumerate(CHUNKS):
                        act.wait_ge(pe_s, 15 * p + PE_OF[f"cons{i}"])
                        act.activation(alloc[:, c0:c0 + wd], ps[RING[i]][:, 0:wd], ACT.Sigmoid, bias=eps[:, 0:1]).then_inc(act_s, 1)
                    act.wait_ge(dve_s, STEPS * p + at["comp2"])
                    act.activation(outgoing[:, 3], comp[:, 2], ACT.Exp).then_inc(act_s, 1)

                act.wait_ge(bias_loaded, 16)
                act.wait_ge(eps_s, 1)
                keep_q(0)
                pairs(act, body)


def stage_attention(nc, g, w_qkv, b_qkv, src, o_T):
    g.new_stage()
    STEPS = 2 * NT
    NC = len(CHUNKS)
    CH = STEPS * NC
    MC = NT * NC
    with ExitStack() as c:
        w = g.sb(c, "att_w", [P, KT, 3, P], F32)
        bias_qk = g.sb(c, "att_bias_qk", [P, 2, KT], F32)
        bias_v = g.sb(c, "att_bias_v", [TT, 2, 64], F32)
        q_a = g.sb(c, "att_q_a", [P, 2, N], F32R)
        q_b = g.sb(c, "att_q_b", [P, 2, N], F32R)
        k_a = g.sb(c, "att_k_a", [P, 2, N], F32R)
        k_b = g.sb(c, "att_k_b", [P, 2, N], F32R)
        v = g.sb(c, "att_v", [TT, NT, 3, 64], F32)
        block_mask = g.sb(c, "att_block_mask", [NT, NT, TT], BF16)
        top = g.sb(c, "att_top", [TT, NT, NC], F32)
        neg_top = g.sb(c, "att_neg_top", [TT, NT], F32)
        prob = g.sb(c, "att_prob", [TT, 2, N], F32)
        raw = g.sb(c, "att_raw", [P, 2, N], F32)
        inv = g.sb(c, "att_inv", [P, N], F32)
        filled = g.sem("att_filled")
        bias_loaded = g.sem("att_bias_loaded")
        loaded = g.sem("att_w_loaded")
        v_bias_loaded = g.sem("att_v_bias_loaded")
        w_used = g.sem("att_w_used")
        projected = g.sem("att_projected")
        k_projected = g.sem("att_k_projected")
        q_high = g.sem("att_q_high")
        k_high = g.sem("att_k_high")
        k_turn = g.sem("att_k_turn")
        copied = g.sem("att_q_b_copied")
        copy_turn = g.sem("att_copy_turn")
        lows = g.sem("att_lows")
        v_s = g.sem("att_v_s")
        sampled = g.sem("att_sampled")
        reduced = g.sem("att_reduced")
        maxed = g.sem("att_maxed")
        turned = g.sem("att_max_turned")
        shifts = g.sem("att_shifts")
        scored = g.sem("att_scored")
        exped = g.sem("att_exped")
        summed = g.sem("att_summed")
        taken = g.sem("att_taken")
        inverted = g.sem("att_inverted")
        done = g.sem("att_done")
        ps = g.psum
        THIRDS = ((0, 4), (4, 8), (8, 10))
        own = (slice(0, 64), slice(64, 128))
        other = (slice(64, 128), slice(0, 64))
        shift_rows = (slice(64, 64 + NT), slice(0, NT))
        with nc.Block() as block:
            @block.sync
            def _(sp):
                sp.dma_start(bias_qk[:, :, :], b_qkv[0:2 * D].rearrange("(n m f) -> f n m", f=P, n=2), allow_slow_non_contiguous=True).then_inc(bias_loaded, 16)
                with sp.Fori(0, KT) as p:
                    sp.wait_ge(w_used, p + 1)
                    for n in range(3):
                        sp.dma_start(w[:, :, n], w_qkv.rearrange("(k f) (n m) -> f k n m", f=P, n=3)[:, :, n, bass.ds(p * P, P)]).then_inc(loaded, 16)
                    sp.wait_ge(v_s, 3 * p + 1)
                    sp.dma_start(bias_v[:, :, :].rearrange("p h e -> p (h e)"),
                                 b_qkv.rearrange("(n m) -> n m", n=3)[2:3, bass.ds(p * P, P)].partition_broadcast(TT)).then_inc(v_bias_loaded, 16)

            @block.gpsimd
            def _(pool):
                pool.sem_inc(w_used, 1)
                fills = [(v[:, :, 1], 1.0), (block_mask[:, :, :], 0.0)]
                for h in range(2):
                    fills += [(q_b[other[h], h].bitcast(F32), 0.0), (k_b[other[h], h].bitcast(F32), 0.0),
                              (k_b[shift_rows[h], h].bitcast(F32), 1.0)]
                for n, (to, value) in enumerate(fills):
                    pool.memset(to, value).then_inc(filled, 1)
                    pool.wait_ge(filled, n + 1)
                pool.affine_select(out=block_mask[:, :, :], in_=block_mask[:, :, :], compare_op=ALU.not_equal, fill=1.0,
                                   base=0, pattern=[[-1, NT], [0, TT]], channel_multiplier=1).then_inc(filled, 1)
                pool.wait_ge(filled, 9)
                with pool.Fori(0, KT) as p:
                    pool.wait_ge(q_high, p + 1)
                    pool.sem_inc(copy_turn, 1)
                    for h in range(2):
                        pool.tensor_copy(q_b[own[h], h], q_a[own[h], h]).then_inc(copied, 1)
                    pool.wait_ge(copied, 2 * p + 2)

            @block.tensor
            def _(pe):
                pe.wait_ge(filled, 9)
                with pe.Fori(0, KT) as p:
                    pe.wait_ge(loaded, 48 * p + 48)
                    pe.wait_ge(exped, CH * p + NC)
                    project_T(pe, ps[3:6], w[:, :, 0], src).then_inc(projected, 1)
                    pe.wait_ge(taken, 2 * p + 1)
                    for n, (c0, wd) in enumerate(CHUNKS):
                        for kk in range(KT):
                            op = pe.matmul(ps[n][:, 0:wd], w[:, kk, 1], src[:, kk, c0:c0 + wd], start=(kk == 0), stop=(kk == KT - 1))
                        op.then_inc(k_projected, 1)
                    pe.wait_ge(lows, 3 * p + 1)

                    def project_v(t):
                        b = t // 4
                        for kk in range(KT):
                            op = pe.matmul(ps[3 + b][0:TT, (t % 4) * P:(t % 4 + 1) * P], src[:, kk, t * TT:(t + 1) * TT],
                                           w[:, kk, 2], start=(kk == 0), stop=(kk == KT - 1))
                        if t + 1 == THIRDS[b][1]:
                            op.then_inc(projected, 1)

                    def sample(s):
                        h, t, n = s // MC, s % MC // NC, s % NC
                        c0, wd = CHUNKS[n]
                        if s == 0:
                            pe.wait_ge(lows, 3 * p + 2)
                        if s == MC:
                            pe.wait_ge(shifts, 2 * p + 1)
                        pe.wait_ge(reduced, CH * p + s + 1)
                        pe.matmul(ps[6 + s % 2][0:TT, 0:wd], q_a[:, h, t * TT:(t + 1) * TT], k_a[:, h, c0:c0 + wd],
                                  start=True, stop=True).then_inc(sampled, 1)

                    def turn_maxima(h):
                        pe.wait_ge(maxed, 2 * p + h + 1)
                        pe.matmul(ps[6][0:NT, 0:TT], neg_top[:, :], g.ident[0:TT, 0:TT], start=True, stop=True).then_inc(turned, 1)

                    def scores(i):
                        h, j = i // NT, i % NT
                        if i == 0:
                            pe.wait_ge(lows, 3 * p + 3)
                            pe.wait_ge(copied, 2 * p + 2)
                            pe.wait_ge(v_s, 3 * p + 4)
                        if j == 0:
                            pe.wait_ge(shifts, 2 * p + h + 1)
                        for n, (c0, wd) in enumerate(CHUNKS):
                            pe.wait_ge(exped, CH * p + NC * i + n + 1)
                            pe.matmul(ps[3 + n][0:TT, 0:wd], k_a[:, h, j * TT:(j + 1) * TT], q_a[:, h, c0:c0 + wd], start=True, stop=False)
                            pe.matmul(ps[3 + n][0:TT, 0:wd], k_b[:, h, j * TT:(j + 1) * TT], q_b[:, h, c0:c0 + wd],
                                      start=False, stop=True).then_inc(scored, 1)

                    def weigh(i, n):
                        h, j = i // NT, i % NT
                        c0, wd = CHUNKS[n]
                        if n == 0:
                            pe.wait_ge(exped, CH * p + NC * i + 2 * NC)
                            if j == 0:
                                pe.wait_ge(taken, 2 * p + h + 1)
                        op = pe.matmul(ps[n][:, 0:wd], v[:, j, h:h + 2], prob[:, i % 2, c0:c0 + wd], start=(j == 0), stop=(j == NT - 1))
                        if n == NC - 1:
                            op.then_inc(summed, 1)

                    AHEAD = 2
                    for t in range(AHEAD):
                        project_v(t)
                    for t in range(NT):
                        for n in range(NC):
                            sample(t * NC + n)
                        if t + AHEAD < NT:
                            project_v(t + AHEAD)
                        if t + AHEAD == NT:
                            pe.wait_ge(projected, 4 * p + 4)
                            pe.sem_inc(w_used, 1)
                    turn_maxima(0)
                    s = MC
                    scores(0)
                    for i in range(STEPS):
                        if i + 1 < STEPS:
                            scores(i + 1)
                        for n in range(NC):
                            for _ in range(2 if n == 1 else 1):
                                if s < CH:
                                    sample(s)
                                    s += 1
                            weigh(i, n)
                        if i == NT - 3:
                            turn_maxima(1)

            @block.scalar
            def _(act):
                act.sem_inc(exped, NC)
                act.sem_inc(taken, 1)
                act.wait_ge(bias_loaded, 16)
                with act.Fori(0, KT) as p:
                    def high(i, to, b0, n):
                        c0, wd = CHUNKS[n]
                        for h in range(2):
                            op = act.activation(to[own[h], h, c0:c0 + wd], ps[b0 + n][own[h], 0:wd], ACT.Identity,
                                                bias=bias_qk[own[h], i, bass.ds(p, 1)])
                        return op

                    act.wait_ge(projected, 4 * p + 1)
                    for n in range(NC):
                        op = high(0, q_a, 3, n)
                    op.then_inc(q_high, 1)
                    for n in range(NC):
                        act.wait_ge(k_projected, NC * p + n + 1)
                        act.sem_inc(k_turn, 1)
                        high(1, k_a, 0, n).then_inc(k_high, 1)

                    def take(h):
                        act.wait_ge(summed, STEPS * p + NT * (h + 1) + 2)
                        act.wait_ge(done, 2 * p + h + 1)
                        for n, (c0, wd) in enumerate(CHUNKS):
                            op = act.activation(raw[:, h, c0:c0 + wd], ps[n][:, 0:wd], ACT.Copy)
                        op.then_inc(taken, 1)

                    for i in range(STEPS):
                        act.wait_ge(summed, STEPS * p + i + 1)
                        for n, (c0, wd) in enumerate(CHUNKS):
                            act.wait_ge(scored, CH * p + NC * i + n + 1)
                            act.activation(prob[:, i % 2, c0:c0 + wd], ps[3 + n][0:TT, 0:wd], ACT.Exp, scale=0.125).then_inc(exped, 1)
                        if i == NT:
                            take(0)
                    take(1)

            @block.vector
            def _(dve):
                dve.sem_inc(reduced, 2)
                dve.sem_inc(summed, 2)
                dve.sem_inc(v_s, 1)
                dve.sem_inc(done, 2)
                dve.wait_ge(bias_loaded, 16)
                dve.wait_ge(filled, 9)
                with dve.Fori(0, KT) as p:
                    def low(i, to, high, b0, half, n):
                        c0, wd = CHUNKS[n]
                        for h in range(2):
                            op = dve.scalar_tensor_tensor(out=to[half[h], h, c0:c0 + wd], in0=ps[b0 + n][own[h], 0:wd],
                                                          scalar=bias_qk[own[h], i, bass.ds(p, 1)],
                                                          in1=high[own[h], h, c0:c0 + wd].bitcast(F32),
                                                          op0=ALU.add, op1=ALU.subtract)
                        return op

                    dve.wait_ge(q_high, p + 1)
                    for n in range(NC):
                        op = low(0, q_a, q_a, 3, other, n)
                    op.then_inc(lows, 1)
                    for n, (c0, wd) in enumerate(CHUNKS):
                        dve.wait_ge(k_high, NC * p + n + 1)
                        for h in range(2):
                            op = dve.tensor_copy(k_a[other[h], h, c0:c0 + wd], k_a[own[h], h, c0:c0 + wd])
                        if n == NC - 1:
                            op.then_inc(lows, 1)
                        op = low(1, k_b, k_a, 0, own, n)
                        if n == NC - 1:
                            op.then_inc(lows, 1)
                    dve.wait_ge(v_bias_loaded, 16 * p + 16)

                    def keep_v(b):
                        t0, t1 = THIRDS[b]
                        dve.wait_ge(projected, 4 * p + b + 2)
                        dve.tensor_tensor(v[:, t0:t1, 0:3:2], ps[3 + b][0:TT, 0:(t1 - t0) * P].rearrange("p (t h e) -> p t h e", h=2, e=64),
                                          bias_v[:, :, :].unsqueeze(1).broadcast_to([TT, t1 - t0, 2, 64]), ALU.add).then_inc(v_s, 1)

                    def most(s):
                        wd = CHUNKS[s % NC][1]
                        dve.wait_ge(sampled, CH * p + s + 1)
                        dve.tensor_reduce(top[:, s % MC // NC, s % NC:s % NC + 1], ps[6 + s % 2][0:TT, 0:wd], AX_X, ALU.max).then_inc(reduced, 1)

                    def shift(h):
                        dve.wait_ge(reduced, CH * p + MC * (h + 1) + 2)
                        dve.tensor_reduce(neg_top[:, :], top[:, :, :], AX_X, ALU.max, negate=True).then_inc(maxed, 1)
                        dve.wait_ge(turned, 2 * p + h + 1)
                        dve.tensor_tensor(q_b[shift_rows[h], h].rearrange("p (t n) -> p t n", n=TT), wide(ps[6][0:NT, 0:TT], NT),
                                          block_mask[:, :, :], ALU.mult).then_inc(shifts, 1)

                    def finish(h):
                        dve.wait_ge(taken, 2 * p + h + 2)
                        dve.reciprocal(inv[own[h], :], raw[other[h], h]).then_inc(inverted, 1)
                        dve.wait_ge(inverted, 2 * p + h + 1)
                        dve.tensor_tensor(o_T[own[h], bass.ds(p, 1), :].squeeze(1), raw[own[h], h], inv[own[h], :], ALU.mult).then_inc(done, 1)

                    for s in range(MC):
                        most(s)
                        if s in (2 * NC, 6 * NC, 8 * NC):
                            keep_v((2, 6, 8).index(s // NC))
                    shift(0)
                    for s in range(MC, CH):
                        most(s)
                    shift(1)
                    finish(0)
                    finish(1)


def stage_gates(nc, g, gate_w, b2, src, z_T, y_high, y_low):
    g.new_stage()
    NE = 8
    with ExitStack() as c:
        wg = g.sb(c, "gates_w", [P, KT, NE], F32)
        b2_sb = g.sb(c, "gates_b2", [NE, D], F32)
        logit = g.sb(c, "gates_logit", [TT, NT, NE], F32)
        above = g.sb(c, "gates_above", [TT, NT, NE, NE], F32)
        equal = g.sb(c, "gates_equal", [TT, NT, NE, NE], F32)
        lower = g.sb(c, "gates_lower", [TT, NE, NE], F32)
        rank = g.sb(c, "gates_rank", [TT, NT, NE], F32)
        top = g.sb(c, "gates_top", [TT, NT, 3], F32)
        diff = g.sb(c, "gates_diff", [TT, NT, NE], F32)
        gate = g.sb(c, "gates_gate", [TT, NT, NE], F32)
        rows = g.sb(c, "gates_rows", [NE, N], F32)
        loaded = g.sem("gates_loaded")
        lower_s = g.sem("gates_lower_s")
        logit_rows = g.sem("gates_logit_rows")
        logit_rows_kept = g.sem("gates_logit_rows_kept")
        logits = g.sem("gates_logits")
        chain = g.sem("gates_chain")
        diffed = g.sem("gates_diffed")
        exped = g.sem("gates_exped")
        gated = g.sem("gates_gated")
        turned = g.sem("gates_turned")
        row_kept = g.sem("gates_row_kept")
        stored = g.sem("gates_stored")
        biased = g.sem("gates_biased")
        added = g.sem("gates_added")
        high_s = g.sem("gates_y_high")
        ps = g.psum
        with nc.Block() as block:
            @block.sync
            def _(sp):
                sp.dma_start(wg[:, :, :], gate_w.rearrange("(k f) e -> f k e", f=P)).then_inc(loaded, 16)
                sp.dma_start(b2_sb[:, :], b2).then_inc(loaded, 16)
                sp.wait_ge(row_kept, NT)
                sp.dma_start(g.gates_dram, rows[:, :]).then_inc(stored, 16)
                sp.wait_ge(stored, 16)

            @block.gpsimd
            def _(pool):
                pool.memset(lower[:, :, :], 1.0).then_inc(lower_s, 1)
                pool.wait_ge(lower_s, 1)
                pool.affine_select(out=lower[:, :, :], in_=lower[:, :, :], compare_op=ALU.is_gt, fill=0.0,
                                   base=0, pattern=[[1, NE], [-1, NE]], channel_multiplier=0).then_inc(lower_s, 1)

            @block.tensor
            def _(pe):
                pe.wait_ge(loaded, 32)
                for n, (c0, wd) in enumerate(CHUNKS):
                    for k in range(KT):
                        op = pe.matmul(ps[5 + n][0:NE, 0:wd], wg[:, k], src[:, k, c0:c0 + wd], start=(k == 0), stop=(k == KT - 1))
                    op.then_inc(logit_rows, 1)
                pe.wait_ge(logit_rows_kept, 3)
                for t in range(NT):
                    op = pe.transpose(ps[0][0:TT, t * NE:(t + 1) * NE], rows[:, t * TT:(t + 1) * TT], g.ident[0:NE, 0:NE])
                op.then_inc(logits, 1)
                pe.wait_ge(gated, 1)
                for t in range(NT):
                    if t >= 2:
                        pe.wait_ge(row_kept, t - 1)
                    pe.transpose(ps[t % 2][0:NE, 0:TT], gate[:, t], g.ident[0:TT, 0:TT]).then_inc(turned, 1)
                pe.wait_ge(row_kept, NT)
                for m in range(KT):
                    if m >= 2:
                        pe.wait_ge(added, m - 1)
                    for n, (c0, wd) in enumerate(CHUNKS):
                        op = pe.matmul(ps[2 + 3 * (m % 2) + n][:, 0:wd], b2_sb[:, m * P:(m + 1) * P], rows[:, c0:c0 + wd], start=True, stop=True)
                    op.then_inc(biased, 1)

            @block.scalar
            def _(act):
                for k in range(KT):
                    act.activation(y_high[:, k], src[:, k], ACT.Copy).then_inc(high_s, 1)
                for n, (c0, wd) in enumerate(CHUNKS):
                    act.wait_ge(logit_rows, n + 1)
                    act.activation(rows[:, c0:c0 + wd], ps[5 + n][0:NE, 0:wd], ACT.Copy).then_inc(logit_rows_kept, 1)
                act.wait_ge(diffed, 1)
                act.activation(diff[:, :, :], diff[:, :, :], ACT.Exp).then_inc(exped, 1)

            @block.vector
            def _(dve):
                n = [0]

                def step(op):
                    n[0] += 1
                    op.then_inc(chain, 1)
                    dve.wait_ge(chain, n[0])

                for k in range(KT):
                    dve.wait_ge(high_s, k + 1)
                    dve.tensor_tensor(y_low[:, k], src[:, k], y_high[:, k].bitcast(F32), ALU.subtract)
                dve.wait_ge(logits, 1)
                step(dve.tensor_copy(logit[:, :, :], ps[0][0:TT, 0:NT * NE].rearrange("p (t e) -> p t e", e=NE)))
                step(dve.tensor_reduce(top[:, :, 0:1], logit[:, :, :], AX_X, ALU.max))
                dve.tensor_tensor(diff[:, :, :], logit[:, :, :], top[:, :, 0:1].broadcast_to([TT, NT, NE]), ALU.subtract).then_inc(diffed, 1)
                of_f = logit[:, :, :].unsqueeze(2).broadcast_to([TT, NT, NE, NE])
                of_e = logit[:, :, :].unsqueeze(3).broadcast_to([TT, NT, NE, NE])
                step(dve.tensor_tensor(above[:, :, :, :], of_f, of_e, ALU.is_gt))
                step(dve.tensor_tensor(equal[:, :, :, :], of_f, of_e, ALU.is_equal))
                dve.wait_ge(lower_s, 2)
                step(dve.tensor_tensor(equal[:, :, :, :], equal[:, :, :, :], lower[:, :, :].unsqueeze(1).broadcast_to([TT, NT, NE, NE]), ALU.mult))
                step(dve.tensor_tensor(above[:, :, :, :], above[:, :, :, :], equal[:, :, :, :], ALU.add))
                step(dve.tensor_reduce(rank[:, :, :], above[:, :, :, :], AX_X, ALU.add))
                dve.wait_ge(exped, 1)
                step(dve.scalar_tensor_tensor(out=diff[:, :, :], in0=rank[:, :, :], scalar=2.0, in1=diff[:, :, :], op0=ALU.is_lt, op1=ALU.mult))
                step(dve.tensor_reduce(top[:, :, 1:2], diff[:, :, :], AX_X, ALU.add))
                step(dve.reciprocal(top[:, :, 2:3], top[:, :, 1:2]))
                dve.tensor_tensor(gate[:, :, :], diff[:, :, :], top[:, :, 2:3].broadcast_to([TT, NT, NE]), ALU.mult).then_inc(gated, 1)
                for t in range(NT):
                    dve.wait_ge(turned, t + 1)
                    dve.tensor_copy(rows[:, t * TT:(t + 1) * TT], ps[t % 2][0:NE, 0:TT]).then_inc(row_kept, 1)
                for m in range(KT):
                    dve.wait_ge(biased, m + 1)
                    for i, (c0, wd) in enumerate(CHUNKS):
                        op = dve.tensor_tensor(z_T[:, m, c0:c0 + wd], z_T[:, m, c0:c0 + wd], ps[2 + 3 * (m % 2) + i][:, 0:wd], ALU.add)
                    op.then_inc(added, 1)


def stage_experts(nc, g, w1, b1, w2, y_high, y_low, spare, acc):
    g.new_stage()
    NE, HT = 8, 3
    with ExitStack() as c:
        W1N, W2N = KT * HT * P, HT * D
        w1_raw = spare[:, 0:W1N].rearrange("p (k m) -> p k m", k=KT)
        w2_raw = spare[:, W1N:W1N + W2N].rearrange("p (k m) -> p k m", k=HT)
        gate = spare[:, W1N + W2N:W1N + W2N + N]
        w1_hl = g.sb(c, "exp_w1", [P, 2, KT, HT * P], F32R)
        w2_hl = g.sb(c, "exp_w2", [P, 2, HT, D], F32R)
        b1_sb = g.sb(c, "exp_b1", [P, NE, HT], F32)
        hid = g.sb(c, "exp_hid", [P, HT, N], F32)
        hid_hl = g.sb(c, "exp_hid_hl", [P, 2, HT, N], F32R)
        b1_loaded = g.sem("exp_b1_loaded")
        w1_loaded, w2_loaded = g.sem("exp_w1_loaded"), g.sem("exp_w2_loaded")
        w1_high, w1_low = g.sem("exp_w1_high"), g.sem("exp_w1_low")
        w2_high, w2_low = g.sem("exp_w2_high"), g.sem("exp_w2_low")
        gate_loaded = g.sem("exp_gate_loaded")
        up = g.sem("exp_up")
        made = g.sem("exp_made")
        gated = g.sem("exp_gated")
        hid_high, hid_low = g.sem("exp_hid_high"), g.sem("exp_hid_low")
        down = g.sem("exp_down")
        drained = g.sem("exp_drained")
        pool_turn = g.sem("exp_pool_turn")
        ps = g.psum
        w1_v = w1.rearrange("e (k f) m -> f e k m", f=P)
        w2_v = w2.rearrange("e (k f) m -> f e k m", f=P)
        X, Y, Z = (0, 1, 2), (3, 4, 5), (6, 7, 5)
        UP_BANKS, DOWN_BANKS = (X, Y, X), (Y, X, Y, X, Y, Z)

        def experts(engine, body):
            with engine.Fori(0, NE - 1) as e:
                body(e)
            body(NE - 1)

        with nc.Block() as block:
            @block.sync
            def _(sp):
                sp.dma_start(w1_raw, w1_v[:, 0]).then_inc(w1_loaded, 16)
                sp.dma_start(b1_sb[:, :, :], b1.rearrange("e (m f) -> f e m", f=P), allow_slow_non_contiguous=True).then_inc(b1_loaded, 16)
                sp.dma_start(w2_raw, w2_v[:, 0]).then_inc(w2_loaded, 16)
                sp.dma_start(gate, g.gates_dram[0:1, :].partition_broadcast(P)).then_inc(gate_loaded, 16)
                with sp.Fori(1, NE) as e:
                    sp.wait_ge(w1_low, e)
                    sp.dma_start(w1_raw, w1_v[:, bass.ds(e, 1)].squeeze(1)).then_inc(w1_loaded, 16)
                    sp.wait_ge(w2_low, e)
                    sp.dma_start(w2_raw, w2_v[:, bass.ds(e, 1)].squeeze(1)).then_inc(w2_loaded, 16)
                    sp.wait_ge(gated, HT * e)
                    sp.dma_start(gate, g.gates_dram[bass.ds(e, 1), :].partition_broadcast(P)).then_inc(gate_loaded, 16)

            @block.gpsimd
            def _(pool):
                def low_of(hl, raw, high_sem, e, sem):
                    pool.wait_ge(high_sem, e + 1)
                    pool.sem_inc(pool_turn, 1)
                    pool.tensor_tensor(hl[:, 1], raw, hl[:, 0].bitcast(F32), ALU.subtract).then_inc(sem, 1)

                for e in range(2):
                    low_of(w1_hl, w1_raw, w1_high, e, w1_low)
                with pool.Fori(0, NE - 2) as e:
                    low_of(w2_hl, w2_raw, w2_high, e, w2_low)
                    low_of(w1_hl, w1_raw, w1_high, e + 2, w1_low)
                for e in (NE - 2, NE - 1):
                    low_of(w2_hl, w2_raw, w2_high, e, w2_low)

            @block.tensor
            def _(pe):
                def products(banks, hl, k_tiles, cols, right, chunks, sem):
                    for k in range(k_tiles):
                        for left, right_parts in ((0, (0, 1)), (1, (0,))):
                            for part in right_parts:
                                for n in chunks:
                                    c0, wd = CHUNKS[n]
                                    op = pe.matmul(ps[banks[n]][:, 0:wd], hl[:, left, k, cols], right[part][:, k, c0:c0 + wd],
                                                   start=(k == 0 and left == 0 and part == 0), stop=(k == k_tiles - 1 and left == 1))
                    if sem is not None:
                        op.then_inc(sem, 1)

                def first(e, m):
                    products(UP_BANKS[m], w1_hl, KT, slice(m * P, (m + 1) * P), (y_high, y_low), range(3), up)

                def second(e):
                    pe.wait_ge(w2_low, e + 1)
                    pe.wait_ge(hid_low, HT * e + 2 * HT)
                    hid_parts = (hid_hl[:, 0], hid_hl[:, 1])
                    for m in range(KT):
                        cols = slice(m * P, (m + 1) * P)
                        if m >= 2:
                            pe.wait_ge(drained, KT * e + m + KT - 1)
                        if DOWN_BANKS[m] is not Z:
                            products(DOWN_BANKS[m], w2_hl, HT, cols, hid_parts, range(3), down)
                        else:
                            products(Z, w2_hl, HT, cols, hid_parts, (0, 1), None)
                            pe.wait_ge(drained, KT * e + m + KT)
                            products(Z, w2_hl, HT, cols, hid_parts, (2,), down)

                pe.wait_ge(w1_low, 1)
                for m in range(HT):
                    if m == 2:
                        pe.wait_ge(made, 1)
                    first(0, m)
                with pe.Fori(0, NE - 1) as e:
                    pe.wait_ge(w1_low, e + 2)
                    for m in range(HT):
                        if m == 0:
                            pe.wait_ge(drained, KT * e + 4)
                            pe.wait_ge(made, HT * e + 3)
                        elif m == 1:
                            pe.wait_ge(drained, KT * e + KT)
                        else:
                            pe.wait_ge(made, HT * e + HT + 1)
                        first(e + 1, m)
                    pe.wait_ge(made, HT * e + HT + 3)
                    second(e)
                pe.wait_ge(drained, KT * NE)
                second(NE - 1)

            @block.scalar
            def _(act):
                def high_of(hl, raw, loaded, e, last_used, sem):
                    act.wait_ge(loaded, 16 * e + 16)
                    if last_used is not None:
                        act.wait_ge(*last_used)
                    act.activation(hl[:, 0], raw, ACT.Copy).then_inc(sem, 1)

                def gelu(e, m):
                    act.wait_ge(up, HT * e + m + 1)
                    act.wait_ge(hid_low, HT * e + m + 1)
                    for n, (c0, wd) in enumerate(CHUNKS):
                        op = act.activation(hid[:, m, c0:c0 + wd], ps[UP_BANKS[m][n]][:, 0:wd], ACT.Gelu,
                                            bias=b1_sb[:, bass.ds(e, 1), m:m + 1].squeeze(1))
                    op.then_inc(made, 1)

                def body(e):
                    high_of(w2_hl, w2_raw, w2_loaded, e, (down, KT * e + 1), w2_high)
                    for m in range(HT):
                        act.wait_ge(gated, HT * e + m + 1)
                        act.wait_ge(down, KT * e + 1)
                        act.activation(hid_hl[:, 0, m], hid[:, m], ACT.Copy).then_inc(hid_high, 1)

                high_of(w1_hl, w1_raw, w1_loaded, 0, None, w1_high)
                act.wait_ge(b1_loaded, 16)
                for m in range(HT):
                    gelu(0, m)
                high_of(w1_hl, w1_raw, w1_loaded, 1, (up, HT), w1_high)
                with act.Fori(0, NE - 2) as e:
                    body(e)
                    for m in range(HT):
                        gelu(e + 1, m)
                    high_of(w1_hl, w1_raw, w1_loaded, e + 2, (up, HT * e + 2 * HT), w1_high)
                body(NE - 2)
                for m in range(HT):
                    gelu(NE - 1, m)
                body(NE - 1)

            @block.vector
            def _(dve):
                dve.sem_inc(hid_low, HT)
                dve.sem_inc(drained, KT)
                dve.sem_inc(down, 1)

                def body(e):
                    dve.wait_ge(gate_loaded, 16 * e + 16)
                    for m in range(HT):
                        dve.wait_ge(made, HT * e + m + 1)
                        dve.tensor_tensor(hid[:, m], hid[:, m], gate, ALU.mult).then_inc(gated, 1)
                    for m in range(HT):
                        dve.wait_ge(hid_high, HT * e + m + 1)
                        dve.tensor_tensor(hid_hl[:, 1, m], hid[:, m], hid_hl[:, 0, m].bitcast(F32), ALU.subtract).then_inc(hid_low, 1)
                    for m in range(KT):
                        dve.wait_ge(down, KT * e + m + 2)
                        dve.wait_ge(drained, KT * e + m + 1)
                        for n, (c0, wd) in enumerate(CHUNKS):
                            op = dve.tensor_tensor(acc[:, m, c0:c0 + wd], acc[:, m, c0:c0 + wd],
                                                   ps[DOWN_BANKS[m][n]][:, 0:wd], ALU.add)
                        op.then_inc(drained, 1)

                experts(dve, body)


class Ground:

    def __init__(self, nc, ctx):
        self.nc = nc
        self.stage_sems, self.cleared_sems = [], []
        self.psum = [ctx.enter_context(nc.psum_tensor(f"bank{i}", [P, 512], F32)) for i in range(8)]
        self.ident = self.sb(ctx, "ident", [P, P], F32)
        self.ones = self.sb(ctx, "ones", [P, P], F32)
        self.pair_mask = self.sb(ctx, "pair_mask", [P, P], F32)
        self.eps5 = self.sb(ctx, "eps5", [P, 1], F32)
        self.far = self.sb(ctx, "far", [P, 1], F32)
        self.no_edge = None

    def sb(self, ctx, name, shape, dt):
        return ctx.enter_context(self.nc.sbuf_tensor(name, shape, dt))

    def sem(self, name):
        s = self.nc.alloc_semaphore(name)
        self.stage_sems.append(s)
        return s

    def new_stage(self):
        for s in self.cleared_sems:
            self.nc.release_semaphore(s)
        for s in self.stage_sems:
            self.nc.gpsimd.sem_clear(s)
        self.cleared_sems, self.stage_sems = self.stage_sems, []


def program(nc, x, src, dst, W, out, until=None):
    with ExitStack() as ctx:
        g = Ground(nc, ctx)
        stage_constants(nc, g)
        g.x_T = g.sb(ctx, "x_T", [P, KT, N], F32)
        g.y_T = g.sb(ctx, "y_T", [P, KT, N], F32)
        counts_memory, gat_memory, no_edge_memory = (ctx.enter_context(ExitStack()) for _ in range(3))
        counts = g.sb(counts_memory, "counts_T", [P, NT, N], F32)
        g.counts_T = counts[0:TT]
        g.ft = g.sb(gat_memory, "ft", [TT, NT, KT, P], F32)
        g.a_cols = g.sb(gat_memory, "a_cols", [TT, NT, 2, H], F32)
        g.a1_fifth = g.sb(gat_memory, "a1_fifth", [TT, NT, H], F32)
        g.w_res = g.sb(gat_memory, "w_res", [P, P], F32)
        g.a1_max = g.sb(gat_memory, "a1_max", [TT, NT, H], F32)
        g.no_edge = g.sb(no_edge_memory, "no_edge", [TT, NT, N], BF16)
        g.counts_dram = nc.dram_tensor("counts_dram", (TT, NT * N), F32).ap().rearrange("p (j n) -> p j n", j=NT)
        stage_adjacency(nc, g, src, dst, x)
        stage_load(nc, g)
        stage_norm(nc, g, "ln0", g.x_T, g.y_T)
        if until == "ln0":
            g.x_T = g.y_T
            return stage_store(nc, g, out)
        g.a1_dram = nc.dram_tensor("a1_rows_dram", (H, N), F32).ap()
        g.uv_dram = nc.dram_tensor("uv_rows_dram", (2 * H, N), F32).ap()
        stage_gat_project(nc, g, W)
        with ExitStack() as c:
            o_T = g.sb(c, "o_T", [P, KT, N], F32)
            stage_mix0(nc, g, W["L0_mix_w_qkv"], g.y_T, o_T, counts[:, :, :].rearrange("p j n -> p (j n)"))
            stage_linear(nc, g, "mix0_proj", W["L0_mix_w_proj"], W["L0_mix_b_proj"], o_T, KT, KT, ACT.Identity, add_to=g.x_T,
                         refill=(g.counts_T[:, :, :], g.counts_dram))
        no_edge_memory.close()
        stage_gat_rows(nc, g)
        stage_gat_attend(nc, g)
        gat_memory.close()
        if until in ('gat', 'mix0'):
            return stage_store(nc, g, out)
        stage_norm(nc, g, "ln1", g.x_T, g.y_T)
        with ExitStack() as c:
            weight = g.sb(c, "ffn0_weight", [P, 1], F32)
            expert = g.sb(c, "ffn0_expert", [P, 1], I32)
            hid_T = g.sb(c, "ffn0_hid_T", [P, 3, N], F32)
            stage_choose(nc, g, W["L0_ffn_Wg"], g.y_T, weight[:, :], expert[:, :])
            stage_linear(nc, g, "ffn0_up", W["L0_ffn_W1"], W["L0_ffn_b1"], g.y_T, KT, 3, ACT.Gelu, dst=hid_T, expert=expert[0:1, 0:1])
            stage_linear(nc, g, "ffn0_down", W["L0_ffn_W2"], W["L0_ffn_b2"], hid_T, 3, KT, ACT.Identity, add_to=g.x_T,
                         times=weight[:, 0:1], expert=expert[0:1, 0:1])
        if until == "ffn0":
            return stage_store(nc, g, out)
        stage_norm(nc, g, "ln2", g.x_T, g.y_T)
        stage_gcn(nc, g, W["L1_gnn_W"], W["L1_gnn_b"], g.y_T, g.x_T)
        if until == "gcn":
            return stage_store(nc, g, out)
        counts_memory.close()
        with ExitStack() as c:
            o_T = g.sb(c, "o_T1", [P, KT, N], F32)
            stage_mix1(nc, g, W["L1_mix_W_qkv"], W["L1_mix_b_qkv"], g.y_T, o_T)
            stage_linear_split(nc, g, "mix1_proj", W["L1_mix_W_proj"], W["L1_mix_b_proj"], o_T, ACT.Sigmoid, g.x_T, scale=2.0)
        if until == "mix1":
            return stage_store(nc, g, out)
        z_T = g.y_T
        stage_norm(nc, g, "ln3", g.x_T, z_T)
        with ExitStack() as c:
            o_T = g.sb(c, "o_T2", [P, KT, N], F32)
            with ExitStack() as c2:
                zn_T = g.sb(c2, "zn_T", [P, KT, N], F32)
                stage_norm(nc, g, "ln4", z_T, zn_T, W["L1_ffn_ln1_g"], W["L1_ffn_ln1_b"])
                stage_attention(nc, g, W["L1_ffn_qkv_w"], W["L1_ffn_qkv_b"], zn_T, o_T)
            stage_linear_split(nc, g, "att_proj", W["L1_ffn_proj_w"], W["L1_ffn_proj_b"], o_T, ACT.Identity, z_T)
        stage_norm(nc, g, "ln5", z_T, z_T, W["L1_ffn_ln2_g"], W["L1_ffn_ln2_b"], acc=g.x_T)
        g.gates_dram = nc.dram_tensor("gates_dram", (8, N), F32).ap()
        y_high = g.sb(ctx, "y_high", [P, KT, N], F32R)
        y_low = g.sb(ctx, "y_low", [P, KT, N], F32R)
        stage_gates(nc, g, W["L1_ffn_gate_w"], W["L1_ffn_b2"], g.y_T, g.x_T, y_high, y_low)
        stage_experts(nc, g, W["L1_ffn_w1"], W["L1_ffn_b1"], W["L1_ffn_w2"], y_high, y_low,
                      g.y_T[:, :, :].rearrange("p k n -> p (k n)"), g.x_T)
        stage_store(nc, g, out)


_INS = ['x', 'src', 'dst', 'L0_gnn_W_fc', 'L0_gnn_attn_l', 'L0_gnn_attn_r', 'L0_gnn_W_res', 'L0_mix_w_qkv', 'L0_mix_w_proj', 'L0_mix_b_proj', 'L0_ffn_Wg', 'L0_ffn_W1', 'L0_ffn_b1', 'L0_ffn_W2', 'L0_ffn_b2', 'L1_gnn_W', 'L1_gnn_b', 'L1_mix_W_qkv', 'L1_mix_b_qkv', 'L1_mix_W_proj', 'L1_mix_b_proj', 'L1_ffn_ln1_g', 'L1_ffn_ln1_b', 'L1_ffn_qkv_w', 'L1_ffn_qkv_b', 'L1_ffn_proj_w', 'L1_ffn_proj_b', 'L1_ffn_ln2_g', 'L1_ffn_ln2_b', 'L1_ffn_gate_w', 'L1_ffn_w1', 'L1_ffn_b1', 'L1_ffn_w2', 'L1_ffn_b2']


def kernel(**inputs):
    import numpy as _np
    import concourse.bacc as _bacc
    from concourse import mybir as _mybir
    from concourse.bass_utils import run_bass_kernel_spmd as _run

    nc = _bacc.Bacc("TRN2", target_bir_lowering=False, num_devices=1)
    arrays, W = {}, {}
    for name in _INS:
        a = _np.ascontiguousarray(inputs[name])
        arrays[f"in_{name}_dram"] = a
        W[name] = nc.dram_tensor(f"in_{name}_dram", a.shape, _mybir.dt.from_np(a.dtype), kind="ExternalInput").ap()
    out = nc.dram_tensor("out_0_dram", (N, D), F32, kind="ExternalOutput").ap()
    program(nc, W["x"], W["src"], W["dst"], W, out)
    r = _run(nc, [arrays], core_ids=[0])
    return r.results[0]["out_0_dram"]
```
